# Optimizing a Trainium2 kernel written in Bass

```python
import numpy as np
import jax
import jax.numpy as jnp

def _softmax(x, axis=-1):
    return jax.nn.softmax(x, axis=axis)

def _gelu(x):
    return jax.nn.gelu(x, approximate=True)

def _silu(x):
    return jax.nn.silu(x)

def _sigmoid(x):
    return jax.nn.sigmoid(x)

def _layernorm(x, axis=-1, eps=1e-05):
    m = jnp.mean(x, axis=axis, keepdims=True)
    v = jnp.var(x, axis=axis, keepdims=True)
    return (x - m) / jnp.sqrt(v + eps)

def _scatter_add(tgt, idx, src, axis=0):
    return tgt.at[idx].add(src)

def _segment_sum(src, seg, n):
    return jax.ops.segment_sum(src, seg, n)
kernel_name = 'mk_macaron_d2_jaxref_r8_2e67de'

def setup_inputs(seed: int=0):
    np.random.seed(seed)
    _w = jnp.asarray

    def _L0_attn_setup():
        import jax, jax.numpy as jnp
        import numpy as np
        import math
        B, T, C = (4, 256, 128)
        N_HEADS = 16
        D_HEAD = C // N_HEADS

        def _rope_tables(d_head, max_seq_len):
            half = d_head // 2
            theta = 1.0 / 10000.0 ** (jnp.arange(half, dtype=jnp.float32) / half)
            pos = jnp.arange(max_seq_len, dtype=jnp.float32)
            freqs = jnp.outer(pos, theta)
            cos = jnp.concatenate([jnp.cos(freqs), jnp.cos(freqs)], axis=-1)
            sin = jnp.concatenate([jnp.sin(freqs), jnp.sin(freqs)], axis=-1)
            return (cos, sin)

        def _rotate_half(x):
            d = x.shape[-1] // 2
            return jnp.concatenate([-x[..., d:], x[..., :d]], axis=-1)

        def _apply_rope(x, cos, sin):
            return x * cos[None, None] + _rotate_half(x) * sin[None, None]
        key = jax.random.key(seed)
        k1, k2, k3 = jax.random.split(key, 3)
        x = jax.random.normal(k1, (B, T, C), dtype=jnp.float32)
        W_qkv = jax.random.normal(k2, (C, 3 * C), dtype=jnp.float32) * (1.0 / math.sqrt(C))
        W_proj = jax.random.normal(k3, (C, C), dtype=jnp.float32) * (1.0 / math.sqrt(C))
        return {'x': x, 'W_qkv': W_qkv, 'W_proj': W_proj}
    _L0_attn_in = _L0_attn_setup()

    def _L0_ffn_setup():
        import jax, jax.numpy as jnp
        import numpy as np
        B, S, D = (4, 256, 128)
        EXP = 4
        H = EXP * D
        E = 8
        TOP_K = 2
        key = jax.random.key(seed)
        ks = jax.random.split(key, 8)
        scale1 = 1.0 / np.sqrt(D)
        scale2 = 1.0 / np.sqrt(H)
        x = jax.random.normal(ks[0], (B, S, D), dtype=jnp.float32)
        W1 = jax.random.uniform(ks[1], (E, D, H), jnp.float32, -scale1, scale1)
        b1 = jax.random.uniform(ks[2], (E, H), jnp.float32, -scale1, scale1)
        W2 = jax.random.uniform(ks[3], (E, H, D), jnp.float32, -scale2, scale2)
        b2 = jax.random.uniform(ks[4], (E, D), jnp.float32, -scale2, scale2)
        Wr = jax.random.uniform(ks[5], (D, E), jnp.float32, -scale1, scale1)
        br = jax.random.uniform(ks[6], (E,), jnp.float32, -scale1, scale1)
        return {'input_emb': x, 'W1': W1, 'b1': b1, 'W2': W2, 'b2': b2, 'Wr': Wr, 'br': br}
    _L0_ffn_in = _L0_ffn_setup()

    def _L1_attn_setup():
        import jax, jax.numpy as jnp
        import numpy as np
        WS = 8
        H = 16
        SHIFT = 4

        def _relative_position_index(ws):
            coords = np.stack(np.meshgrid(np.arange(ws), np.arange(ws), indexing='ij'))
            cf = coords.reshape(2, -1)
            rel = cf[:, :, None] - cf[:, None, :]
            rel = rel.transpose(1, 2, 0).astype(np.int64)
            rel[..., 0] += ws - 1
            rel[..., 1] += ws - 1
            rel[..., 0] *= 2 * ws - 1
            return rel.sum(-1)
        key = jax.random.key(seed)
        ks = jax.random.split(key, 5)
        B, N, C = (4, 1024, 128)
        x = jax.random.normal(ks[0], (B, N, C), dtype=jnp.float32)
        w_qkv = jax.random.normal(ks[1], (C, 3 * C), dtype=jnp.float32) * 0.02
        b_qkv = jnp.zeros((3 * C,), dtype=jnp.float32)
        w_proj = jax.random.normal(ks[2], (C, C), dtype=jnp.float32) * 0.02
        b_proj = jnp.zeros((C,), dtype=jnp.float32)
        bias_table = jax.random.normal(ks[3], ((2 * WS - 1) ** 2, H), dtype=jnp.float32) * 0.02
        return {'x': x, 'w_qkv': w_qkv, 'b_qkv': b_qkv, 'w_proj': w_proj, 'b_proj': b_proj, 'bias_table': bias_table}
    _L1_attn_in = _L1_attn_setup()

    def _L1_ffn_setup():
        import jax, jax.numpy as jnp
        import numpy as np
        S_LEN, BATCH, HIDDEN = (256, 2, 128)
        N_HEADS, N_KV = (16, 8)
        N_EXP, TOP_K, CAP_F = (8, 2, 1.25)
        FFN = 512
        HEAD_DIM = HIDDEN // N_HEADS
        Q_PER_KV = N_HEADS // N_KV
        EPS = 1e-05
        NEG = -1000000000.0

        def _ln(x, w, b):
            mu = jnp.mean(x, -1, keepdims=True)
            var = jnp.var(x, -1, keepdims=True)
            return (x - mu) * jax.lax.rsqrt(var + EPS) * w + b

        def _forward(hidden_states, ln1_weight, ln1_bias, ln2_weight, ln2_bias, qkv_weight, proj_weight, router_weight, moe_w1, moe_w2):
            S, B, H = hidden_states.shape
            ln1 = _ln(hidden_states, ln1_weight, ln1_bias)
            qkv = (ln1 @ qkv_weight.T).reshape(S, B, N_KV, (Q_PER_KV + 2) * HEAD_DIM)
            q_dim = Q_PER_KV * HEAD_DIM
            q = qkv[..., :q_dim].reshape(S, B, N_HEADS, HEAD_DIM)
            k = jnp.repeat(qkv[..., q_dim:q_dim + HEAD_DIM], Q_PER_KV, axis=2)
            v = jnp.repeat(qkv[..., q_dim + HEAD_DIM:], Q_PER_KV, axis=2)
            scores = jnp.einsum('sbhd,tbhd->bhst', q, k) / jnp.sqrt(jnp.float32(HEAD_DIM))
            causal = jnp.tril(jnp.ones((S, S), bool))
            attn = jax.nn.softmax(jnp.where(causal[None, None], scores, NEG), axis=-1)
            attn_out = jnp.einsum('bhst,tbhd->sbhd', attn, v).reshape(S, B, H)
            hidden_after_attn = hidden_states + attn_out @ proj_weight.T
            x = _ln(hidden_after_attn, ln2_weight, ln2_bias).reshape(-1, H)
            N = S * B
            probs = jax.nn.softmax(x.astype(jnp.float32) @ router_weight, axis=-1)
            top_p, top_i = jax.lax.top_k(probs, TOP_K)
            top_p = top_p / jnp.sum(top_p, -1, keepdims=True)
            flat_exp = top_i.reshape(-1)
            order = jnp.argsort(flat_exp)
            sorted_exp = flat_exp[order]
            counts = jnp.bincount(sorted_exp, length=N_EXP)
            offsets = jnp.concatenate([jnp.zeros((1,), counts.dtype), jnp.cumsum(counts)])
            within = jnp.arange(N * TOP_K) - offsets[sorted_exp]
            cap = int(np.ceil(N * TOP_K / N_EXP * CAP_F))
            keep = within < cap
            slot = jnp.where(keep, sorted_exp * cap + within, N_EXP * cap)
            tok_id = order // TOP_K
            padded_tokens = jnp.zeros((N_EXP * cap + 1, H), x.dtype).at[slot].set(x[tok_id])[:-1]
            padded_probs = jnp.zeros((N_EXP * cap + 1,), jnp.float32).at[slot].set(top_p.reshape(-1)[order])[:-1]
            padded_ids = jnp.zeros((N_EXP * cap + 1,), jnp.int32).at[slot].set(tok_id.astype(jnp.int32))[:-1]
            exp_in = padded_tokens.reshape(N_EXP, cap, H)
            act = jax.nn.gelu(jnp.einsum('ech,ehf->ecf', exp_in, moe_w1), approximate=False)
            exp_out = jnp.einsum('ecf,efh->ech', act, moe_w2).reshape(N_EXP * cap, H)
            weighted = exp_out * padded_probs[:, None].astype(exp_out.dtype)
            moe = jnp.zeros((N, H), exp_out.dtype).at[padded_ids].add(weighted)
            return hidden_after_attn + moe.reshape(S, B, H)
        ks = jax.random.split(jax.random.key(seed), 6)
        qkv_out = N_KV * (Q_PER_KV + 2) * HEAD_DIM
        sc = 0.02
        return {'hidden_states': jax.random.normal(ks[0], (S_LEN, BATCH, HIDDEN), jnp.float32), 'ln1_weight': jnp.ones((HIDDEN,), jnp.float32), 'ln1_bias': jnp.zeros((HIDDEN,), jnp.float32), 'ln2_weight': jnp.ones((HIDDEN,), jnp.float32), 'ln2_bias': jnp.zeros((HIDDEN,), jnp.float32), 'qkv_weight': jax.random.normal(ks[1], (qkv_out, HIDDEN), jnp.float32) * sc, 'proj_weight': jax.random.normal(ks[2], (HIDDEN, HIDDEN), jnp.float32) * sc, 'router_weight': jax.random.normal(ks[3], (HIDDEN, N_EXP), jnp.float32) * sc, 'moe_w1': jax.random.normal(ks[4], (N_EXP, HIDDEN, FFN), jnp.float32) * sc, 'moe_w2': jax.random.normal(ks[5], (N_EXP, FFN, HIDDEN), jnp.float32) * sc}
    _L1_ffn_in = _L1_ffn_setup()
    _d = {'L0_attn_x': _L0_attn_in['x'], 'L0_attn_W_qkv': _L0_attn_in['W_qkv'], 'L0_attn_W_proj': _L0_attn_in['W_proj'], 'L0_ffn_W1': _L0_ffn_in['W1'], 'L0_ffn_b1': _L0_ffn_in['b1'], 'L0_ffn_W2': _L0_ffn_in['W2'], 'L0_ffn_b2': _L0_ffn_in['b2'], 'L0_ffn_Wr': _L0_ffn_in['Wr'], 'L0_ffn_br': _L0_ffn_in['br'], 'L1_attn_w_qkv': _L1_attn_in['w_qkv'], 'L1_attn_b_qkv': _L1_attn_in['b_qkv'], 'L1_attn_w_proj': _L1_attn_in['w_proj'], 'L1_attn_b_proj': _L1_attn_in['b_proj'], 'L1_attn_bias_table': _L1_attn_in['bias_table'], 'L1_ffn_ln1_weight': _L1_ffn_in['ln1_weight'], 'L1_ffn_ln1_bias': _L1_ffn_in['ln1_bias'], 'L1_ffn_ln2_weight': _L1_ffn_in['ln2_weight'], 'L1_ffn_ln2_bias': _L1_ffn_in['ln2_bias'], 'L1_ffn_qkv_weight': _L1_ffn_in['qkv_weight'], 'L1_ffn_proj_weight': _L1_ffn_in['proj_weight'], 'L1_ffn_router_weight': _L1_ffn_in['router_weight'], 'L1_ffn_moe_w1': _L1_ffn_in['moe_w1'], 'L1_ffn_moe_w2': _L1_ffn_in['moe_w2']}
    _x0 = _d['L0_attn_x']
    _d['L0_attn_x'] = jax.random.normal(jax.random.fold_in(jax.random.key(seed), 1), (4, 512, 128), dtype=_x0.dtype)
    del _x0
    return _d

def reference(L0_attn_x, L0_attn_W_qkv, L0_attn_W_proj, L0_ffn_W1, L0_ffn_b1, L0_ffn_W2, L0_ffn_b2, L0_ffn_Wr, L0_ffn_br, L1_attn_w_qkv, L1_attn_b_qkv, L1_attn_w_proj, L1_attn_b_proj, L1_attn_bias_table, L1_ffn_ln1_weight, L1_ffn_ln1_bias, L1_ffn_ln2_weight, L1_ffn_ln2_bias, L1_ffn_qkv_weight, L1_ffn_proj_weight, L1_ffn_router_weight, L1_ffn_moe_w1, L1_ffn_moe_w2):

    def _L0_attn_ref(x, W_qkv, W_proj):
        import jax, jax.numpy as jnp
        import numpy as np
        import math
        B, T, C = (4, 256, 128)
        N_HEADS = 16
        D_HEAD = C // N_HEADS

        def _rope_tables(d_head, max_seq_len):
            half = d_head // 2
            theta = 1.0 / 10000.0 ** (jnp.arange(half, dtype=jnp.float32) / half)
            pos = jnp.arange(max_seq_len, dtype=jnp.float32)
            freqs = jnp.outer(pos, theta)
            cos = jnp.concatenate([jnp.cos(freqs), jnp.cos(freqs)], axis=-1)
            sin = jnp.concatenate([jnp.sin(freqs), jnp.sin(freqs)], axis=-1)
            return (cos, sin)

        def _rotate_half(x):
            d = x.shape[-1] // 2
            return jnp.concatenate([-x[..., d:], x[..., :d]], axis=-1)

        def _apply_rope(x, cos, sin):
            return x * cos[None, None] + _rotate_half(x) * sin[None, None]
        b, t, c = x.shape
        qkv = x @ W_qkv
        q, k, v = jnp.split(qkv, 3, axis=-1)

        def reshape(z):
            return z.reshape(b, t, N_HEADS, D_HEAD).transpose(0, 2, 1, 3)
        q, k, v = (reshape(q), reshape(k), reshape(v))
        cos, sin = _rope_tables(D_HEAD, t)
        q = _apply_rope(q, cos, sin)
        k = _apply_rope(k, cos, sin)
        scale = 1.0 / math.sqrt(D_HEAD)
        att = jnp.einsum('bhqd,bhkd->bhqk', q, k) * scale
        causal = jnp.tril(jnp.ones((t, t), dtype=bool))
        att = jnp.where(causal[None, None], att, -jnp.inf)
        att = jax.nn.softmax(att, axis=-1)
        out = jnp.einsum('bhqk,bhkd->bhqd', att, v)
        out = out.transpose(0, 2, 1, 3).reshape(b, t, c)
        return out @ W_proj

    def _L0_ffn_ref(input_emb, W1, b1, W2, b2, Wr, br):
        import jax, jax.numpy as jnp
        import numpy as np
        B, S, D = (4, 256, 128)
        EXP = 4
        H = EXP * D
        E = 8
        TOP_K = 2
        logits = jnp.einsum('bsd,de->bse', input_emb, Wr) + br
        route_w = jax.nn.softmax(logits, axis=-1)
        _, topk_idx = jax.lax.top_k(route_w, TOP_K)
        mask = jax.nn.one_hot(topk_idx, E, dtype=route_w.dtype).sum(-2)
        routed = route_w * mask
        routed = routed / routed.sum(axis=-1, keepdims=True)
        h = jax.nn.relu(jnp.einsum('bsd,edh->ebsh', input_emb, W1) + b1[:, None, None, :])
        expert_out = jnp.einsum('ebsh,ehd->ebsd', h, W2) + b2[:, None, None, :]
        return jnp.einsum('bse,ebsd->bsd', routed, expert_out)

    def _L1_attn_ref(x, w_qkv, b_qkv, w_proj, b_proj, bias_table):
        import jax, jax.numpy as jnp
        import numpy as np
        WS = 8
        H = 16
        SHIFT = 4

        def _relative_position_index(ws):
            coords = np.stack(np.meshgrid(np.arange(ws), np.arange(ws), indexing='ij'))
            cf = coords.reshape(2, -1)
            rel = cf[:, :, None] - cf[:, None, :]
            rel = rel.transpose(1, 2, 0).astype(np.int64)
            rel[..., 0] += ws - 1
            rel[..., 1] += ws - 1
            rel[..., 0] *= 2 * ws - 1
            return rel.sum(-1)
        B, N, C = x.shape
        D = C // H
        pad_len = -N % WS
        if pad_len:
            x = jnp.pad(x, ((0, 0), (0, pad_len), (0, 0)))
        Np = N + pad_len
        if SHIFT > 0:
            x = jnp.roll(x, -SHIFT, axis=1)
        nw = Np // WS
        xw = x.reshape(B * nw, WS, C)
        qkv = xw @ w_qkv + b_qkv
        q, k, v = jnp.split(qkv, 3, axis=-1)

        def to_heads(t):
            return t.reshape(-1, WS, H, D).transpose(0, 2, 1, 3)
        q, k, v = (to_heads(q), to_heads(k), to_heads(v))
        attn = jnp.einsum('bhqd,bhkd->bhqk', q, k) * D ** (-0.5)
        idx = _relative_position_index(WS)[:WS, :WS]
        bias = bias_table[idx.reshape(-1)].reshape(WS, WS, H)
        bias = bias.transpose(2, 0, 1)
        attn = jax.nn.softmax(attn + bias[None], axis=-1)
        out = jnp.einsum('bhqk,bhkd->bhqd', attn, v)
        out = out.transpose(0, 2, 1, 3).reshape(-1, WS, C)
        out = out @ w_proj + b_proj
        out = out.reshape(B, Np, C)
        if SHIFT > 0:
            out = jnp.roll(out, SHIFT, axis=1)
        return out[:, :N, :]

    def _L1_ffn_ref(hidden_states, ln1_weight, ln1_bias, ln2_weight, ln2_bias, qkv_weight, proj_weight, router_weight, moe_w1, moe_w2):
        import jax, jax.numpy as jnp
        import numpy as np
        S_LEN, BATCH, HIDDEN = (256, 2, 128)
        N_HEADS, N_KV = (16, 8)
        N_EXP, TOP_K, CAP_F = (8, 2, 1.25)
        FFN = 512
        HEAD_DIM = HIDDEN // N_HEADS
        Q_PER_KV = N_HEADS // N_KV
        EPS = 1e-05
        NEG = -1000000000.0

        def _ln(x, w, b):
            mu = jnp.mean(x, -1, keepdims=True)
            var = jnp.var(x, -1, keepdims=True)
            return (x - mu) * jax.lax.rsqrt(var + EPS) * w + b

        def _forward(hidden_states, ln1_weight, ln1_bias, ln2_weight, ln2_bias, qkv_weight, proj_weight, router_weight, moe_w1, moe_w2):
            S, B, H = hidden_states.shape
            ln1 = _ln(hidden_states, ln1_weight, ln1_bias)
            qkv = (ln1 @ qkv_weight.T).reshape(S, B, N_KV, (Q_PER_KV + 2) * HEAD_DIM)
            q_dim = Q_PER_KV * HEAD_DIM
            q = qkv[..., :q_dim].reshape(S, B, N_HEADS, HEAD_DIM)
            k = jnp.repeat(qkv[..., q_dim:q_dim + HEAD_DIM], Q_PER_KV, axis=2)
            v = jnp.repeat(qkv[..., q_dim + HEAD_DIM:], Q_PER_KV, axis=2)
            scores = jnp.einsum('sbhd,tbhd->bhst', q, k) / jnp.sqrt(jnp.float32(HEAD_DIM))
            causal = jnp.tril(jnp.ones((S, S), bool))
            attn = jax.nn.softmax(jnp.where(causal[None, None], scores, NEG), axis=-1)
            attn_out = jnp.einsum('bhst,tbhd->sbhd', attn, v).reshape(S, B, H)
            hidden_after_attn = hidden_states + attn_out @ proj_weight.T
            x = _ln(hidden_after_attn, ln2_weight, ln2_bias).reshape(-1, H)
            N = S * B
            probs = jax.nn.softmax(x.astype(jnp.float32) @ router_weight, axis=-1)
            top_p, top_i = jax.lax.top_k(probs, TOP_K)
            top_p = top_p / jnp.sum(top_p, -1, keepdims=True)
            flat_exp = top_i.reshape(-1)
            order = jnp.argsort(flat_exp)
            sorted_exp = flat_exp[order]
            counts = jnp.bincount(sorted_exp, length=N_EXP)
            offsets = jnp.concatenate([jnp.zeros((1,), counts.dtype), jnp.cumsum(counts)])
            within = jnp.arange(N * TOP_K) - offsets[sorted_exp]
            cap = int(np.ceil(N * TOP_K / N_EXP * CAP_F))
            keep = within < cap
            slot = jnp.where(keep, sorted_exp * cap + within, N_EXP * cap)
            tok_id = order // TOP_K
            padded_tokens = jnp.zeros((N_EXP * cap + 1, H), x.dtype).at[slot].set(x[tok_id])[:-1]
            padded_probs = jnp.zeros((N_EXP * cap + 1,), jnp.float32).at[slot].set(top_p.reshape(-1)[order])[:-1]
            padded_ids = jnp.zeros((N_EXP * cap + 1,), jnp.int32).at[slot].set(tok_id.astype(jnp.int32))[:-1]
            exp_in = padded_tokens.reshape(N_EXP, cap, H)
            act = jax.nn.gelu(jnp.einsum('ech,ehf->ecf', exp_in, moe_w1), approximate=False)
            exp_out = jnp.einsum('ecf,efh->ech', act, moe_w2).reshape(N_EXP * cap, H)
            weighted = exp_out * padded_probs[:, None].astype(exp_out.dtype)
            moe = jnp.zeros((N, H), exp_out.dtype).at[padded_ids].add(weighted)
            return hidden_after_attn + moe.reshape(S, B, H)
        return _forward(hidden_states, ln1_weight, ln1_bias, ln2_weight, ln2_bias, qkv_weight, proj_weight, router_weight, moe_w1, moe_w2)
    x = L0_attn_x
    x = x + 0.5 * _L0_ffn_ref(_layernorm(x, axis=-1), L0_ffn_W1, L0_ffn_b1, L0_ffn_W2, L0_ffn_b2, L0_ffn_Wr, L0_ffn_br)
    x = x + _L0_attn_ref(_layernorm(x, axis=-1), L0_attn_W_qkv, L0_attn_W_proj)
    x = x + 0.5 * _L0_ffn_ref(_layernorm(x, axis=-1), L0_ffn_W1, L0_ffn_b1, L0_ffn_W2, L0_ffn_b2, L0_ffn_Wr, L0_ffn_br)
    x = x + 0.5 * _L1_ffn_ref(_layernorm(x, axis=-1), L1_ffn_ln1_weight, L1_ffn_ln1_bias, L1_ffn_ln2_weight, L1_ffn_ln2_bias, L1_ffn_qkv_weight, L1_ffn_proj_weight, L1_ffn_router_weight, L1_ffn_moe_w1, L1_ffn_moe_w2)
    x = x + _L1_attn_ref(_layernorm(x, axis=-1), L1_attn_w_qkv, L1_attn_b_qkv, L1_attn_w_proj, L1_attn_b_proj, L1_attn_bias_table)
    x = x + 0.5 * _L1_ffn_ref(_layernorm(x, axis=-1), L1_ffn_ln1_weight, L1_ffn_ln1_bias, L1_ffn_ln2_weight, L1_ffn_ln2_bias, L1_ffn_qkv_weight, L1_ffn_proj_weight, L1_ffn_router_weight, L1_ffn_moe_w1, L1_ffn_moe_w2)
    return x

_drawn_inputs = setup_inputs


def setup_inputs(seed=0):
    import zlib

    import numpy as np

    out = dict(_drawn_inputs(seed))
    spreads = {'L1_attn_b_qkv': (0.0, 0.504),
     'L1_attn_b_proj': (0.0, 0.1),
     'L1_ffn_ln1_weight': (1.0, 0.6),
     'L1_ffn_ln1_bias': (0.0, 2.0),
     'L1_ffn_ln2_weight': (1.0, 0.6),
     'L1_ffn_ln2_bias': (0.0, 2.0)}
    factors = {'L0_ffn_b1': 3.534,
     'L0_ffn_b2': 2.879,
     'L1_attn_w_qkv': 4.618,
     'L1_attn_w_proj': 2.877,
     'L1_attn_bias_table': 8.0,
     'L1_ffn_router_weight': 2.985}
    for name, (base, spread) in spreads.items():
        noise = np.random.default_rng([zlib.crc32(name.encode()), seed]).standard_normal(out[name].shape)
        drawn = base * np.exp(spread * noise) if base else spread * noise
        out[name] = jnp.asarray(drawn.astype(out[name].dtype))
    for name, factor in factors.items():
        out[name] = (out[name] * factor).astype(out[name].dtype)
    return out
```

```python
from contextlib import ExitStack

import numpy as np

import concourse.bass as bass
from concourse import mybir

F32 = mybir.dt.float32
F32R = mybir.dt.float32r
BF16 = mybir.dt.bfloat16
ALU = mybir.AluOpType
ACT = mybir.ActivationFunctionType
X = mybir.AxisListType.X

P = 128
B, T, C = 4, 512, 128
NT = B * T // P
TB = T // P
H, D = 16, 8
E, FF = 8, 512
HB = FF // P
KV = 8
SEQ = 4
CAP = 640
WS, SHIFT = 8, 4
NW = B * T // WS // P
XTW = T + WS
EPS = 1e-5
SCALE = float(D) ** -0.5
MASKED = -1.0e9
HEADS_G = 4
NG = H // HEADS_G
MAX_ROW = 24

CONST_COLS = dict(ident=128, before=128, ones=128, mask_qk=128, mask_kq=128, cos=T, sin=T,
                  q_hi=512, q_lo=512, k_hi=512, k_lo=512, one_row=1, rev=128)


def const_array():
    c = {n: np.zeros((P, w), np.float32) for n, w in CONST_COLS.items()}
    i = np.arange(P)
    c["ident"][i, i] = 1
    c["before"][:] = i[:, None] < i[None, :]
    c["ones"][:] = 1
    c["mask_qk"][:] = np.where(i[:, None] >= i[None, :], 0, -1e30)
    c["mask_kq"][:] = c["mask_qk"].T
    half = D // 2
    theta = (1.0 / np.float32(10000.0) ** (np.arange(half, dtype=np.float32) / half)).astype(np.float32)
    freqs = np.outer(np.arange(T, dtype=np.float32), theta).astype(np.float32)
    c["cos"][:] = np.cos(freqs).astype(np.float32).T[i % half]
    c["sin"][:] = np.sin(freqs).astype(np.float32).T[i % half]
    for h in range(H):
        g, j = divmod(h, HEADS_G)
        for d in range(D):
            for name, thirds in (("q_hi", (0, 1)), ("q_lo", (2,)), ("k_hi", (0, 2)), ("k_lo", (1,))):
                for s in thirds:
                    c[name][h * D + d, g * P + 32 * j + D * s + d] = 1
    c["one_row"][MAX_ROW::32] = 1
    c["rev"][:] = E - np.arange(P) % E
    return np.concatenate([c[n] for n in CONST_COLS], axis=1)


def build(nc, a, out, stages="ABCDEF"):
    ctx = ExitStack()
    with ctx:
        def sb(name, shape, dt=F32):
            return ctx.enter_context(nc.sbuf_tensor(name, shape, dt))

        def sem(name):
            return ctx.enter_context(nc.semaphore(name))

        x = sb("x", [P, NT, C])
        xn = sb("xn", [P, NT, C])
        xT = sb("xT", [P, B, XTW])
        const = sb("constants", [P, sum(CONST_COLS.values())])
        cc, at = {}, 0
        for n, w in CONST_COLS.items():
            cc[n] = const[:, at:at + w]
            at += w
        ident, ones = cc["ident"], cc["ones"]
        small = sb("small", [P, NT, 6])
        mv = sb("mv", [P, NT, 2])
        veps = sb("veps", [P, NT])
        rstd = sb("rstd", [P, NT])
        mhalf = sb("mhalf", [P, NT])
        wr0 = sb("wr0", [P, E])
        br0 = sb("br0", [P, E])
        wr1 = sb("wr1", [P, E])
        b1T = sb("b1T", [P, E * HB])
        b1r = sb("b1r", [E * HB, P])
        b2 = sb("b2", [E, C])
        wT = sb("wT", [E, NT * P])
        w1 = sb("w1", [P, 2, FF])
        w2 = sb("w2", [P, 2, HB, C])
        hid = sb("hid", [P, 2, HB, T])
        rt = sb("rt", [P, 12, NT, E])
        rs = sb("rs", [P, 8, NT])
        gate = sb("gate", [P, NT, E])
        lnw = sb("lnw", [P, 4])
        lnr = sb("lnr", [4, P])
        big = sb("big", [P, 20608])
        w0qkv = sb("w0qkv", [P, 3 * C])
        w0rot = sb("w0rot", [P, 2 * C])
        w0proj = sb("w0proj", [P, C])
        w1qkv = sb("w1qkv", [P, 3 * C])
        b1qkv = sb("b1qkv", [P, 3 * C])
        w1proj = sb("w1proj", [P, C])
        b1proj = sb("b1proj", [P, C])
        btab = sb("btab", [P, 2 * WS - 1, H])
        gq_raw = sb("gq_raw", [P, 2, C])
        gqT = sb("gqT", [P, 2 * C])
        gp_raw = sb("gp_raw", [P, C])
        gpT = sb("gpT", [P, C])
        sel = sb("sel", [P, 4, 512], F32R)
        negid = sb("negid", [P, P], F32R)
        mask = sb("mask", [P, 3, P], BF16)
        mrow = sb("mrow", [P, TB, P], F32R)
        kaug = sb("kaug", [P, 2, T], F32R)
        qaug = sb("qaug", [P, 2, T], F32R)
        qaug2 = sb("qaug2", [P, 2, T], F32R)
        qk_hl = sb("qk_hl", [P, 4, T], F32R)

        psum_all = ctx.enter_context(nc.psum_tensor("psum_all", [P, 8, 512], F32))
        psum = [psum_all[:, i, :] for i in range(8)]

        s_in = sem("s_in")
        s_tick = sem("s_tick")
        s_vz = sem("s_vz")
        s_row = sem("s_row")
        s_done = sem("s_done")
        s_out = sem("s_out")
        s_const = sem("s_const")
        s_pool = sem("s_pool")
        s_dve = sem("s_dve")
        s_act = sem("s_act")
        s_setup_ps = sem("s_setup_ps")
        s_setup = sem("s_setup")
        s_var = sem("s_var")
        s_rstd = sem("s_rstd")
        s_src = sem("s_src")
        s_tps = sem("s_tps")
        s_xT = sem("s_xT")
        s_logit = sem("s_logit")
        s_soft = sem("s_soft")
        s_exp = sem("s_exp")
        s_gate = sem("s_gate")
        s_rank = sem("s_rank")
        s_wTc = sem("s_wTc")
        s_b2 = sem("s_b2")
        s_w = [sem("s_w0"), sem("s_w1")]
        s_hps = sem("s_hps")
        s_h = sem("s_h")
        s_y = sem("s_y")
        s_x = sem("s_x")
        s_xb, s_qk, s_qkd, s_v, s_vd = map(sem, ("s_xb", "s_qk", "s_qkd", "s_v", "s_vd"))
        s_kps, s_kd, s_qps, s_qd = map(sem, ("s_kps", "s_kd", "s_qps", "s_qd"))
        s_s, s_m, s_mt, s_q2 = map(sem, ("s_s", "s_m", "s_mt", "s_q2"))
        s_st, s_p, s_pv, s_o = map(sem, ("s_st", "s_p", "s_pv", "s_o"))
        s_ot, s_at, s_att, s_attT, s_pr, s_xa = map(sem, ("s_ot", "s_at", "s_att", "s_attT", "s_pr", "s_xa"))
        s_g = {n: sem("s_g_" + n) for n in ("qps", "qkv", "sc", "ex", "pr", "ha")}
        s_wn = {n: sem("s_wn_" + n) for n in ("qps", "qkv", "sc", "ex", "pr")}

        big_at = [0]

        def carve(cols, dt=F32):
            v = big[:, big_at[0]:big_at[0] + cols]
            big_at[0] += cols
            return v

        xb = carve(T)
        rope = carve(4 * T).rearrange("p (a t) -> p a t", a=4)
        vaug = carve(TB * H * 32).rearrange("p (k h w) -> p k h w", k=TB, h=H)
        pT = carve(2 * 5 * 1024).rearrange("p (u c w) -> p u c w", u=2, c=5)
        oT = carve(NG * T).rearrange("p (g t) -> p g t", g=NG)
        rden = carve(TB * H).rearrange("p (a h) -> p a h", a=TB)
        att = carve(TB * C).rearrange("p (a c) -> p a c", a=TB)
        attT = carve(T)
        big_at[0] = 0
        gqkv = carve(NT * 256).rearrange("p (t c) -> p t c", t=NT)
        gprod = carve(10 * 512).rearrange("p (i e) -> p i e", i=10)
        gsc = carve(SEQ * SEQ * 64).rearrange("p (s t e) -> p s t e", s=SEQ, t=SEQ)
        gp = carve(SEQ * SEQ * 64).rearrange("p (s t e) -> p s t e", s=SEQ, t=SEQ)
        gsm = carve(4 * 256).rearrange("p (i s e) -> p i s e", i=4, s=SEQ)
        go = carve(NT * C).rearrange("p (t c) -> p t c", t=NT)
        big_at[0] = 0
        wqkv = carve(NW * WS * 3 * C).rearrange("p (n o c) -> p n o c", n=NW, o=WS)
        wprod = carve(2 * NW * WS * C).rearrange("p (u e) -> p u e", u=2)
        wsc = carve(WS * NW * WS * H).rearrange("p (q e) -> p q e", q=WS)
        wpp = carve(WS * NW * WS * H).rearrange("p (q e) -> p q e", q=WS)
        wsm = carve(3 * WS * NW * H).rearrange("p (i a h) -> p i a h", i=3, h=H)
        wo = carve(NW * WS * C).rearrange("p (n o c) -> p n o c", n=NW, o=WS)
        wbr = carve((2 * WS - 1) * H).rearrange("p (r h) -> p r h", h=H)
        xW = carve(NW * WS * P).rearrange("p (n o w) -> p n o w", n=NW, o=WS)

        block = ctx.enter_context(nc.Block())
        plan = [("AC" if s in "AC" else s) for s in stages]
        t_count = {"A": 1, "B": 1, "C": 1, "D": 3, "E": 2, "F": 3}
        n_count = {"A": 1, "B": 1, "C": 1, "D": 3, "E": 1, "F": 3}
        first_t, first_n, moe_no, gqa_no = {}, {}, {}, {}
        t0 = n0 = m0 = g0 = 0
        for s in stages:
            first_t[s], first_n[s], moe_no[s], gqa_no[s] = t0, n0, m0, g0
            t0, n0 = t0 + t_count[s], n0 + n_count[s]
            m0 += s in "ACDF"
            g0 += s in "DF"
        X_MOE = NT + E * NT
        NCHUNK = E * B

        def groups(t):
            return slice(4 * t, 4 * t + 4)

        r_l0 = {moe_no[s]: i for i, s in enumerate(s for s in stages if s in "AC")}

        def loads():
            bc = lambda v, n: v.rearrange("(o n) -> o n", o=1).broadcast_to((P, n))
            yield x[:], a["L0_attn_x"].rearrange("b (t p) c -> p (b t) c", p=P)
            yield const[:], a["const"]
            yield wr0[:], a["L0_ffn_Wr"]
            yield br0[:], bc(a["L0_ffn_br"], E)
            yield wr1[:], a["L1_ffn_router_weight"]
            yield b1r[:], a["L0_ffn_b1"].rearrange("e (h p) -> (e h) p", p=P)
            yield b2[:], a["L0_ffn_b2"]
            yield w0qkv[:], a["L0_attn_W_qkv"]
            yield w0proj[:], a["L0_attn_W_proj"]
            yield w1qkv[:], a["L1_attn_w_qkv"]
            yield b1qkv[:], bc(a["L1_attn_b_qkv"], 3 * C)
            yield w1proj[:], a["L1_attn_w_proj"]
            yield b1proj[:], bc(a["L1_attn_b_proj"], C)
            first = (WS - 1) * (2 * WS - 1)
            rows = a["L1_attn_bias_table"][first:first + 2 * WS - 1, :]
            yield btab[:], rows.rearrange("(o r) h -> o r h", o=1).broadcast_to((P, 2 * WS - 1, H))
            yield gq_raw[:], a["L1_ffn_qkv_weight"].rearrange("(i p) c -> p i c", p=P)
            yield gp_raw[:], a["L1_ffn_proj_weight"]
            for i, n in enumerate(("ln1_weight", "ln1_bias", "ln2_weight", "ln2_bias")):
                yield lnr[i:i + 1, :], a["L1_ffn_" + n].rearrange("(o n) -> o n", o=1)

        N_IN = 16 * 20

        @block.sync
        def _(sp):
            n_in = 0
            for tile, src in loads():
                sp.dma_start(tile, src).then_inc(s_in, 16)
            for s in stages:
                if s not in "ACDF":
                    continue
                r = moe_no[s]
                w1_d, w2_d = (a["L0_ffn_W1"], a["L0_ffn_W2"]) if s in "AC" else (a["L1_ffn_moe_w1"], a["L1_ffn_moe_w2"])
                with sp.Fori(0, E // 2) as i:
                    for u in range(2):
                        sp.wait_ge(s_y, 8 * i + r * NCHUNK + 4 * u + 1)
                        sp.dma_start(w1[:, u], w1_d[bass.ds(2 * i + u, 1)].rearrange("e p f -> (e p) f")).then_inc(s_w[u], 16)
                        sp.dma_start(w2[:, u], w2_d[bass.ds(2 * i + u, 1)].rearrange("e (h p) c -> p (e h) c", p=P)).then_inc(s_w[u], 16)
            sp.wait_ge(s_done, 1)
            sp.dma_start(out.rearrange("b (t p) c -> p (b t) c", p=P), x[:]).then_inc(s_out, 16)
            sp.wait_ge(s_out, 16)


        @block.gpsimd
        def _(pool):
            nc.gpsimd.memset(mhalf[:], -0.5).then_inc(s_pool, 1)
            nc.gpsimd.memset(mrow[:].bitcast(F32), 0.0).then_inc(s_pool, 1)
            pool.wait_ge(s_pool, 1)
            for n in range(n0):
                pool.wait_ge(s_var, n + 1)
                nc.gpsimd.tensor_tensor(rstd[:], veps[:], mhalf[:], ALU.pow).then_inc(s_rstd, 1)

        @block.tensor
        def _(pe):
            mm = nc.tensor.matmul
            pe.sem_inc(s_y, 5)
            rows_done = [0]
            pe.wait_ge(s_in, N_IN)
            nc.tensor.transpose(psum[4][:, 0:E * HB], b1r[:], ident[0:E * HB, 0:E * HB])
            nc.tensor.transpose(psum[4][:, 32:36], lnr[:], ident[0:4, 0:4])
            nc.tensor.transpose(psum[4][:, 128:256], gp_raw[:], ident)
            for i in range(2):
                last = nc.tensor.transpose(psum[4][:, 256 + 128 * i:384 + 128 * i], gq_raw[:, i], ident)
            last.then_inc(s_setup_ps, 1)

            def turn(t, src):
                for g in range(4):
                    pe.wait_ge(s_src, 4 * t + g + 1)
                    for k in range(4):
                        ins = nc.tensor.transpose(psum[g][:, P * k:P * k + P], src(4 * g + k), ident)
                    ins.then_inc(s_tps, 1)

            def moe(kind, r, t):
                pe.wait_ge(s_xT, 4 * t + 4)
                for k in range(NT):
                    ins = mm(psum[4][:, E * k:E * k + E], xT[:, k // 4, P * (k % 4):P * (k % 4) + P],
                             (wr0 if kind == 0 else wr1)[:], start=True, stop=True)
                ins.then_inc(s_logit, 1)
                pe.wait_ge(s_gate, r + 1)
                if kind == 0:
                    for k in range(NT):
                        ins = nc.tensor.transpose(psum[k // 4][0:E, P * (k % 4):P * (k % 4) + P], gate[:, k, :], ident)
                        if k % 4 == 3:
                            ins.then_inc(s_rank, 1)
                    for k in range(NT):
                        if k % 4 == 0:
                            pe.wait_ge(s_wTc, 4 * (r_l0[r]) + k // 4 + 1)
                        ins = mm(psum[4 + k // 4][:, P * (k % 4):P * (k % 4) + P], wT[:, P * k:P * k + P], b2[:],
                                 start=True, stop=True)
                        if k % 4 == 3:
                            ins.then_inc(s_b2, 1)
                else:
                    chosen = rt[:, 10].rearrange("p t e -> p (t e)")
                    mm(psum[5][:, 0:P], cc["before"], chosen, start=True, stop=True)
                    mm(psum[5][:, P:2 * P], ones, chosen, start=True, stop=True).then_inc(s_rank, 4)
                pe.wait_ge(s_x, r * X_MOE + NT)
                with pe.Fori(0, E // 2) as i:
                    def first(m):
                        u, c = m // 4, m % 4
                        if c == 0:
                            pe.wait_ge(s_w[u], 32 * i + 32 * (r * (E // 2) + 1))
                        for h in range(HB):
                            pe.wait_ge(s_h, 32 * i + r * NCHUNK * HB + 4 * m + h + 1)
                            mm(psum[h][:], w1[:, u, P * h:P * h + P], xT[:, c, 0:T],
                               start=True, stop=True).then_inc(s_hps, 1)

                    def second(m):
                        u, c = m // 4, m % 4
                        pe.wait_ge(s_h, 32 * i + r * NCHUNK * HB + 4 * m + 8)
                        pe.wait_ge(s_x, 32 * i + r * X_MOE + NT + 4 * m - 4)
                        for k in range(4):
                            for h in range(HB):
                                ins = mm(psum[4 + m % 2][:, P * k:P * k + P], hid[:, m % 2, h, P * k:P * k + P],
                                         w2[:, u, h], start=(h == 0), stop=(h == HB - 1))
                        ins.then_inc(s_y, 1)

                    first(0)
                    for m in range(8):
                        if m < 7:
                            first(m + 1)
                        second(m)

            def rope_attention(t):
                pe.wait_ge(s_xT, 4 * t + 4)
                for b in range(B):
                    pe.wait_ge(s_xb, b + 1)
                    for n, w in enumerate((w0qkv[:, 0:C], w0rot[:, 0:C], w0qkv[:, C:2 * C], w0rot[:, C:2 * C])):
                        ins = mm(psum[2 + n][:], w, xb, start=True, stop=True)
                    ins.then_inc(s_qk, 1)
                    for k in range(TB):
                        ins = mm(psum[7][:, P * k:P * k + P], xb[:, P * k:P * k + P], w0qkv[:, 2 * C:3 * C],
                                 start=True, stop=True)
                    ins.then_inc(s_v, 1)

                    def prep(g):
                        n = b * NG + g
                        pe.wait_ge(s_vd, b + 1)
                        if n >= 1:
                            pe.wait_ge(s_q2, n)
                        pe.wait_ge(s_qkd, b + 1)
                        mm(psum[7][:], sel[:, 2, P * g:P * g + P], qk_hl[:, 2], start=True, stop=False)
                        mm(psum[7][:], sel[:, 3, P * g:P * g + P], qk_hl[:, 3], start=False, stop=True).then_inc(s_kps, 1)
                        if g >= 1:
                            pe.wait_ge(s_qd, n)
                        if g >= 2:
                            pe.wait_ge(s_o, n - 1)
                        if g == 0 and b:
                            pe.wait_ge(s_xa, b)
                        mm(psum[6][:], sel[:, 0, P * g:P * g + P], qk_hl[:, 0], start=True, stop=False)
                        mm(psum[6][:], sel[:, 1, P * g:P * g + P], qk_hl[:, 1], start=False, stop=True).then_inc(s_qps, 1)

                    def score(m, col, qt, j, g):
                        rows, w = slice(32 * j, 32 * j + 32), P * (qt + 1)
                        mm(psum[m % 2][:, col:col + w], qaug[rows, g % 2, P * qt:P * qt + P], kaug[rows, g % 2, 0:w],
                           start=True, stop=False, skip_group_check=True)
                        return mm(psum[m % 2][:, col + P * qt:col + w], mask[:, 0], mask[:, 1],
                                  start=False, stop=True, skip_group_check=True)

                    def score_chunks(g):
                        n = b * NG + g
                        pe.wait_ge(s_kd, n + 1)
                        pe.wait_ge(s_qd, n + 1)
                        for c in range(8):
                            m = n * 12 + c
                            if m >= 2:
                                pe.wait_ge(s_m, m - 1)
                            score(m, 0, 3 - c // 4, c % 4, g).then_inc(s_s, 1)
                            yield
                        for qt in (1, 0):
                            m = n * 12 + 10 - 2 * qt
                            for i in range(2):
                                pe.wait_ge(s_m, m - 1 + i)
                                score(m + i, 0, qt, 2 * i, g).then_inc(s_row, 1)
                                rows_done[0] += 1
                            for i in range(2):
                                pe.wait_ge(s_row, rows_done[0] - 1 + i)
                                score(m + i, P * (qt + 1), qt, 2 * i + 1, g).then_inc(s_s, 1)
                            yield

                    def exp_chunks(g):
                        n = b * NG + g
                        pe.wait_ge(s_q2, n + 1)
                        for c in range(5):
                            m = n * 5 + c
                            if m >= 2:
                                pe.wait_ge(s_p, m - 1)
                            bank = 2 + 2 * (m % 2)
                            if c != 2:
                                j = c if c < 2 else c - 1
                                parts = [(bank, 0, j, 0), (bank + 1, 0, j, 1), (bank + 1, 384, j, 3)]
                            else:
                                parts = [(bank + j // 2, 256 * (j % 2), j, 2) for j in (0, 2, 1, 3)]
                            for i, (bk, col, j, kt) in enumerate(parts):
                                if c == 2 and i >= 2:
                                    pe.wait_ge(s_row, rows_done[0] - 1 + i - 2)
                                rows = slice(32 * j, 32 * j + 32)
                                w = T - P * kt
                                mm(psum[bk][:, col:col + w], kaug[rows, g % 2, P * kt:P * kt + P], qaug2[rows, g % 2, P * kt:T],
                                   start=True, stop=False, skip_group_check=True)
                                ins = mm(psum[bk][:, col:col + P], mask[:, 0], mask[:, 2], start=False, stop=True, skip_group_check=True)
                                if c == 2 and i < 2:
                                    ins.then_inc(s_row, 1)
                                    rows_done[0] += 1
                            ins.then_inc(s_st, 1)
                            yield

                    def maxima(g):
                        n = b * NG + g
                        pe.wait_ge(s_m, (n + 1) * 12)
                        pe.wait_ge(s_kd, n + 1)
                        for qt in range(TB):
                            ins = mm(psum[7][:, P * qt:P * qt + P], mrow[:, qt], negid[:], start=True, stop=True)
                        ins.then_inc(s_mt, 1)

                    def values(g):
                        n = b * NG + g
                        pe.wait_ge(s_p, (n + 1) * 5)
                        pe.wait_ge(s_qd, min(n + 2, b * NG + NG))
                        for kt in range(TB):
                            for j in range(4):
                                h = 4 * g + j
                                if kt == 2:
                                    src = pT[:, g % 2, 2, 256 * j:256 * j + 256]
                                else:
                                    c = j if j < 2 else j + 1
                                    o = {0: 0, 1: 512, 3: 896}[kt]
                                    src = pT[:, g % 2, c, o:o + T - P * kt]
                                ins = mm(psum[6][32 * j:32 * j + 32, P * kt:T], vaug[:, kt, h, :], src,
                                         start=(kt == 0), stop=(kt == TB - 1))
                        ins.then_inc(s_pv, 1)

                    prep(0)
                    for _ in score_chunks(0):
                        pass
                    for g in range(NG):
                        maxima(g)
                        more = iter(())
                        if g + 1 < NG:
                            prep(g + 1)
                            more = score_chunks(g + 1)
                        for _ in exp_chunks(g):
                            next(more, None)
                            next(more, None)
                        for _ in more:
                            pass
                        values(g)
                    for qt in range(TB):
                        m = 4 * b + qt
                        pe.wait_ge(s_o, NG * (b + 1))
                        if m >= 2 and qt >= 2:
                            pe.wait_ge(s_at, m - 1)
                        for g in range(NG):
                            ins = nc.tensor.transpose(psum[qt % 2][:, P * g:P * g + P], oT[:, g, P * qt:P * qt + P], ident)
                        ins.then_inc(s_ot, 1)
                    pe.wait_ge(s_at, 4 * b + 4)
                    for qt in range(TB):
                        ins = nc.tensor.transpose(psum[7][:, P * qt:P * qt + P], att[:, qt], ident)
                    ins.then_inc(s_att, 1)
                    pe.wait_ge(s_attT, b + 1)
                    for qt in range(TB):
                        ins = mm(psum[6][:, P * qt:P * qt + P], attT[:, P * qt:P * qt + P], w0proj[:], start=True, stop=True)
                    ins.then_inc(s_pr, 1)

            def grouped_attention(t, q):
                pe.wait_ge(s_xT, 4 * t + 4)
                for k in range(NT // 2):
                    m = q * 8 + k
                    if k >= 2:
                        pe.wait_ge(s_g["qkv"], m - 1)
                    for i in range(2):
                        ins = mm(psum[4 + k % 2][:, 256 * i:256 * i + 256],
                                 xT[:, k // 2, P * (2 * k + i - 4 * (k // 2)):P * (2 * k + i - 4 * (k // 2)) + P], gqT[:],
                                 start=True, stop=True)
                    ins.then_inc(s_g["qps"], 1)
                turn(t + 1, lambda k: go[:, k, :])
                for k in range(4):
                    pe.wait_ge(s_xT, 4 * (t + 1) + k + 1)
                    for i in range(4):
                        ins = mm(psum[4 + k][:, P * i:P * i + P], xT[:, k, P * i:P * i + P], gpT[:], start=True, stop=True)
                    ins.then_inc(s_g["pr"], 1)

            def window_attention(t):
                pe.wait_ge(s_xT, 4 * t + 4)
                for k in range(NW * WS):
                    n, o = divmod(k, WS)
                    if k >= 2:
                        pe.wait_ge(s_wn["qkv"], k - 1)
                    mm(psum[4 + k % 2][:, 0:3 * C], xW[:, n, o], w1qkv[:], start=True, stop=True).then_inc(s_wn["qps"], 1)
                turn(t + 1, lambda k: wo[:, k // WS, k % WS, :])
                for k in range(4):
                    pe.wait_ge(s_xT, 4 * (t + 1) + 4)
                    for i in range(4):
                        ins = mm(psum[4 + k][:, P * i:P * i + P], xT[:, k, P * i:P * i + P], w1proj[:], start=True, stop=True)
                    ins.then_inc(s_wn["pr"], 1)

            for s in stages:
                t = first_t[s]
                pe.wait_ge(s_setup, 1)
                turn(t, (lambda k: go[:, k, :]) if s in "DF" else (lambda k: xn[:, k, :]))
                if s in "AC":
                    moe(0, moe_no[s], t)
                elif s == "B":
                    pe.wait_ge(s_const, 12)
                    rope_attention(t)
                elif s in "DF":
                    grouped_attention(t, gqa_no[s])
                    turn(t + 2, lambda k: xn[:, k, :])
                    moe(1, moe_no[s], t + 2)
                else:
                    window_attention(t)


        @block.scalar
        def _(act):
            A = nc.scalar.activation
            act.sem_inc(s_h, 4)
            act.wait_ge(s_in, N_IN)
            act.wait_ge(s_setup_ps, 1)
            A(b1T[:], psum[4][:, 0:E * HB], ACT.Identity).then_inc(s_act, 1)
            A(lnw[:], psum[4][:, 32:36], ACT.Identity).then_inc(s_act, 1)
            A(gpT[:], psum[4][:, 128:256], ACT.Identity).then_inc(s_act, 1)
            A(gqT[:], psum[4][:, 256:512], ACT.Identity).then_inc(s_act, 1)
            act.wait_ge(s_act, 4)
            act.drain().then_inc(s_setup, 1)
            chain = [4]

            def turned(t, mode):
                for g in range(4):
                    act.wait_ge(s_tps, 4 * t + g + 1)
                    src = psum[g][:]
                    if mode == "windows":
                        n, o0 = g // 2, 4 * (g % 2)
                        dst = xT[:, 2 * n:2 * n + 2, SHIFT + o0:SHIFT + o0 + T]
                        dst = dst.rearrange("p b (w o) -> p b w o", o=WS)[:, :, :, 0:4]
                        ins = None
                        for o in range(4):
                            ins = A(dst[:, :, :, o], src[:, P * o:P * o + P].rearrange("p (b w) -> p b w", b=2), ACT.Identity)
                            if o < 3 or g == 3:
                                ins.then_inc(s_act, 1)
                                chain[0] += 1
                        if g == 3:
                            act.wait_ge(s_act, chain[0])
                            act.wait_ge(s_xT, 4 * t + 3)
                            ins = A(xT[:, :, 0:SHIFT], xT[:, :, T:T + SHIFT], ACT.Identity)
                        ins.then_inc(s_xT, 1)
                        continue
                    if mode == "to windows":
                        nw = T // WS
                        dst = xW[:, g // 2, :, nw * (g % 2):nw * (g % 2) + nw]
                        A(dst[:, :, 0:nw - 1], src[:, SHIFT:T - SHIFT].rearrange("p (w o) -> p o w", o=WS), ACT.Identity)
                        A(dst[:, 0:SHIFT, nw - 1], src[:, T - SHIFT:T], ACT.Identity)
                        A(dst[:, SHIFT:WS, nw - 1], src[:, 0:SHIFT], ACT.Identity).then_inc(s_xT, 1)
                        continue
                    if mode in (0, 2):
                        ins = A(xT[:, g, 0:T], src, ACT.Identity, scale=lnw[:, mode:mode + 1], bias=lnw[:, mode + 1:mode + 2])
                    else:
                        ins = A(xT[:, g, 0:T], src, ACT.Identity)
                    ins.then_inc(s_xT, 1)

            def moe(kind, r):
                act.wait_ge(s_soft, r + 1)
                A(rt[:, 1], rt[:, 0], ACT.Exp).then_inc(s_exp, 1)
                if kind == 0:
                    for g in range(4):
                        act.wait_ge(s_rank, 4 * r + g + 1)
                        A(wT[:, 512 * g:512 * g + 512], psum[g][0:E, :], ACT.Identity).then_inc(s_wTc, 1)
                with act.Fori(0, E // 2) as i:
                    for m in range(8):
                        u, c = m // 4, m % 4
                        act.wait_ge(s_y, 8 * i + r * NCHUNK + m + 4)
                        for h in range(HB):
                            act.wait_ge(s_hps, 32 * i + r * NCHUNK * HB + 4 * m + h + 1)
                            if kind == 0:
                                act.sem_inc(s_tick, 1)
                                A(hid[:, m % 2, h], psum[h][:], ACT.Relu,
                                  bias=b1T[:, bass.ds(i * (2 * HB) + (u * HB + h), 1)]).then_inc(s_h, 1)
                            else:
                                A(hid[:, m % 2, h], psum[h][:], ACT.Gelu).then_inc(s_h, 1)

            def rope_attention(t):
                act.wait_ge(s_xT, 4 * t + 4)
                for b in range(B):
                    if b:
                        act.wait_ge(s_v, b)
                    A(xb, xT[:, b, 0:T], ACT.Identity).then_inc(s_xb, 1)
                    act.wait_ge(s_v, b + 1)
                    act.wait_ge(s_vz, 1)
                    A(vaug[:, :, :, 0:D], psum[7][:].rearrange("p (k h d) -> p k h d", k=TB, h=H), ACT.Identity).then_inc(s_vd, 1)

                    def keys(g):
                        n = b * NG + g
                        act.wait_ge(s_kps, n + 1)
                        A(kaug[:, g % 2], psum[7][:], ACT.Identity, bias=cc["one_row"]).then_inc(s_kd, 1)

                    keys(0)
                    for g in range(NG):
                        n = b * NG + g
                        if g + 1 < NG:
                            keys(g + 1)
                        for c in range(5):
                            act.wait_ge(s_st, n * 5 + c + 1)
                            bank = 2 + 2 * ((n * 5 + c) % 2)
                            A(pT[:, g % 2, c], psum_all[:, bank:bank + 2, :].rearrange("p b w -> p (b w)"), ACT.Exp, scale=SCALE).then_inc(s_p, 1)
                        act.wait_ge(s_pv, n + 1)
                        A(oT[:, g], psum[6][:], ACT.Identity).then_inc(s_o, 1)
                    act.wait_ge(s_att, b + 1)
                    A(attT, psum[7][:], ACT.Identity).then_inc(s_attT, 1)

            for s in stages:
                t = first_t[s]
                if s in "AC":
                    turned(t, "plain")
                    moe(0, moe_no[s])
                elif s == "B":
                    turned(t, "plain")
                    rope_attention(t)
                elif s in "DF":
                    turned(t, 0)
                    q = gqa_no[s]
                    act.wait_ge(s_g["sc"], q + 1)
                    A(gp, gsc, ACT.Exp, scale=SCALE).then_inc(s_g["ex"], 1)
                    turned(t + 1, "plain")
                    turned(t + 2, 2)
                    moe(1, moe_no[s])
                else:
                    turned(t, "to windows")
                    act.wait_ge(s_wn["sc"], 1)
                    A(wpp, wsc, ACT.Exp).then_inc(s_wn["ex"], 1)
                    turned(t + 1, "windows")

        @block.vector
        def _(dve):
            V = nc.vector
            n = [0]

            def mark(ins):
                ins.then_inc(s_dve, 1)
                n[0] += 1

            def settle():
                dve.wait_ge(s_dve, n[0])

            def seq(ins):
                mark(ins)
                settle()

            tt = V.tensor_tensor
            dve.wait_ge(s_in, N_IN)
            for i, name in enumerate(("q_hi", "q_lo", "k_hi", "k_lo")):
                V.tensor_copy(sel[:, i], cc[name]).then_inc(s_const, 1)
            V.tensor_scalar(negid[:], ident, -1.0, None, ALU.mult).then_inc(s_const, 1)
            for i, name in enumerate(("ident", "mask_qk", "mask_kq")):
                V.tensor_copy(mask[:, i], cc[name]).then_inc(s_const, 1)
            src = w0qkv[:, 0:2 * C].rearrange("p (a z d) -> p a z d", z=2, d=D // 2)
            dst = w0rot[:].rearrange("p (a z d) -> p a z d", z=2, d=D // 2)
            V.tensor_scalar(dst[:, :, 0], src[:, :, 1], -1.0, None, ALU.mult).then_inc(s_const, 1)
            V.tensor_copy(dst[:, :, 1], src[:, :, 0]).then_inc(s_const, 1)
            V.memset(veps[:], 0.0).then_inc(s_const, 1)
            V.memset(rt[:, 11], 0.0).then_inc(s_const, 1)
            dve.wait_ge(s_const, 12)
            dve.wait_ge(s_pool, 2)

            def norm(i, src, dst, turn=None):
                for k in range(NT):
                    mark(V.bn_stats(small[:, k], src[:, k]))
                settle()
                for k in range(NT):
                    mark(V.bn_aggr(mv[:, k], small[:, k]))
                settle()
                V.tensor_scalar(veps[:], mv[:, :, 1], EPS, None, ALU.add).then_inc(s_var, 1)
                dve.wait_ge(s_rstd, i + 1)
                for k in range(NT):
                    ins = V.tensor_scalar(dst[:, k], src[:, k], mv[:, k, 0:1], rstd[:, k:k + 1], ALU.subtract, ALU.mult)
                    if turn is not None and k % 4 == 3:
                        ins.then_inc(s_src, 1)
                    else:
                        mark(ins)
                if turn is not None:
                    dve.wait_ge(s_src, 4 * turn + 4)
                settle()

            def moe(kind, r, t, base_tile=None):
                L, Pr, eq, oh1, p2, oh2 = (rt[:, i] for i in (0, 1, 2, 3, 4, 5))
                bc = lambda v: v.unsqueeze(2).broadcast_to((P, NT, E))
                dve.wait_ge(s_logit, r + 1)
                ps = psum[4][:, 0:P].rearrange("p (t e) -> p t e", e=E)
                if kind == 0:
                    seq(tt(L, ps, br0[:].unsqueeze(1).broadcast_to((P, NT, E)), ALU.add))
                else:
                    seq(V.tensor_copy(L, ps))
                seq(V.tensor_reduce(rs[:, 0], L, X, ALU.max))
                tt(L, L, bc(rs[:, 0]), ALU.subtract).then_inc(s_soft, 1)
                dve.wait_ge(s_exp, r + 1)
                seq(V.tensor_reduce(rs[:, 1], Pr, X, ALU.add))
                seq(V.reciprocal(rs[:, 2], rs[:, 1]))
                seq(tt(Pr, Pr, bc(rs[:, 2]), ALU.mult))
                rev = cc["rev"].rearrange("p (t e) -> p t e", e=E)
                for src, top, onehot in ((Pr, 3, oh1), (p2, 4, oh2)):
                    seq(V.tensor_reduce(rs[:, top], src, X, ALU.max))
                    seq(tt(eq, src, bc(rs[:, top]), ALU.is_equal))
                    seq(tt(eq, eq, rev, ALU.mult))
                    seq(V.tensor_reduce(rs[:, 5], eq, X, ALU.max))
                    seq(tt(onehot, eq, bc(rs[:, 5]), ALU.is_equal))
                    if top == 3:
                        seq(V.scalar_tensor_tensor(out=p2, in0=oh1, scalar=-2.0, in1=Pr, op0=ALU.mult, op1=ALU.add))
                seq(tt(rs[:, 6], rs[:, 3], rs[:, 4], ALU.add))
                seq(V.reciprocal(rs[:, 7], rs[:, 6]))
                chosen = rt[:, 10]
                seq(tt(chosen, oh1, oh2, ALU.add))
                if kind == 1:
                    dve.drain().then_inc(s_gate, 1)
                seq(tt(gate[:], Pr, chosen, ALU.mult))
                seq(V.scalar_tensor_tensor(out=gate[:], in0=gate[:], scalar=0.5, in1=bc(rs[:, 7]), op0=ALU.mult, op1=ALU.mult))
                if kind == 0:
                    dve.drain().then_inc(s_gate, 1)
                    for k in range(NT):
                        if k % 4 == 0:
                            dve.wait_ge(s_b2, 4 * r_l0[r] + k // 4 + 1)
                        tt(x[:, k], psum[4 + k // 4][:, P * (k % 4):P * (k % 4) + P], x[:, k], ALU.add).then_inc(s_x, 1)
                else:
                    dve.wait_ge(s_rank, 4 * r + 4)
                    tot = psum[5][:, P:2 * P].rearrange("p (t e) -> p t e", e=E)
                    seq(V.tensor_copy(rt[:, 6, 1:NT], tot[:, 0:NT - 1]))
                    seq(V.tensor_copy(rt[:, 6, 0:1], rt[:, 11, 0:1]))
                    cur, other, step = 6, 7, 1
                    while step < NT:
                        mark(tt(rt[:, other, step:NT], rt[:, cur, step:NT], rt[:, cur, 0:NT - step], ALU.add))
                        seq(V.tensor_copy(rt[:, other, 0:step], rt[:, cur, 0:step]))
                        cur, other, step = other, cur, 2 * step
                    seq(tt(rt[:, 8], psum[5][:, 0:P].rearrange("p (t e) -> p t e", e=E), rt[:, cur], ALU.add))
                    seq(V.tensor_scalar(rt[:, 9], rt[:, 8], float(CAP), None, ALU.is_lt))
                    seq(tt(gate[:], gate[:], rt[:, 9], ALU.mult))
                    for k in range(NT):
                        V.scalar_tensor_tensor(out=x[:, k], in0=go[:, k], scalar=0.5, in1=x[:, k],
                                               op0=ALU.mult, op1=ALU.add).then_inc(s_x, 1)
                dve.wait_ge(s_x, r * X_MOE + NT)
                with dve.Fori(0, E // 2) as i:
                    for m in range(8):
                        u, c = m // 4, m % 4
                        dve.wait_ge(s_y, 8 * i + r * NCHUNK + m + 6)
                        dve.wait_ge(s_x, 32 * i + r * X_MOE + NT + 4 * m - 12)
                        for k in range(4):
                            V.scalar_tensor_tensor(out=x[:, 4 * c + k], in0=psum[4 + m % 2][:, P * k:P * k + P],
                                                   scalar=gate[:, 4 * c + k, bass.ds(i * 2 + u, 1)], in1=x[:, 4 * c + k],
                                                   op0=ALU.mult, op1=ALU.add).then_inc(s_x, 1)
                dve.wait_ge(s_x, (r + 1) * X_MOE)

            def rope_attention(t):
                seq(V.memset(vaug, 0.0))
                V.memset(vaug[:, :, :, D:D + 1], 1.0).then_inc(s_vz, 1)
                for b in range(B):
                    dve.wait_ge(s_qk, b + 1)
                    for i in range(2):
                        mark(tt(rope[:, 2 * i], psum[2 + 2 * i][:], cc["cos"], ALU.mult))
                        mark(tt(rope[:, 2 * i + 1], psum[3 + 2 * i][:], cc["sin"], ALU.mult))
                    settle()
                    for i in range(2):
                        mark(tt(rope[:, 2 * i], rope[:, 2 * i], rope[:, 2 * i + 1], ALU.add))
                    settle()
                    for i in range(2):
                        mark(V.tensor_copy(qk_hl[:, 2 * i], rope[:, 2 * i]))
                    settle()
                    for i in range(2):
                        seq(tt(qk_hl[:, 2 * i + 1], rope[:, 2 * i], qk_hl[:, 2 * i].bitcast(F32), ALU.subtract))
                    dve.drain().then_inc(s_qkd, 1)

                    def queries(g):
                        n_ = b * NG + g
                        dve.wait_ge(s_qps, n_ + 1)
                        V.tensor_copy(qaug[:, g % 2], psum[6][:]).then_inc(s_qd, 1)

                    def row_max(g):
                        n_ = b * NG + g
                        if n_:
                            dve.wait_ge(s_mt, n_)
                        chunks = [(3, 0, 1), (3, 1, 1), (3, 2, 1), (3, 3, 1), (2, 0, 1), (2, 1, 1), (2, 2, 1), (2, 3, 1),
                                  (1, 0, 2), (1, 2, 2), (0, 0, 2), (0, 2, 2)]
                        for c, (qt, j, nh) in enumerate(chunks):
                            m = n_ * 12 + c
                            dve.wait_ge(s_s, m + 1)
                            w = P * (qt + 1)
                            src = psum[m % 2][:, 0:w * nh].rearrange("p (h k) -> p h k", h=nh)
                            dst = mrow[:, qt, 32 * j + MAX_ROW:32 * (j + nh - 1) + MAX_ROW + 1:32]
                            V.tensor_reduce(dst, src, X, ALU.max).then_inc(s_m, 1)

                    def add_max(g):
                        n_ = b * NG + g
                        dve.wait_ge(s_mt, n_ + 1)
                        tt(qaug2[:, g % 2], psum[7][:], qaug[:, g % 2].bitcast(F32), ALU.add).then_inc(s_q2, 1)

                    queries(0)
                    row_max(0)
                    for g in range(NG):
                        add_max(g)
                        if g + 1 < NG:
                            queries(g + 1)
                            row_max(g + 1)
                    for qt in range(TB):
                        dve.wait_ge(s_ot, 4 * b + qt + 1)
                        o4 = psum[qt % 2][:].rearrange("p (h w) -> p h w", h=H)
                        seq(V.reciprocal(rden[:, qt], o4[:, :, D]))
                        tt(att[:, qt].rearrange("p (h d) -> p h d", h=H), o4[:, :, 0:D],
                           rden[:, qt].unsqueeze(2).broadcast_to((P, H, D)), ALU.mult).then_inc(s_at, 1)
                    dve.wait_ge(s_pr, b + 1)
                    tt(x[:, TB * b:TB * b + TB].rearrange("p a c -> p (a c)"), psum[6][:],
                       x[:, TB * b:TB * b + TB].rearrange("p a c -> p (a c)"), ALU.add).then_inc(s_xa, 1)
                dve.wait_ge(s_xa, B)

            def grouped_attention(t, q):
                for k in range(NT // 2):
                    dve.wait_ge(s_g["qps"], q * 8 + k + 1)
                    V.tensor_copy(gqkv[:, 2 * k:2 * k + 2].rearrange("p a c -> p (a c)"), psum[4 + k % 2][:]).then_inc(s_g["qkv"], 1)
                mark(V.memset(gsc, MASKED))
                dve.wait_ge(s_g["qkv"], q * 8 + 8)
                settle()
                at = lambda s: gqkv[:, 4 * s:4 * s + 4].rearrange("p a (n w) -> p (a n) w", w=4 * D)
                q_of = lambda s: at(s)[:, :, 0:2 * D].rearrange("p m (i d) -> p m i d", i=2)
                k_of = lambda s: at(s)[:, :, 2 * D:3 * D].unsqueeze(2).broadcast_to((P, 32, 2, D))
                v_of = lambda s: at(s)[:, :, 3 * D:4 * D].unsqueeze(2).broadcast_to((P, 32, 2, D))
                pairs = [(s, u) for s in range(SEQ) for u in range(s + 1)]
                v4 = lambda v: v.rearrange("p (m i d) -> p m i d", i=2, d=D)
                for i, (s, u) in enumerate(pairs):
                    mark(tt(v4(gprod[:, i]), q_of(s), k_of(u), ALU.mult))
                settle()
                for i, (s, u) in enumerate(pairs):
                    mark(V.tensor_reduce(gsc[:, s, u], gprod[:, i].rearrange("p (e d) -> p e d", d=D), X, ALU.add))
                settle()
                key_last = lambda v: v.rearrange("p s t e -> p s e t")
                seq(V.tensor_reduce(gsm[:, 0], key_last(gsc), X, ALU.max))
                over = lambda v: v.unsqueeze(2).broadcast_to((P, SEQ, SEQ, 64))
                tt(gsc, gsc, over(gsm[:, 0]), ALU.subtract).then_inc(s_g["sc"], 1)
                dve.wait_ge(s_g["ex"], q + 1)
                seq(V.tensor_reduce(gsm[:, 1], key_last(gp), X, ALU.add))
                seq(V.reciprocal(gsm[:, 2], gsm[:, 1]))
                seq(tt(gp, gp, over(gsm[:, 2]), ALU.mult))
                for i, (s, u) in enumerate(pairs):
                    pr = gp[:, s, u].rearrange("p (m i) -> p m i", i=2).unsqueeze(3).broadcast_to((P, 32, 2, D))
                    mark(tt(v4(gprod[:, i]), pr, v_of(u), ALU.mult))
                settle()
                gos = go.rearrange("p (s a) c -> p s (a c)", s=SEQ)
                first = {s: s * (s + 1) // 2 for s in range(SEQ)}
                for u in range(SEQ):
                    for s in range(max(u, 0), SEQ):
                        if u == 0:
                            mark(V.tensor_copy(gos[:, s], gprod[:, first[s]]))
                        else:
                            mark(tt(gos[:, s], gos[:, s], gprod[:, first[s] + u], ALU.add))
                    settle()
                for g in range(4):
                    dve.drain().then_inc(s_src, 1)
                for k in range(4):
                    dve.wait_ge(s_g["pr"], 4 * q + k + 1)
                    flat = lambda v: v[:, 4 * k:4 * k + 4].rearrange("p a c -> p (a c)")
                    mark(tt(flat(go), psum[4 + k][:], flat(xn), ALU.add))
                settle()

            def window_attention(t):
                for k in range(NW * WS):
                    i, o = divmod(k, WS)
                    dve.wait_ge(s_wn["qps"], k + 1)
                    tt(wqkv[:, i, o], psum[4 + k % 2][:, 0:3 * C], b1qkv[:], ALU.add).then_inc(s_wn["qkv"], 1)
                for r in range(2 * WS - 1):
                    mark(V.tensor_copy(wbr[:, r], btab[:, 2 * WS - 2 - r]))
                dve.wait_ge(s_wn["qkv"], NW * WS)
                settle()
                K16 = NW * WS
                keys = wqkv.rearrange("p n o c -> p (n o) c")
                for q in range(WS):
                    u = q % 2
                    qv = wqkv[:, :, q, 0:C].unsqueeze(2).broadcast_to((P, NW, WS, C))
                    seq(tt(wprod[:, u].rearrange("p (n k c) -> p n k c", n=NW, k=WS), qv,
                           wqkv[:, :, :, C:2 * C], ALU.mult))
                    seq(V.tensor_reduce(wsc[:, q], wprod[:, u].rearrange("p (e d) -> p e d", d=D), X, ALU.add))
                for q in range(WS):
                    bias = wbr[:, WS - 1 - q:2 * WS - 1 - q].rearrange("p k h -> p (k h)").unsqueeze(1).broadcast_to((P, NW, WS * H))
                    v = wsc[:, q].rearrange("p (n e) -> p n e", n=NW)
                    mark(V.scalar_tensor_tensor(out=v, in0=v, scalar=SCALE, in1=bias, op0=ALU.mult, op1=ALU.add))
                settle()
                flat = lambda v: v.rearrange("p q (n k h) -> p (q n) k h", n=NW, k=WS)
                last = lambda v: flat(v).rearrange("p a k h -> p a h k")
                over = lambda v: v.unsqueeze(2).broadcast_to((P, NW * WS, WS, H))
                seq(V.tensor_reduce(wsm[:, 0], last(wsc), X, ALU.max))
                tt(flat(wsc), flat(wsc), over(wsm[:, 0]), ALU.subtract).then_inc(s_wn["sc"], 1)
                dve.wait_ge(s_wn["ex"], 1)
                seq(V.tensor_reduce(wsm[:, 1], last(wpp), X, ALU.add))
                seq(V.reciprocal(wsm[:, 2], wsm[:, 1]))
                seq(tt(flat(wpp), flat(wpp), over(wsm[:, 2]), ALU.mult))
                for q in range(WS):
                    u = q % 2
                    pr = wpp[:, q].rearrange("p (m h) -> p m h", h=H).unsqueeze(3).broadcast_to((P, K16, H, D))
                    vv = keys[:, :, 2 * C:3 * C].rearrange("p m (h d) -> p m h d", h=H)
                    seq(tt(wprod[:, u].rearrange("p (m h d) -> p m h d", h=H, d=D), pr, vv, ALU.mult))
                    seq(V.tensor_reduce(wo[:, :, q], wprod[:, u].rearrange("p (n k c) -> p n c k", n=NW, k=WS), X, ALU.add))
                for g in range(4):
                    dve.drain().then_inc(s_src, 1)
                for k in range(4):
                    dve.wait_ge(s_wn["pr"], k + 1)
                    xs = x[:, 4 * k:4 * k + 4]
                    seq(tt(xs, xs, b1proj[:].unsqueeze(1).broadcast_to((P, 4, C)), ALU.add))
                    xf = xs.rearrange("p a c -> p (a c)")
                    seq(tt(xf, psum[4 + k][:], xf, ALU.add))

            for s in stages:
                t, i = first_t[s], first_n[s]
                if s in "AC":
                    norm(i, x, xn, t)
                    moe(0, moe_no[s], t)
                elif s == "B":
                    norm(i, x, xn, t)
                    rope_attention(t)
                elif s in "DF":
                    norm(i, x, xn)
                    norm(i + 1, xn, go, t)
                    grouped_attention(t, gqa_no[s])
                    norm(i + 2, go, xn, t + 2)
                    moe(1, moe_no[s], t + 2)
                else:
                    norm(i, x, xn, t)
                    window_attention(t)
            dve.drain().then_inc(s_done, 1)


_INS = ["L0_attn_x", "L0_attn_W_qkv", "L0_attn_W_proj", "L0_ffn_W1", "L0_ffn_b1", "L0_ffn_W2", "L0_ffn_b2",
        "L0_ffn_Wr", "L0_ffn_br", "L1_attn_w_qkv", "L1_attn_b_qkv", "L1_attn_w_proj", "L1_attn_b_proj",
        "L1_attn_bias_table", "L1_ffn_ln1_weight", "L1_ffn_ln1_bias", "L1_ffn_ln2_weight", "L1_ffn_ln2_bias",
        "L1_ffn_qkv_weight", "L1_ffn_proj_weight", "L1_ffn_router_weight", "L1_ffn_moe_w1", "L1_ffn_moe_w2"]


def kernel(**inputs):
    import concourse.bacc as bacc
    from concourse.bass_utils import run_bass_kernel_spmd

    nc = bacc.Bacc("TRN2", target_bir_lowering=False, num_devices=1)
    arrays = {name: np.ascontiguousarray(inputs[name]) for name in _INS}
    arrays["const"] = const_array()
    a = {n: nc.dram_tensor(f"in_{n}_dram", v.shape, mybir.dt.from_np(v.dtype), kind="ExternalInput").ap()
         for n, v in arrays.items()}
    out = nc.dram_tensor("out_0_dram", (B, T, C), F32, kind="ExternalOutput").ap()
    build(nc, a, out)
    r = run_bass_kernel_spmd(nc, [{f"in_{n}_dram": v for n, v in arrays.items()}], core_ids=[0])
    return r.results[0]["out_0_dram"]
```

```python
from contextlib import ExitStack

import numpy as np

import concourse.bass as bass
from concourse import mybir

F32 = mybir.dt.float32
F32R = mybir.dt.float32r
BF16 = mybir.dt.bfloat16
ALU = mybir.AluOpType
ACT = mybir.ActivationFunctionType
X = mybir.AxisListType.X

P = 128
B, T, C = 4, 512, 128
NT = B * T // P
TB = T // P
H, D = 16, 8
E, FF = 8, 512
HB = FF // P
KV = 8
SEQ = 4
CAP = 640
WS, SHIFT = 8, 4
NW = B * T // WS // P
XTW = T + WS
EPS = 1e-5
SCALE = float(D) ** -0.5
MASKED = -1.0e9
HEADS_G = 4
NG = H // HEADS_G
MAX_ROW = 24

CONST_COLS = dict(ident=128, before=128, ones=128, mask_qk=128, mask_kq=128, cos=T, sin=T,
                  one_row=1, rev=128, tile_of=16)
SELECT = ("q_hi", "q_lo", "k_hi", "k_lo")


def const_array():
    c = {n: np.zeros((P, w), np.float32) for n, w in CONST_COLS.items()}
    c |= {n: np.zeros((P, NG * P), np.float32) for n in SELECT}
    i = np.arange(P)
    c["ident"][i, i] = 1
    c["before"][:] = i[:, None] < i[None, :]
    c["ones"][:] = 1
    c["mask_qk"][:] = np.where(i[:, None] >= i[None, :], 0, -1e30)
    c["mask_kq"][:] = c["mask_qk"].T
    half = D // 2
    theta = (1.0 / np.float32(10000.0) ** (np.arange(half, dtype=np.float32) / half)).astype(np.float32)
    freqs = np.outer(np.arange(T, dtype=np.float32), theta).astype(np.float32)
    c["cos"][:] = np.cos(freqs).astype(np.float32).T[i % half]
    c["sin"][:] = np.sin(freqs).astype(np.float32).T[i % half]
    for h in range(H):
        g, j = divmod(h, HEADS_G)
        for d in range(D):
            for name, thirds in (("q_hi", (0, 1)), ("q_lo", (2,)), ("k_hi", (0, 2)), ("k_lo", (1,))):
                for s in thirds:
                    c[name][h * D + d, g * P + 32 * j + D * s + d] = 1
    c["one_row"][MAX_ROW::32] = 1
    c["rev"][:] = E - np.arange(P) % E
    c["tile_of"][i, i // E] = 1
    return np.concatenate([c[n] for n in (*CONST_COLS, *SELECT)], axis=1)


def build(nc, a, out, stages="ABCDEF"):
    ctx = ExitStack()
    with ctx:
        def sb(name, shape, dt=F32):
            return ctx.enter_context(nc.sbuf_tensor(name, shape, dt))

        def sem(name):
            return ctx.enter_context(nc.semaphore(name))

        x = sb("x", [P, NT, C])
        xn = sb("xn", [P, NT, C])
        xT = sb("xT", [P, B, XTW])
        const = sb("constants", [P, sum(CONST_COLS.values())])
        cc, at = {}, 0
        for n, w in CONST_COLS.items():
            cc[n] = const[:, at:at + w]
            at += w
        ident, ones = cc["ident"], cc["ones"]
        small = sb("small", [P, NT, 6])
        mv = sb("mv", [P, NT, 2])
        veps = sb("veps", [P, NT])
        rstd = sb("rstd", [P, NT])
        mhalf = sb("mhalf", [P, NT])
        wr0 = sb("wr0", [P, E])
        br0 = sb("br0", [P, E])
        wr1 = sb("wr1", [P, E])
        b1T = sb("b1T", [P, E * HB])
        b1r = sb("b1r", [E * HB, P])
        b2m = sb("b2m", [P, NT, C])
        gT = sb("gT", [P, P])
        w1 = sb("w1", [P, 2, FF])
        w2 = sb("w2", [P, 2, HB, C])
        w1h = sb("w1h", [P, 2, FF], F32R)
        w1l = sb("w1l", [P, 2, FF], F32R)
        w2h = sb("w2h", [P, 2, HB, C], F32R)
        w2l = sb("w2l", [P, 2, HB, C], F32R)
        xTh = sb("xTh", [P, B, T], F32R)
        xTl = sb("xTl", [P, B, T], F32R)
        bigr = sb("bigr", [P, 8192], F32R)
        rt = sb("rt", [P, 12, NT, E])
        rs = sb("rs", [P, 8, NT])
        gate = sb("gate", [P, NT, E])
        lnw = sb("lnw", [P, 4])
        lnr = sb("lnr", [4, P])
        big = sb("big", [P, 18048])
        w0qkv = sb("w0qkv", [P, 3 * C])
        w0rot = sb("w0rot", [P, 2 * C])
        w0proj = sb("w0proj", [P, C])
        w1qkv = sb("w1qkv", [P, 3 * C])
        b1qkv = sb("b1qkv", [P, 3 * C])
        w1proj = sb("w1proj", [P, C])
        b1proj = sb("b1proj", [P, C])
        btab = sb("btab", [P, 2 * WS - 1, H])
        gq_raw = sb("gq_raw", [P, 2, C])
        gqT = sb("gqT", [P, 2 * C])
        gp_raw = sb("gp_raw", [P, C])
        gpT = sb("gpT", [P, C])
        negid = sb("negid", [P, P], F32R)
        mask = sb("mask", [P, 3, P], BF16)
        hh = bigr[:, 0:4096].rearrange("p (u h t) -> p u h t", u=2, h=HB)
        hl = bigr[:, 4096:8192].rearrange("p (u h t) -> p u h t", u=2, h=HB)
        sel = bigr[:, 0:2048].rearrange("p (i c) -> p i c", i=4)
        kaug = bigr[:, 2048:3072].rearrange("p (u t) -> p u t", u=2)
        qaug = bigr[:, 3072:4096].rearrange("p (u t) -> p u t", u=2)
        qaug2 = bigr[:, 4096:5120].rearrange("p (u t) -> p u t", u=2)
        qk_hl = bigr[:, 5120:7168].rearrange("p (i t) -> p i t", i=4)
        mrow = bigr[:, 7168:7680].rearrange("p (a w) -> p a w", a=TB)

        psum_all = ctx.enter_context(nc.psum_tensor("psum_all", [P, 8, 512], F32))
        psum = [psum_all[:, i, :] for i in range(8)]

        s_in = sem("s_in")
        s_tick = sem("s_tick")
        s_vz = sem("s_vz")
        s_row = sem("s_row")
        s_rope = sem("s_rope")
        s_done = sem("s_done")
        s_out = sem("s_out")
        s_const = sem("s_const")
        s_pool = sem("s_pool")
        s_dve = sem("s_dve")
        s_act = sem("s_act")
        s_setup_ps = sem("s_setup_ps")
        s_setup = sem("s_setup")
        s_var = sem("s_var")
        s_rstd = sem("s_rstd")
        s_src = sem("s_src")
        s_tps = sem("s_tps")
        s_xT = sem("s_xT")
        s_logit = sem("s_logit")
        s_soft = sem("s_soft")
        s_exp = sem("s_exp")
        s_gate = sem("s_gate")
        s_rank = sem("s_rank")
        s_gTp = sem("s_gTp")
        s_gT = sem("s_gT")
        s_gd = sem("s_gd")
        s_gb = [sem("s_gb0"), sem("s_gb1")]
        s_w = [sem("s_w0"), sem("s_w1")]
        s_ws = sem("s_ws")
        s_xTl = sem("s_xTl")
        s_hps = sem("s_hps")
        s_h = sem("s_h")
        s_hl = sem("s_hl")
        s_y = sem("s_y")
        s_c = sem("s_c")
        s_acc = sem("s_acc")
        s_tail = sem("s_tail")
        s_x = sem("s_x")
        s_b2 = sem("s_b2")
        s_split, s_wl, s_hcopy, s_hpart, s_ytmp = map(sem, ("s_split", "s_wl", "s_hcopy", "s_hpart", "s_ytmp"))
        s_selin = sem("s_selin")
        s_sel = sem("s_sel")
        s_xb, s_qk, s_qkd, s_v, s_vd = map(sem, ("s_xb", "s_qk", "s_qkd", "s_v", "s_vd"))
        s_kps, s_kd, s_qps, s_qd = map(sem, ("s_kps", "s_kd", "s_qps", "s_qd"))
        s_s, s_m, s_mt, s_q2 = map(sem, ("s_s", "s_m", "s_mt", "s_q2"))
        s_st, s_p, s_pv, s_o = map(sem, ("s_st", "s_p", "s_pv", "s_o"))
        s_ot, s_at, s_att, s_attT, s_pr, s_xa = map(sem, ("s_ot", "s_at", "s_att", "s_attT", "s_pr", "s_xa"))
        s_g = {n: sem("s_g_" + n) for n in ("qps", "qkv", "sc", "ex", "pr", "ha")}
        s_wn = {n: sem("s_wn_" + n) for n in ("qps", "qkv", "sc", "ex", "pr")}

        big_at = [0]

        def carve(cols, dt=F32):
            v = big[:, big_at[0]:big_at[0] + cols]
            big_at[0] += cols
            return v

        xb = carve(T)
        rope = carve(4 * T).rearrange("p (a t) -> p a t", a=4)
        vaug = carve(TB * H * 32).rearrange("p (k h w) -> p k h w", k=TB, h=H)
        pT = carve(2 * 5 * 1024).rearrange("p (u c w) -> p u c w", u=2, c=5)
        oT = carve(NG * T).rearrange("p (g t) -> p g t", g=NG)
        rden = carve(TB * H).rearrange("p (a h) -> p a h", a=TB)
        att = carve(TB * C).rearrange("p (a c) -> p a c", a=TB)
        attT = carve(T)
        big_at[0] = 0
        gqkv = carve(NT * 256).rearrange("p (t c) -> p t c", t=NT)
        gprod = carve(10 * 512).rearrange("p (i e) -> p i e", i=10)
        gsc = carve(SEQ * SEQ * 64).rearrange("p (s t e) -> p s t e", s=SEQ, t=SEQ)
        gp = carve(SEQ * SEQ * 64).rearrange("p (s t e) -> p s t e", s=SEQ, t=SEQ)
        gsm = carve(4 * 256).rearrange("p (i s e) -> p i s e", i=4, s=SEQ)
        go = carve(NT * C).rearrange("p (t c) -> p t c", t=NT)
        big_at[0] = 0
        wqkv = carve(NW * WS * 3 * C).rearrange("p (n o c) -> p n o c", n=NW, o=WS)
        wprod = carve(2 * NW * WS * C).rearrange("p (u e) -> p u e", u=2)
        wsc = carve(WS * NW * WS * H).rearrange("p (q e) -> p q e", q=WS)
        wpp = carve(WS * NW * WS * H).rearrange("p (q e) -> p q e", q=WS)
        wsm = carve(3 * WS * NW * H).rearrange("p (i a h) -> p i a h", i=3, h=H)
        wo = carve(NW * WS * C).rearrange("p (n o c) -> p n o c", n=NW, o=WS)
        wbr = carve((2 * WS - 1) * H).rearrange("p (r h) -> p r h", h=H)
        xW = wo.rearrange("p n o c -> p (n o c)").rearrange("p (n o w) -> p n o w", n=NW, o=WS)
        big_at[0] = 0
        hid = carve(2 * HB * T).rearrange("p (u h t) -> p u h t", u=2, h=HB)
        accT = carve(B * T).rearrange("p (b t) -> p b t", b=B)
        gbc = carve(2 * B * T).rearrange("p (u b t) -> p u b t", u=2, b=B)
        ytmp = carve(2 * T).rearrange("p (u t) -> p u t", u=2)
        b2rep = ytmp[:, 0, 0:C]
        sel_raw = big[:, 4608:6656].rearrange("p (i c) -> p i c", i=4)
        gates_d = nc.dram_tensor("gates", (E, B * T), F32, kind="Internal").ap()

        block = ctx.enter_context(nc.Block())
        plan = [("AC" if s in "AC" else s) for s in stages]
        t_count = {"A": 1, "B": 1, "C": 1, "D": 3, "E": 2, "F": 3}
        n_count = {"A": 1, "B": 1, "C": 1, "D": 3, "E": 1, "F": 3}
        first_t, first_n, moe_no, gqa_no = {}, {}, {}, {}
        t0 = n0 = m0 = g0 = 0
        for s in stages:
            first_t[s], first_n[s], moe_no[s], gqa_no[s] = t0, n0, m0, g0
            t0, n0 = t0 + t_count[s], n0 + n_count[s]
            m0 += s in "ACDF"
            g0 += s in "DF"
        NCHUNK = E * B
        moe_after = [first_n[s] + n_count[s] - 1 for s in stages if s in "ACDF"]
        sp_e = E // 2

        def groups(t):
            return slice(4 * t, 4 * t + 4)

        kinds = [int(s in "DF") for s in stages if s in "ACDF"]
        rank_no = [sum(kinds[:r]) for r in range(len(kinds))]

        def loads():
            bc = lambda v, n: v.rearrange("(o n) -> o n", o=1).broadcast_to((P, n))
            yield x[:], a["L0_attn_x"].rearrange("b (t p) c -> p (b t) c", p=P)
            yield const[:], a["const"][:, 0:sum(CONST_COLS.values())]
            yield wr0[:], a["L0_ffn_Wr"]
            yield br0[:], bc(a["L0_ffn_br"], E)
            yield wr1[:], a["L1_ffn_router_weight"]
            yield b1r[:], a["L0_ffn_b1"].rearrange("e (h p) -> (e h) p", p=P)
            yield b2rep, a["L0_ffn_b2"].rearrange("(o e) c -> o e c", o=1).broadcast_to((NT, E, C))
            yield w0qkv[:], a["L0_attn_W_qkv"]
            yield w0proj[:], a["L0_attn_W_proj"]
            yield w1qkv[:], a["L1_attn_w_qkv"]
            yield b1qkv[:], bc(a["L1_attn_b_qkv"], 3 * C)
            yield w1proj[:], a["L1_attn_w_proj"]
            yield b1proj[:], bc(a["L1_attn_b_proj"], C)
            first = (WS - 1) * (2 * WS - 1)
            rows = a["L1_attn_bias_table"][first:first + 2 * WS - 1, :]
            yield btab[:], rows.rearrange("(o r) h -> o r h", o=1).broadcast_to((P, 2 * WS - 1, H))
            yield gq_raw[:], a["L1_ffn_qkv_weight"].rearrange("(i p) c -> p i c", p=P)
            yield gp_raw[:], a["L1_ffn_proj_weight"]
            for i, n in enumerate(("ln1_weight", "ln1_bias", "ln2_weight", "ln2_bias")):
                yield lnr[i:i + 1, :], a["L1_ffn_" + n].rearrange("(o n) -> o n", o=1)

        N_IN = 16 * 20

        @block.sync
        def _(sp):
            n_in = 0
            for tile, src in loads():
                sp.dma_start(tile, src).then_inc(s_in, 16)
            for s in stages:
                if s == "B":
                    sp.wait_ge(s_rope, 1)
                    sp.dma_start(sel_raw, a["const"][:, sum(CONST_COLS.values()):].rearrange("p (i c) -> p i c", i=4)).then_inc(s_selin, 16)
                if s not in "ACDF":
                    continue
                r = moe_no[s]
                w1_d, w2_d = (a["L0_ffn_W1"], a["L0_ffn_W2"]) if s in "AC" else (a["L1_ffn_moe_w1"], a["L1_ffn_moe_w2"])

                def weights(e, u, i):
                    sp.wait_ge(s_ws, 2 * i + u + r * E + 1)
                    sp.dma_start(w1[:, u], w1_d[e].rearrange("e p f -> (e p) f")).then_inc(s_w[u], 16)
                    sp.dma_start(w2[:, u], w2_d[e].rearrange("e (h p) c -> p (e h) c", p=P)).then_inc(s_w[u], 16)

                def gates(e, u, i):
                    sp.wait_ge(s_c, 8 * i + 4 * u + r * NCHUNK + 4)
                    sp.dma_start(gbc[:, u], gates_d[e].rearrange("e (b t) -> e b t", b=B).broadcast_to((P, B, T))).then_inc(s_gb[u], 16)

                for u in range(2):
                    weights(slice(u, u + 1), u, 0)
                sp.wait_ge(s_gd, 16 * (r + 1))
                with sp.Fori(0, E // 2 - 1) as i:
                    for u in range(2):
                        gates(bass.ds(2 * i + u, 1), u, i)
                        weights(bass.ds(2 * i + (2 + u), 1), u, i + 1)
                for u in range(2):
                    gates(slice(E - 2 + u, E - 1 + u), u, E // 2 - 1)
            sp.wait_ge(s_done, 1)
            sp.dma_start(out.rearrange("b (t p) c -> p (b t) c", p=P), x[:]).then_inc(s_out, 16)
            sp.wait_ge(s_out, 16)


        @block.gpsimd
        def _(pool):
            nc.gpsimd.memset(mhalf[:], -0.5).then_inc(s_pool, 1)
            pool.wait_ge(s_pool, 1)
            for n in range(n0):
                pool.wait_ge(s_var, n + 1)
                nc.gpsimd.tensor_tensor(rstd[:], veps[:], mhalf[:], ALU.pow).then_inc(s_rstd, 1)
                if n in moe_after:
                    r = moe_after.index(n)
                    pool.wait_ge(s_gT, r + 1)
                    pool.dma_start(gates_d.rearrange("e (t p) -> t e p", p=P), gT[:]).then_inc(s_gd, 16)
                    nc.gpsimd.memset(accT, 0.0).then_inc(s_acc, 1)

        @block.tensor
        def _(pe):
            mm = nc.tensor.matmul
            pe.sem_inc(s_y, 5)
            rows_done = [0]
            pe.wait_ge(s_in, N_IN)
            nc.tensor.transpose(psum[4][:, 0:E * HB], b1r[:], ident[0:E * HB, 0:E * HB])
            nc.tensor.transpose(psum[4][:, 32:36], lnr[:], ident[0:4, 0:4])
            nc.tensor.transpose(psum[4][:, 128:256], gp_raw[:], ident)
            for i in range(2):
                last = nc.tensor.transpose(psum[4][:, 256 + 128 * i:384 + 128 * i], gq_raw[:, i], ident)
            last.then_inc(s_setup_ps, 1)

            def turn(t, src):
                for g in range(4):
                    pe.wait_ge(s_src, 4 * t + g + 1)
                    for k in range(4):
                        ins = nc.tensor.transpose(psum[g][:, P * k:P * k + P], src(4 * g + k), ident)
                    ins.then_inc(s_tps, 1)

            def moe(kind, r, t):
                pe.wait_ge(s_xT, 4 * t + 4)
                for k in range(NT):
                    ins = mm(psum[7][:, E * k:E * k + E], xT[:, k // 4, P * (k % 4):P * (k % 4) + P],
                             (wr0 if kind == 0 else wr1)[:], start=True, stop=True)
                ins.then_inc(s_logit, 1)

                def first(i, m):
                    u, c = m // 4 % 2, m % 4
                    if c == 0:
                        pe.wait_ge(s_ws, 2 * i + r * E + m // 4 + 3)
                    for h in range(HB):
                        pe.wait_ge(s_h, 32 * i + r * NCHUNK * HB + 4 * m + h + 1)
                        hs = slice(P * h, P * h + P)
                        mm(psum[h][:], w1h[:, u, hs], xTh[:, c], start=True, stop=False)
                        mm(psum[h][:], w1h[:, u, hs], xTl[:, c], start=False, stop=False)
                        mm(psum[h][:], w1l[:, u, hs], xTh[:, c], start=False, stop=True).then_inc(s_hps, 1)

                def second(i, m):
                    u, c = m // 4, m % 4
                    pe.wait_ge(s_hl, 8 * i + r * NCHUNK + m + 1)
                    pe.wait_ge(s_c, 8 * i + r * NCHUNK + m + 7)
                    for h in range(HB):
                        y, v = psum[4 + m % 2][:], m % 2
                        mm(y, w2h[:, u, h], hh[:, v, h], start=(h == 0), stop=False)
                        mm(y, w2h[:, u, h], hl[:, v, h], start=False, stop=False)
                        ins = mm(y, w2l[:, u, h], hh[:, v, h], start=False, stop=(h == HB - 1))
                    ins.then_inc(s_y, 1)

                pe.wait_ge(s_xTl, 4 * r + 4)
                first(0, 0)
                if kind == 1:
                    pe.wait_ge(s_gate, 2 * r + 1)
                    chosen = rt[:, 10].rearrange("p t e -> p (t e)")
                    mm(psum[7][:, 0:P], cc["before"], chosen, start=True, stop=True)
                    mm(psum[7][:, P:2 * P], ones, chosen, start=True, stop=True).then_inc(s_rank, 1)
                pe.wait_ge(s_gate, 2 * r + 2)
                nc.tensor.transpose(psum[7][:, 0:P], gate[:].rearrange("p t e -> p (t e)"), ident).then_inc(s_gTp, 1)
                last = E // 2 - 1
                with pe.Fori(0, last) as i:
                    for m in range(8):
                        first(i, m + 1)
                        second(i, m)
                for m in range(8):
                    if m < 7:
                        first(last, m + 1)
                    second(last, m)
                if kind == 0:
                    pe.wait_ge(s_b2, 1)
                for c in range(B):
                    pe.wait_ge(s_c, (r + 1) * NCHUNK + 8 - (B - 1 - c))
                    if c < 2:
                        pe.wait_ge(s_c, (r + 1) * NCHUNK + 8 - (1 - c))
                    else:
                        pe.wait_ge(s_x, 4 * r + c - 1)
                    for k in range(4):
                        ins = mm(psum[4 + c % 2][:, P * k:P * k + P], accT[:, c, P * k:P * k + P], ident,
                                 start=True, stop=(kind == 1))
                        if kind == 0:
                            ins = mm(psum[4 + c % 2][:, P * k:P * k + P], gT[:], b2m[:, 4 * c + k], start=False, stop=True)
                    ins.then_inc(s_tail, 1)

            def rope_attention(t):
                pe.wait_ge(s_xT, 4 * t + 4)
                for b in range(B):
                    pe.wait_ge(s_xb, b + 1)
                    for n, w in enumerate((w0qkv[:, 0:C], w0rot[:, 0:C], w0qkv[:, C:2 * C], w0rot[:, C:2 * C])):
                        ins = mm(psum[2 + n][:], w, xb, start=True, stop=True)
                    ins.then_inc(s_qk, 1)
                    for k in range(TB):
                        ins = mm(psum[7][:, P * k:P * k + P], xb[:, P * k:P * k + P], w0qkv[:, 2 * C:3 * C],
                                 start=True, stop=True)
                    ins.then_inc(s_v, 1)

                    def prep(g):
                        n = b * NG + g
                        pe.wait_ge(s_vd, b + 1)
                        if n >= 1:
                            pe.wait_ge(s_q2, n)
                        pe.wait_ge(s_qkd, b + 1)
                        mm(psum[7][:], sel[:, 2, P * g:P * g + P], qk_hl[:, 2], start=True, stop=False)
                        mm(psum[7][:], sel[:, 3, P * g:P * g + P], qk_hl[:, 3], start=False, stop=True).then_inc(s_kps, 1)
                        if g >= 1:
                            pe.wait_ge(s_qd, n)
                        if g >= 2:
                            pe.wait_ge(s_o, n - 1)
                        if g == 0 and b:
                            pe.wait_ge(s_xa, b)
                        mm(psum[6][:], sel[:, 0, P * g:P * g + P], qk_hl[:, 0], start=True, stop=False)
                        mm(psum[6][:], sel[:, 1, P * g:P * g + P], qk_hl[:, 1], start=False, stop=True).then_inc(s_qps, 1)

                    def score(m, col, qt, j, g):
                        rows, w = slice(32 * j, 32 * j + 32), P * (qt + 1)
                        mm(psum[m % 2][:, col:col + w], qaug[rows, g % 2, P * qt:P * qt + P], kaug[rows, g % 2, 0:w],
                           start=True, stop=False, skip_group_check=True)
                        return mm(psum[m % 2][:, col + P * qt:col + w], mask[:, 0], mask[:, 1],
                                  start=False, stop=True, skip_group_check=True)

                    def score_chunks(g):
                        n = b * NG + g
                        pe.wait_ge(s_kd, n + 1)
                        pe.wait_ge(s_qd, n + 1)
                        for c in range(8):
                            m = n * 12 + c
                            if m >= 2:
                                pe.wait_ge(s_m, m - 1)
                            score(m, 0, 3 - c // 4, c % 4, g).then_inc(s_s, 1)
                            yield
                        for qt in (1, 0):
                            m = n * 12 + 10 - 2 * qt
                            for i in range(2):
                                pe.wait_ge(s_m, m - 1 + i)
                                score(m + i, 0, qt, 2 * i, g).then_inc(s_row, 1)
                                rows_done[0] += 1
                            for i in range(2):
                                pe.wait_ge(s_row, rows_done[0] - 1 + i)
                                score(m + i, P * (qt + 1), qt, 2 * i + 1, g).then_inc(s_s, 1)
                            yield

                    def exp_chunks(g):
                        n = b * NG + g
                        pe.wait_ge(s_q2, n + 1)
                        for c in range(5):
                            m = n * 5 + c
                            if m >= 2:
                                pe.wait_ge(s_p, m - 1)
                            bank = 2 + 2 * (m % 2)
                            if c != 2:
                                j = c if c < 2 else c - 1
                                parts = [(bank, 0, j, 0), (bank + 1, 0, j, 1), (bank + 1, 384, j, 3)]
                            else:
                                parts = [(bank + j // 2, 256 * (j % 2), j, 2) for j in (0, 2, 1, 3)]
                            for i, (bk, col, j, kt) in enumerate(parts):
                                if c == 2 and i >= 2:
                                    pe.wait_ge(s_row, rows_done[0] - 1 + i - 2)
                                rows = slice(32 * j, 32 * j + 32)
                                w = T - P * kt
                                mm(psum[bk][:, col:col + w], kaug[rows, g % 2, P * kt:P * kt + P], qaug2[rows, g % 2, P * kt:T],
                                   start=True, stop=False, skip_group_check=True)
                                ins = mm(psum[bk][:, col:col + P], mask[:, 0], mask[:, 2], start=False, stop=True, skip_group_check=True)
                                if c == 2 and i < 2:
                                    ins.then_inc(s_row, 1)
                                    rows_done[0] += 1
                            ins.then_inc(s_st, 1)
                            yield

                    def maxima(g):
                        n = b * NG + g
                        pe.wait_ge(s_m, (n + 1) * 12)
                        pe.wait_ge(s_kd, n + 1)
                        for qt in range(TB):
                            ins = mm(psum[7][:, P * qt:P * qt + P], mrow[:, qt], negid[:], start=True, stop=True)
                        ins.then_inc(s_mt, 1)

                    def values(g):
                        n = b * NG + g
                        pe.wait_ge(s_p, (n + 1) * 5)
                        pe.wait_ge(s_qd, min(n + 2, b * NG + NG))
                        for kt in range(TB):
                            for j in range(4):
                                h = 4 * g + j
                                if kt == 2:
                                    src = pT[:, g % 2, 2, 256 * j:256 * j + 256]
                                else:
                                    c = j if j < 2 else j + 1
                                    o = {0: 0, 1: 512, 3: 896}[kt]
                                    src = pT[:, g % 2, c, o:o + T - P * kt]
                                ins = mm(psum[6][32 * j:32 * j + 32, P * kt:T], vaug[:, kt, h, :], src,
                                         start=(kt == 0), stop=(kt == TB - 1))
                        ins.then_inc(s_pv, 1)

                    prep(0)
                    for _ in score_chunks(0):
                        pass
                    for g in range(NG):
                        maxima(g)
                        more = iter(())
                        if g + 1 < NG:
                            prep(g + 1)
                            more = score_chunks(g + 1)
                        for _ in exp_chunks(g):
                            next(more, None)
                            next(more, None)
                        for _ in more:
                            pass
                        values(g)
                    for qt in range(TB):
                        m = 4 * b + qt
                        pe.wait_ge(s_o, NG * (b + 1))
                        if m >= 2 and qt >= 2:
                            pe.wait_ge(s_at, m - 1)
                        for g in range(NG):
                            ins = nc.tensor.transpose(psum[qt % 2][:, P * g:P * g + P], oT[:, g, P * qt:P * qt + P], ident)
                        ins.then_inc(s_ot, 1)
                    pe.wait_ge(s_at, 4 * b + 4)
                    for qt in range(TB):
                        ins = nc.tensor.transpose(psum[7][:, P * qt:P * qt + P], att[:, qt], ident)
                    ins.then_inc(s_att, 1)
                    pe.wait_ge(s_attT, b + 1)
                    for qt in range(TB):
                        ins = mm(psum[6][:, P * qt:P * qt + P], attT[:, P * qt:P * qt + P], w0proj[:], start=True, stop=True)
                    ins.then_inc(s_pr, 1)

            def grouped_attention(t, q):
                pe.wait_ge(s_xT, 4 * t + 4)
                for k in range(NT // 2):
                    m = q * 8 + k
                    if k >= 2:
                        pe.wait_ge(s_g["qkv"], m - 1)
                    for i in range(2):
                        ins = mm(psum[4 + k % 2][:, 256 * i:256 * i + 256],
                                 xT[:, k // 2, P * (2 * k + i - 4 * (k // 2)):P * (2 * k + i - 4 * (k // 2)) + P], gqT[:],
                                 start=True, stop=True)
                    ins.then_inc(s_g["qps"], 1)
                turn(t + 1, lambda k: go[:, k, :])
                for k in range(4):
                    pe.wait_ge(s_xT, 4 * (t + 1) + k + 1)
                    for i in range(4):
                        ins = mm(psum[4 + k][:, P * i:P * i + P], xT[:, k, P * i:P * i + P], gpT[:], start=True, stop=True)
                    ins.then_inc(s_g["pr"], 1)

            def window_attention(t):
                pe.wait_ge(s_xT, 4 * t + 4)
                for k in range(NW * WS):
                    n, o = divmod(k, WS)
                    if k >= 2:
                        pe.wait_ge(s_wn["qkv"], k - 1)
                    mm(psum[4 + k % 2][:, 0:3 * C], xW[:, n, o], w1qkv[:], start=True, stop=True).then_inc(s_wn["qps"], 1)
                turn(t + 1, lambda k: wo[:, k // WS, k % WS, :])
                for k in range(4):
                    pe.wait_ge(s_xT, 4 * (t + 1) + 4)
                    for i in range(4):
                        ins = mm(psum[4 + k][:, P * i:P * i + P], xT[:, k, P * i:P * i + P], w1proj[:], start=True, stop=True)
                    ins.then_inc(s_wn["pr"], 1)

            for s in stages:
                t = first_t[s]
                pe.wait_ge(s_setup, 1)
                turn(t, (lambda k: go[:, k, :]) if s in "DF" else (lambda k: xn[:, k, :]))
                if s in "AC":
                    moe(0, moe_no[s], t)
                elif s == "B":
                    pe.wait_ge(s_sel, 1)
                    rope_attention(t)
                elif s in "DF":
                    grouped_attention(t, gqa_no[s])
                    turn(t + 2, lambda k: xn[:, k, :])
                    moe(1, moe_no[s], t + 2)
                else:
                    window_attention(t)


        @block.scalar
        def _(act):
            A = nc.scalar.activation
            act.sem_inc(s_h, 4)
            act.wait_ge(s_in, N_IN)
            act.wait_ge(s_setup_ps, 1)
            A(b1T[:], psum[4][:, 0:E * HB], ACT.Identity).then_inc(s_act, 1)
            A(lnw[:], psum[4][:, 32:36], ACT.Identity).then_inc(s_act, 1)
            A(gpT[:], psum[4][:, 128:256], ACT.Identity).then_inc(s_act, 1)
            A(gqT[:], psum[4][:, 256:512], ACT.Identity).then_inc(s_act, 1)
            act.wait_ge(s_act, 4)
            act.drain().then_inc(s_setup, 1)
            chain = [4]

            def turned(t, mode, split=False):
                for g in range(4):
                    act.wait_ge(s_tps, 4 * t + g + 1)
                    src = psum[g][:]
                    if mode == "windows":
                        n, o0 = g // 2, 4 * (g % 2)
                        dst = xT[:, 2 * n:2 * n + 2, SHIFT + o0:SHIFT + o0 + T]
                        dst = dst.rearrange("p b (w o) -> p b w o", o=WS)[:, :, :, 0:4]
                        ins = None
                        for o in range(4):
                            ins = A(dst[:, :, :, o], src[:, P * o:P * o + P].rearrange("p (b w) -> p b w", b=2), ACT.Identity)
                            if o < 3 or g == 3:
                                ins.then_inc(s_act, 1)
                                chain[0] += 1
                        if g == 3:
                            act.wait_ge(s_act, chain[0])
                            act.wait_ge(s_xT, 4 * t + 3)
                            ins = A(xT[:, :, 0:SHIFT], xT[:, :, T:T + SHIFT], ACT.Identity)
                        ins.then_inc(s_xT, 1)
                        continue
                    if mode == "to windows":
                        nw = T // WS
                        dst = xW[:, g // 2, :, nw * (g % 2):nw * (g % 2) + nw]
                        A(dst[:, :, 0:nw - 1], src[:, SHIFT:T - SHIFT].rearrange("p (w o) -> p o w", o=WS), ACT.Identity)
                        A(dst[:, 0:SHIFT, nw - 1], src[:, T - SHIFT:T], ACT.Identity)
                        A(dst[:, SHIFT:WS, nw - 1], src[:, 0:SHIFT], ACT.Identity).then_inc(s_xT, 1)
                        continue
                    affine = dict(scale=lnw[:, mode:mode + 1], bias=lnw[:, mode + 1:mode + 2]) if mode in (0, 2) else {}
                    ins = A(xT[:, g, 0:T], src, ACT.Identity, **affine)
                    if split:
                        ins = A(xTh[:, g], src, ACT.Identity, **affine)
                    ins.then_inc(s_xT, 1)

            def moe(kind, r):
                act.wait_ge(s_soft, r + 1)
                A(rt[:, 1], rt[:, 0], ACT.Exp).then_inc(s_exp, 1)
                act.wait_ge(s_gTp, r + 1)
                A(gT[:], psum[7][:, 0:P], ACT.Identity).then_inc(s_gT, 1)

            def experts(kind, r):
                moe(kind, r)
                with act.Fori(0, E // 2) as i:
                    for m in range(8):
                        hidden(kind, r, i, m)

            def hidden(kind, r, i, m):
                u, c = m // 4, m % 4
                act.wait_ge(s_y, 8 * i + r * NCHUNK + m + 4)
                for h in range(HB):
                    act.wait_ge(s_hps, 32 * i + r * NCHUNK * HB + 4 * m + h + 1)
                    if kind == 0:
                        act.sem_inc(s_tick, 1)
                        bias = b1T[:, bass.ds(i * (2 * HB) + (u * HB + h), 1)]
                        act_of = lambda dst: A(dst, psum[h][:], ACT.Relu, bias=bias)
                    else:
                        act_of = lambda dst: A(dst, psum[h][:], ACT.Gelu)
                    ins = act_of(hid[:, m % 2, h])
                    if h < HB - 1:
                        ins = act_of(hh[:, m % 2, h])
                    ins.then_inc(s_h, 1)

            def rope_attention(t):
                act.wait_ge(s_xT, 4 * t + 4)
                for b in range(B):
                    if b:
                        act.wait_ge(s_v, b)
                    A(xb, xT[:, b, 0:T], ACT.Identity).then_inc(s_xb, 1)
                    act.wait_ge(s_v, b + 1)
                    act.wait_ge(s_vz, 1)
                    A(vaug[:, :, :, 0:D], psum[7][:].rearrange("p (k h d) -> p k h d", k=TB, h=H), ACT.Identity).then_inc(s_vd, 1)

                    def keys(g):
                        n = b * NG + g
                        act.wait_ge(s_kps, n + 1)
                        A(kaug[:, g % 2], psum[7][:], ACT.Identity, bias=cc["one_row"]).then_inc(s_kd, 1)

                    keys(0)
                    for g in range(NG):
                        n = b * NG + g
                        if g + 1 < NG:
                            keys(g + 1)
                        for c in range(5):
                            act.wait_ge(s_st, n * 5 + c + 1)
                            bank = 2 + 2 * ((n * 5 + c) % 2)
                            A(pT[:, g % 2, c], psum_all[:, bank:bank + 2, :].rearrange("p b w -> p (b w)"), ACT.Exp, scale=SCALE).then_inc(s_p, 1)
                        act.wait_ge(s_pv, n + 1)
                        A(oT[:, g], psum[6][:], ACT.Identity).then_inc(s_o, 1)
                    act.wait_ge(s_att, b + 1)
                    A(attT, psum[7][:], ACT.Identity).then_inc(s_attT, 1)

            for s in stages:
                t = first_t[s]
                if s in "AC":
                    turned(t, "plain", split=True)
                    experts(0, moe_no[s])
                elif s == "B":
                    turned(t, "plain")
                    rope_attention(t)
                elif s in "DF":
                    turned(t, 0)
                    q = gqa_no[s]
                    act.wait_ge(s_g["sc"], q + 1)
                    A(gp, gsc, ACT.Exp, scale=SCALE).then_inc(s_g["ex"], 1)
                    turned(t + 1, "plain")
                    turned(t + 2, 2, split=True)
                    experts(1, moe_no[s])
                else:
                    turned(t, "to windows")
                    act.wait_ge(s_wn["sc"], 1)
                    A(wpp, wsc, ACT.Exp).then_inc(s_wn["ex"], 1)
                    turned(t + 1, "windows")

        @block.vector
        def _(dve):
            V = nc.vector
            n = [0]

            def mark(ins):
                ins.then_inc(s_dve, 1)
                n[0] += 1

            def settle():
                dve.wait_ge(s_dve, n[0])

            def seq(ins):
                mark(ins)
                settle()

            tt = V.tensor_tensor
            dve.wait_ge(s_in, N_IN)
            dve.sem_inc(s_ws, 2)
            dve.sem_inc(s_c, 8)
            tt(b2m[:], b2rep.unsqueeze(1).broadcast_to((P, NT, C)), cc["tile_of"].unsqueeze(2).broadcast_to((P, NT, C)),
               ALU.mult).then_inc(s_b2, 1)
            V.tensor_scalar(negid[:], ident, -1.0, None, ALU.mult).then_inc(s_const, 1)
            for i, name in enumerate(("ident", "mask_qk", "mask_kq")):
                V.tensor_copy(mask[:, i], cc[name]).then_inc(s_const, 1)
            src = w0qkv[:, 0:2 * C].rearrange("p (a z d) -> p a z d", z=2, d=D // 2)
            dst = w0rot[:].rearrange("p (a z d) -> p a z d", z=2, d=D // 2)
            V.tensor_scalar(dst[:, :, 0], src[:, :, 1], -1.0, None, ALU.mult).then_inc(s_const, 1)
            V.tensor_copy(dst[:, :, 1], src[:, :, 0]).then_inc(s_const, 1)
            V.memset(veps[:], 0.0).then_inc(s_const, 1)
            V.memset(rt[:, 11], 0.0).then_inc(s_const, 1)
            dve.wait_ge(s_b2, 1)
            dve.wait_ge(s_const, 8)

            def norm(i, src, dst, turn=None):
                for k in range(NT):
                    mark(V.bn_stats(small[:, k], src[:, k]))
                settle()
                for k in range(NT):
                    mark(V.bn_aggr(mv[:, k], small[:, k]))
                settle()
                V.tensor_scalar(veps[:], mv[:, :, 1], EPS, None, ALU.add).then_inc(s_var, 1)
                dve.wait_ge(s_rstd, i + 1)
                for k in range(NT):
                    ins = V.tensor_scalar(dst[:, k], src[:, k], mv[:, k, 0:1], rstd[:, k:k + 1], ALU.subtract, ALU.mult)
                    if turn is not None and k % 4 == 3:
                        ins.then_inc(s_src, 1)
                    else:
                        mark(ins)
                if turn is not None:
                    dve.wait_ge(s_src, 4 * turn + 4)
                settle()

            def moe(kind, r, t, base_tile=None):
                L, Pr, eq, oh1, p2, oh2 = (rt[:, i] for i in (0, 1, 2, 3, 4, 5))
                bc = lambda v: v.unsqueeze(2).broadcast_to((P, NT, E))
                split_weights(0, 0, r)
                for g in range(4):
                    dve.wait_ge(s_xT, 4 * t + g + 1)
                    tt(xTl[:, g], xT[:, g, 0:T], xTh[:, g].bitcast(F32), ALU.subtract).then_inc(s_xTl, 1)
                dve.wait_ge(s_logit, r + 1)
                ps = psum[7][:, 0:P].rearrange("p (t e) -> p t e", e=E)
                if kind == 0:
                    seq(tt(L, ps, br0[:].unsqueeze(1).broadcast_to((P, NT, E)), ALU.add))
                else:
                    seq(V.tensor_copy(L, ps))
                seq(V.tensor_reduce(rs[:, 0], L, X, ALU.max))
                tt(L, L, bc(rs[:, 0]), ALU.subtract).then_inc(s_soft, 1)
                dve.wait_ge(s_exp, r + 1)
                seq(V.tensor_reduce(rs[:, 1], Pr, X, ALU.add))
                seq(V.reciprocal(rs[:, 2], rs[:, 1]))
                seq(tt(Pr, Pr, bc(rs[:, 2]), ALU.mult))
                rev = cc["rev"].rearrange("p (t e) -> p t e", e=E)
                for src, top, onehot in ((Pr, 3, oh1), (p2, 4, oh2)):
                    seq(V.tensor_reduce(rs[:, top], src, X, ALU.max))
                    seq(tt(eq, src, bc(rs[:, top]), ALU.is_equal))
                    seq(tt(eq, eq, rev, ALU.mult))
                    seq(V.tensor_reduce(rs[:, 5], eq, X, ALU.max))
                    seq(tt(onehot, eq, bc(rs[:, 5]), ALU.is_equal))
                    if top == 3:
                        seq(V.scalar_tensor_tensor(out=p2, in0=oh1, scalar=-2.0, in1=Pr, op0=ALU.mult, op1=ALU.add))
                seq(tt(rs[:, 6], rs[:, 3], rs[:, 4], ALU.add))
                seq(V.reciprocal(rs[:, 7], rs[:, 6]))
                chosen = rt[:, 10]
                seq(tt(chosen, oh1, oh2, ALU.add))
                if kind == 1:
                    dve.drain().then_inc(s_gate, 1)
                seq(tt(gate[:], Pr, chosen, ALU.mult))
                seq(V.scalar_tensor_tensor(out=gate[:], in0=gate[:], scalar=0.5, in1=bc(rs[:, 7]), op0=ALU.mult, op1=ALU.mult))
                if kind == 1:
                    dve.wait_ge(s_rank, rank_no[r] + 1)
                    tot = psum[7][:, P:2 * P].rearrange("p (t e) -> p t e", e=E)
                    mark(V.tensor_copy(rt[:, 6, 1:NT], tot[:, 0:NT - 1]))
                    seq(V.tensor_copy(rt[:, 6, 0:1], rt[:, 11, 0:1]))
                    cur, other, step = 6, 7, 1
                    while step < NT:
                        mark(tt(rt[:, other, step:NT], rt[:, cur, step:NT], rt[:, cur, 0:NT - step], ALU.add))
                        seq(V.tensor_copy(rt[:, other, 0:step], rt[:, cur, 0:step]))
                        cur, other, step = other, cur, 2 * step
                    seq(tt(rt[:, 8], psum[7][:, 0:P].rearrange("p (t e) -> p t e", e=E), rt[:, cur], ALU.add))
                    seq(V.tensor_scalar(rt[:, 9], rt[:, 8], float(CAP), None, ALU.is_lt))
                    seq(tt(gate[:], gate[:], rt[:, 9], ALU.mult))
                dve.drain().then_inc(s_gate, 1 if kind == 1 else 2)
                experts(kind, r)

            def split_weights(i, e, r):
                u, k = e % 2, e // 2
                dve.wait_ge(s_w[u], 32 * i + 32 * (r * (E // 2) + k + 1))
                dve.wait_ge(s_y, 8 * i + r * NCHUNK + 4 * e + 1)
                raw = (w1[:, u], w2[:, u])
                for src, hi, lo in zip(raw, (w1h[:, u], w2h[:, u]), (w1l[:, u], w2l[:, u])):
                    V.tensor_copy(hi, src).then_inc(s_split, 1)
                dve.wait_ge(s_split, 2 * (2 * i + e + r * E) + 2)
                tt(w1l[:, u], w1[:, u], w1h[:, u].bitcast(F32), ALU.subtract).then_inc(s_wl, 1)
                tt(w2l[:, u], w2[:, u], w2h[:, u].bitcast(F32), ALU.subtract).then_inc(s_ws, 1)

            def split_hidden(i, m, r):
                v = m % 2
                n4 = r * NCHUNK * HB + 4 * m + 4
                dve.wait_ge(s_h, 32 * i + n4 + 4)
                V.tensor_copy(hh[:, v, HB - 1], hid[:, v, HB - 1]).then_inc(s_hcopy, 1)
                for h in range(HB - 1):
                    tt(hl[:, v, h], hid[:, v, h], hh[:, v, h].bitcast(F32), ALU.subtract).then_inc(s_hpart, 1)
                dve.wait_ge(s_hcopy, 8 * i + r * NCHUNK + m + 1)
                tt(hl[:, v, HB - 1], hid[:, v, HB - 1], hh[:, v, HB - 1].bitcast(F32), ALU.subtract).then_inc(s_hl, 1)

            def add_up(i, m, r):
                u, c = m // 4, m % 4
                if c == 0:
                    dve.wait_ge(s_gb[u], 16 * i + 16 * (r * (E // 2) + 1))
                dve.wait_ge(s_y, 8 * i + r * NCHUNK + m + 6)
                tt(ytmp[:, m % 2], psum[4 + m % 2][:], gbc[:, u, c], ALU.mult).then_inc(s_ytmp, 1)
                dve.wait_ge(s_ytmp, 8 * i + r * NCHUNK + m + 1)
                dve.wait_ge(s_c, 8 * i + r * NCHUNK + m + 5)
                tt(accT[:, c], accT[:, c], ytmp[:, m % 2], ALU.add).then_inc(s_c, 1)

            def experts(kind, r):
                split_hidden(0, 0, r)
                dve.wait_ge(s_acc, r + 1)
                last = E // 2 - 1

                def step(i, m):
                    if m == 1:
                        split_weights(i, 1, r)
                    if m == 5 and not (isinstance(i, int) and i == last):
                        split_weights(i, 2, r)
                    if not (isinstance(i, int) and m == 7):
                        split_hidden(i, m + 1, r)
                    add_up(i, m, r)

                with dve.Fori(0, last) as i:
                    for m in range(8):
                        step(i, m)
                for m in range(8):
                    step(last, m)
                for c in range(B):
                    xs = x[:, 4 * c:4 * c + 4]
                    if kind == 1:
                        seq(V.scalar_tensor_tensor(out=xs, in0=go[:, 4 * c:4 * c + 4], scalar=0.5, in1=xs, op0=ALU.mult, op1=ALU.add))
                    dve.wait_ge(s_tail, 4 * r + c + 1)
                    xf = xs.rearrange("p a c -> p (a c)")
                    tt(xf, psum[4 + c % 2][:], xf, ALU.add).then_inc(s_x, 1)
                dve.wait_ge(s_x, 4 * r + 4)

            def rope_attention(t):
                dve.drain().then_inc(s_rope, 1)
                seq(V.memset(vaug, 0.0))
                mark(V.memset(mrow.bitcast(F32), 0.0))
                dve.wait_ge(s_selin, 16)
                V.tensor_copy(sel, sel_raw).then_inc(s_sel, 1)
                dve.wait_ge(s_sel, 1)
                settle()
                V.memset(vaug[:, :, :, D:D + 1], 1.0).then_inc(s_vz, 1)
                for b in range(B):
                    dve.wait_ge(s_qk, b + 1)
                    for i in range(2):
                        mark(tt(rope[:, 2 * i], psum[2 + 2 * i][:], cc["cos"], ALU.mult))
                        mark(tt(rope[:, 2 * i + 1], psum[3 + 2 * i][:], cc["sin"], ALU.mult))
                    settle()
                    for i in range(2):
                        mark(tt(rope[:, 2 * i], rope[:, 2 * i], rope[:, 2 * i + 1], ALU.add))
                    settle()
                    for i in range(2):
                        mark(V.tensor_copy(qk_hl[:, 2 * i], rope[:, 2 * i]))
                    settle()
                    for i in range(2):
                        seq(tt(qk_hl[:, 2 * i + 1], rope[:, 2 * i], qk_hl[:, 2 * i].bitcast(F32), ALU.subtract))
                    dve.drain().then_inc(s_qkd, 1)

                    def queries(g):
                        n_ = b * NG + g
                        dve.wait_ge(s_qps, n_ + 1)
                        V.tensor_copy(qaug[:, g % 2], psum[6][:]).then_inc(s_qd, 1)

                    def row_max(g):
                        n_ = b * NG + g
                        if n_:
                            dve.wait_ge(s_mt, n_)
                        chunks = [(3, 0, 1), (3, 1, 1), (3, 2, 1), (3, 3, 1), (2, 0, 1), (2, 1, 1), (2, 2, 1), (2, 3, 1),
                                  (1, 0, 2), (1, 2, 2), (0, 0, 2), (0, 2, 2)]
                        for c, (qt, j, nh) in enumerate(chunks):
                            m = n_ * 12 + c
                            dve.wait_ge(s_s, m + 1)
                            w = P * (qt + 1)
                            src = psum[m % 2][:, 0:w * nh].rearrange("p (h k) -> p h k", h=nh)
                            dst = mrow[:, qt, 32 * j + MAX_ROW:32 * (j + nh - 1) + MAX_ROW + 1:32]
                            V.tensor_reduce(dst, src, X, ALU.max).then_inc(s_m, 1)

                    def add_max(g):
                        n_ = b * NG + g
                        dve.wait_ge(s_mt, n_ + 1)
                        tt(qaug2[:, g % 2], psum[7][:], qaug[:, g % 2].bitcast(F32), ALU.add).then_inc(s_q2, 1)

                    queries(0)
                    row_max(0)
                    for g in range(NG):
                        add_max(g)
                        if g + 1 < NG:
                            queries(g + 1)
                            row_max(g + 1)
                    for qt in range(TB):
                        dve.wait_ge(s_ot, 4 * b + qt + 1)
                        o4 = psum[qt % 2][:].rearrange("p (h w) -> p h w", h=H)
                        seq(V.reciprocal(rden[:, qt], o4[:, :, D]))
                        tt(att[:, qt].rearrange("p (h d) -> p h d", h=H), o4[:, :, 0:D],
                           rden[:, qt].unsqueeze(2).broadcast_to((P, H, D)), ALU.mult).then_inc(s_at, 1)
                    dve.wait_ge(s_pr, b + 1)
                    tt(x[:, TB * b:TB * b + TB].rearrange("p a c -> p (a c)"), psum[6][:],
                       x[:, TB * b:TB * b + TB].rearrange("p a c -> p (a c)"), ALU.add).then_inc(s_xa, 1)
                dve.wait_ge(s_xa, B)

            def grouped_attention(t, q):
                for k in range(NT // 2):
                    dve.wait_ge(s_g["qps"], q * 8 + k + 1)
                    V.tensor_copy(gqkv[:, 2 * k:2 * k + 2].rearrange("p a c -> p (a c)"), psum[4 + k % 2][:]).then_inc(s_g["qkv"], 1)
                mark(V.memset(gsc, MASKED))
                dve.wait_ge(s_g["qkv"], q * 8 + 8)
                settle()
                at = lambda s: gqkv[:, 4 * s:4 * s + 4].rearrange("p a (n w) -> p (a n) w", w=4 * D)
                q_of = lambda s: at(s)[:, :, 0:2 * D].rearrange("p m (i d) -> p m i d", i=2)
                k_of = lambda s: at(s)[:, :, 2 * D:3 * D].unsqueeze(2).broadcast_to((P, 32, 2, D))
                v_of = lambda s: at(s)[:, :, 3 * D:4 * D].unsqueeze(2).broadcast_to((P, 32, 2, D))
                pairs = [(s, u) for s in range(SEQ) for u in range(s + 1)]
                v4 = lambda v: v.rearrange("p (m i d) -> p m i d", i=2, d=D)
                for i, (s, u) in enumerate(pairs):
                    mark(tt(v4(gprod[:, i]), q_of(s), k_of(u), ALU.mult))
                settle()
                for i, (s, u) in enumerate(pairs):
                    mark(V.tensor_reduce(gsc[:, s, u], gprod[:, i].rearrange("p (e d) -> p e d", d=D), X, ALU.add))
                settle()
                key_last = lambda v: v.rearrange("p s t e -> p s e t")
                seq(V.tensor_reduce(gsm[:, 0], key_last(gsc), X, ALU.max))
                over = lambda v: v.unsqueeze(2).broadcast_to((P, SEQ, SEQ, 64))
                tt(gsc, gsc, over(gsm[:, 0]), ALU.subtract).then_inc(s_g["sc"], 1)
                dve.wait_ge(s_g["ex"], q + 1)
                seq(V.tensor_reduce(gsm[:, 1], key_last(gp), X, ALU.add))
                seq(V.reciprocal(gsm[:, 2], gsm[:, 1]))
                seq(tt(gp, gp, over(gsm[:, 2]), ALU.mult))
                for i, (s, u) in enumerate(pairs):
                    pr = gp[:, s, u].rearrange("p (m i) -> p m i", i=2).unsqueeze(3).broadcast_to((P, 32, 2, D))
                    mark(tt(v4(gprod[:, i]), pr, v_of(u), ALU.mult))
                settle()
                gos = go.rearrange("p (s a) c -> p s (a c)", s=SEQ)
                first = {s: s * (s + 1) // 2 for s in range(SEQ)}
                for u in range(SEQ):
                    for s in range(max(u, 0), SEQ):
                        if u == 0:
                            mark(V.tensor_copy(gos[:, s], gprod[:, first[s]]))
                        else:
                            mark(tt(gos[:, s], gos[:, s], gprod[:, first[s] + u], ALU.add))
                    settle()
                for g in range(4):
                    dve.drain().then_inc(s_src, 1)
                for k in range(4):
                    dve.wait_ge(s_g["pr"], 4 * q + k + 1)
                    flat = lambda v: v[:, 4 * k:4 * k + 4].rearrange("p a c -> p (a c)")
                    mark(tt(flat(go), psum[4 + k][:], flat(xn), ALU.add))
                settle()

            def window_attention(t):
                for k in range(NW * WS):
                    i, o = divmod(k, WS)
                    dve.wait_ge(s_wn["qps"], k + 1)
                    tt(wqkv[:, i, o], psum[4 + k % 2][:, 0:3 * C], b1qkv[:], ALU.add).then_inc(s_wn["qkv"], 1)
                for r in range(2 * WS - 1):
                    mark(V.tensor_copy(wbr[:, r], btab[:, 2 * WS - 2 - r]))
                dve.wait_ge(s_wn["qkv"], NW * WS)
                settle()
                K16 = NW * WS
                keys = wqkv.rearrange("p n o c -> p (n o) c")
                for q in range(WS):
                    u = q % 2
                    qv = wqkv[:, :, q, 0:C].unsqueeze(2).broadcast_to((P, NW, WS, C))
                    seq(tt(wprod[:, u].rearrange("p (n k c) -> p n k c", n=NW, k=WS), qv,
                           wqkv[:, :, :, C:2 * C], ALU.mult))
                    seq(V.tensor_reduce(wsc[:, q], wprod[:, u].rearrange("p (e d) -> p e d", d=D), X, ALU.add))
                for q in range(WS):
                    bias = wbr[:, WS - 1 - q:2 * WS - 1 - q].rearrange("p k h -> p (k h)").unsqueeze(1).broadcast_to((P, NW, WS * H))
                    v = wsc[:, q].rearrange("p (n e) -> p n e", n=NW)
                    mark(V.scalar_tensor_tensor(out=v, in0=v, scalar=SCALE, in1=bias, op0=ALU.mult, op1=ALU.add))
                settle()
                flat = lambda v: v.rearrange("p q (n k h) -> p (q n) k h", n=NW, k=WS)
                last = lambda v: flat(v).rearrange("p a k h -> p a h k")
                over = lambda v: v.unsqueeze(2).broadcast_to((P, NW * WS, WS, H))
                seq(V.tensor_reduce(wsm[:, 0], last(wsc), X, ALU.max))
                tt(flat(wsc), flat(wsc), over(wsm[:, 0]), ALU.subtract).then_inc(s_wn["sc"], 1)
                dve.wait_ge(s_wn["ex"], 1)
                seq(V.tensor_reduce(wsm[:, 1], last(wpp), X, ALU.add))
                seq(V.reciprocal(wsm[:, 2], wsm[:, 1]))
                seq(tt(flat(wpp), flat(wpp), over(wsm[:, 2]), ALU.mult))
                for q in range(WS):
                    u = q % 2
                    pr = wpp[:, q].rearrange("p (m h) -> p m h", h=H).unsqueeze(3).broadcast_to((P, K16, H, D))
                    vv = keys[:, :, 2 * C:3 * C].rearrange("p m (h d) -> p m h d", h=H)
                    seq(tt(wprod[:, u].rearrange("p (m h d) -> p m h d", h=H, d=D), pr, vv, ALU.mult))
                    seq(V.tensor_reduce(wo[:, :, q], wprod[:, u].rearrange("p (n k c) -> p n c k", n=NW, k=WS), X, ALU.add))
                for g in range(4):
                    dve.drain().then_inc(s_src, 1)
                for k in range(4):
                    dve.wait_ge(s_wn["pr"], k + 1)
                    xs = x[:, 4 * k:4 * k + 4]
                    seq(tt(xs, xs, b1proj[:].unsqueeze(1).broadcast_to((P, 4, C)), ALU.add))
                    xf = xs.rearrange("p a c -> p (a c)")
                    seq(tt(xf, psum[4 + k][:], xf, ALU.add))

            for s in stages:
                t, i = first_t[s], first_n[s]
                if s in "AC":
                    norm(i, x, xn, t)
                    moe(0, moe_no[s], t)
                elif s == "B":
                    norm(i, x, xn, t)
                    rope_attention(t)
                elif s in "DF":
                    norm(i, x, xn)
                    norm(i + 1, xn, go, t)
                    grouped_attention(t, gqa_no[s])
                    norm(i + 2, go, xn, t + 2)
                    moe(1, moe_no[s], t + 2)
                else:
                    norm(i, x, xn, t)
                    window_attention(t)
            dve.drain().then_inc(s_done, 1)


_INS = ["L0_attn_x", "L0_attn_W_qkv", "L0_attn_W_proj", "L0_ffn_W1", "L0_ffn_b1", "L0_ffn_W2", "L0_ffn_b2",
        "L0_ffn_Wr", "L0_ffn_br", "L1_attn_w_qkv", "L1_attn_b_qkv", "L1_attn_w_proj", "L1_attn_b_proj",
        "L1_attn_bias_table", "L1_ffn_ln1_weight", "L1_ffn_ln1_bias", "L1_ffn_ln2_weight", "L1_ffn_ln2_bias",
        "L1_ffn_qkv_weight", "L1_ffn_proj_weight", "L1_ffn_router_weight", "L1_ffn_moe_w1", "L1_ffn_moe_w2"]


def kernel(**inputs):
    import concourse.bacc as bacc
    from concourse.bass_utils import run_bass_kernel_spmd

    nc = bacc.Bacc("TRN2", target_bir_lowering=False, num_devices=1)
    arrays = {name: np.ascontiguousarray(inputs[name]) for name in _INS}
    arrays["const"] = const_array()
    a = {n: nc.dram_tensor(f"in_{n}_dram", v.shape, mybir.dt.from_np(v.dtype), kind="ExternalInput").ap()
         for n, v in arrays.items()}
    out = nc.dram_tensor("out_0_dram", (B, T, C), F32, kind="ExternalOutput").ap()
    build(nc, a, out)
    r = run_bass_kernel_spmd(nc, [{f"in_{n}_dram": v for n, v in arrays.items()}], core_ids=[0])
    return r.results[0]["out_0_dram"]
```

```python
from contextlib import ExitStack

import numpy as np

import concourse.bass as bass
from concourse import mybir

F32 = mybir.dt.float32
F32R = mybir.dt.float32r
BF16 = mybir.dt.bfloat16
ALU = mybir.AluOpType
ACT = mybir.ActivationFunctionType
X = mybir.AxisListType.X

P = 128
B, T, C = 4, 512, 128
NT = B * T // P
TB = T // P
H, D = 16, 8
E, FF = 8, 512
HB = FF // P
KV = 8
SEQ = 4
CAP = 640
WS, SHIFT = 8, 4
NW = B * T // WS // P
XTW = T + WS
EPS = 1e-5
SCALE = float(D) ** -0.5
MASKED = -1.0e9
PE_SUMS = (0, 1, 2, 4, 5, 6)
HEADS_G = 4
NG = H // HEADS_G
SC, EC = 12, 10
MAX_ROW = 24

CONST_COLS = dict(ident=128, before=128, ones=128, mask_qk=128, mask_kq=128, cos=T, sin=T,
                  one_row=1, rev=128, tile_of=16)
SELECT = ("q_hi", "q_lo", "k_hi", "k_lo")


def const_array():
    c = {n: np.zeros((P, w), np.float32) for n, w in CONST_COLS.items()}
    c |= {n: np.zeros((P, NG * P), np.float32) for n in SELECT}
    i = np.arange(P)
    c["ident"][i, i] = 1
    c["before"][:] = i[:, None] < i[None, :]
    c["ones"][:] = 1
    c["mask_qk"][:] = np.where(i[:, None] >= i[None, :], 0, -1e30)
    c["mask_kq"][:] = c["mask_qk"].T
    half = D // 2
    theta = (1.0 / np.float32(10000.0) ** (np.arange(half, dtype=np.float32) / half)).astype(np.float32)
    freqs = np.outer(np.arange(T, dtype=np.float32), theta).astype(np.float32)
    c["cos"][:] = np.cos(freqs).astype(np.float32).T[i % half]
    c["sin"][:] = np.sin(freqs).astype(np.float32).T[i % half]
    for h in range(H):
        g, j = divmod(h, HEADS_G)
        for d in range(D):
            for name, thirds in (("q_hi", (0, 1)), ("q_lo", (2,)), ("k_hi", (0, 2)), ("k_lo", (1,))):
                for s in thirds:
                    c[name][h * D + d, g * P + 32 * j + D * s + d] = 1
    c["one_row"][MAX_ROW::32] = 1
    c["rev"][:] = E - np.arange(P) % E
    c["tile_of"][i, i // E] = 1
    return np.concatenate([c[n] for n in (*CONST_COLS, *SELECT)], axis=1)


def build(nc, a, out, stages="ABCDEF"):
    ctx = ExitStack()
    with ctx:
        def sb(name, shape, dt=F32):
            return ctx.enter_context(nc.sbuf_tensor(name, shape, dt))

        def sem(name):
            return ctx.enter_context(nc.semaphore(name))

        x = sb("x", [P, NT, C])
        xn = sb("xn", [P, NT, C])
        xT = sb("xT", [P, B, XTW])
        const = sb("constants", [P, sum(CONST_COLS.values())])
        cc, at = {}, 0
        for n, w in CONST_COLS.items():
            cc[n] = const[:, at:at + w]
            at += w
        ident, ones = cc["ident"], cc["ones"]
        small = sb("small", [P, NT, 6])
        mv = sb("mv", [P, NT, 2])
        veps = sb("veps", [P, NT])
        rstd = sb("rstd", [P, NT])
        mhalf = sb("mhalf", [P, NT])
        wr0 = sb("wr0", [P, E])
        br0 = sb("br0", [P, E])
        wr1 = sb("wr1", [P, E])
        b1T = sb("b1T", [P, E * HB])
        b1r = sb("b1r", [E * HB, P])
        b2m = sb("b2m", [P, NT, C])
        gT = sb("gT", [P, P])
        w1 = sb("w1", [P, 2, FF])
        w2 = sb("w2", [P, 2, HB, C])
        w1h = sb("w1h", [P, 2, FF], F32R)
        w1l = sb("w1l", [P, 2, FF], F32R)
        w2h = sb("w2h", [P, 2, HB, C], F32R)
        w2l = sb("w2l", [P, 2, HB, C], F32R)
        xTh = sb("xTh", [P, B, T], F32R)
        xTl = sb("xTl", [P, B, T], F32R)
        bigr = sb("bigr", [P, 8192], F32R)
        rt = sb("rt", [P, 12, NT, E])
        rs = sb("rs", [P, 8, NT])
        gate = sb("gate", [P, NT, E])
        lnw = sb("lnw", [P, 4])
        lnr = sb("lnr", [4, P])
        big = sb("big", [P, 18048])
        w0qkv = sb("w0qkv", [P, 3 * C])
        w0rot = sb("w0rot", [P, 2 * C])
        w0proj = sb("w0proj", [P, C])
        w1qkv = sb("w1qkv", [P, 3 * C])
        b1qkv = sb("b1qkv", [P, 3 * C])
        w1proj = sb("w1proj", [P, C])
        b1proj = sb("b1proj", [P, C])
        btab = sb("btab", [P, 2 * WS - 1, H])
        gq_raw = sb("gq_raw", [P, 2, C])
        gqT = sb("gqT", [P, 2 * C])
        gp_raw = sb("gp_raw", [P, C])
        gpT = sb("gpT", [P, C])
        negid = sb("negid", [P, P], F32R)
        mask = sb("mask", [P, 3, P], BF16)
        hh = bigr[:, 0:4096].rearrange("p (u h t) -> p u h t", u=2, h=HB)
        hl = bigr[:, 4096:8192].rearrange("p (u h t) -> p u h t", u=2, h=HB)
        sel = bigr[:, 0:2048].rearrange("p (i c) -> p i c", i=4)
        kaug = bigr[:, 2048:3584].rearrange("p (u t) -> p u t", u=3)
        qaug = bigr[:, 3584:4608].rearrange("p (u t) -> p u t", u=2)
        qaug2 = bigr[:, 4608:5632].rearrange("p (u t) -> p u t", u=2)
        qk_hl = [xTh, xTl]
        mrow = [v.rearrange("p (a w) -> p a w", a=TB) for v in (bigr[:, 5632:6144], bigr[:, 6144:6656])]

        psum_all = ctx.enter_context(nc.psum_tensor("psum_all", [P, 8, 512], F32))
        psum = [psum_all[:, i, :] for i in range(8)]

        s_x_in = [sem("s_x_in0"), sem("s_x_in1")]
        s_in = sem("s_in")
        s_tick = sem("s_tick")
        s_vz = sem("s_vz")
        s_row = sem("s_row")
        s_rope = sem("s_rope")
        s_done = sem("s_done")
        s_out = sem("s_out")
        s_const = sem("s_const")
        s_pool = sem("s_pool")
        s_dve = sem("s_dve")
        s_act = sem("s_act")
        s_setup_ps = sem("s_setup_ps")
        s_setup = sem("s_setup")
        s_var = sem("s_var")
        s_rstd = sem("s_rstd")
        s_src = sem("s_src")
        s_tps = sem("s_tps")
        s_xT = sem("s_xT")
        s_logit = sem("s_logit")
        s_soft = sem("s_soft")
        s_exp = sem("s_exp")
        s_gate = sem("s_gate")
        s_rank = sem("s_rank")
        s_gTp = sem("s_gTp")
        s_gT = sem("s_gT")
        s_gd = sem("s_gd")
        s_gb = [sem("s_gb0"), sem("s_gb1")]
        s_w = [sem("s_w0"), sem("s_w1")]
        s_ws = sem("s_ws")
        s_xTl = sem("s_xTl")
        s_hps = sem("s_hps")
        s_h = sem("s_h")
        s_hl = sem("s_hl")
        s_y = sem("s_y")
        s_c = sem("s_c")
        s_acc = sem("s_acc")
        s_tail = sem("s_tail")
        s_x = sem("s_x")
        s_b2 = sem("s_b2")
        s_split, s_wl, s_hcopy, s_hpart, s_ytmp = map(sem, ("s_split", "s_wl", "s_hcopy", "s_hpart", "s_ytmp"))
        s_selin = sem("s_selin")
        s_sel = sem("s_sel")
        s_qk = sem("s_qk")
        s_qkr = sem("s_qkr")
        s_qsum = sem("s_qsum")
        s_qhi = sem("s_qhi")
        s_qkd = sem("s_qkd")
        s_v = sem("s_v")
        s_vd = sem("s_vd")
        s_kps, s_kd = sem("s_kps"), sem("s_kd")
        s_qps, s_qd = sem("s_qps"), sem("s_qd")
        s_s, s_m = sem("s_s"), sem("s_m")
        s_mt, s_q2 = sem("s_mt"), sem("s_q2")
        s_st, s_p = sem("s_st"), sem("s_p")
        s_pv, s_o = sem("s_pv"), sem("s_o")
        s_ot, s_at = sem("s_ot"), sem("s_at")
        s_att, s_attT = sem("s_att"), sem("s_attT")
        s_pr, s_xa = sem("s_pr"), sem("s_xa")
        s_g = {n: sem("s_g_" + n) for n in ("qps", "qkv", "qk", "sum", "sc", "ex", "pv", "pr")}
        s_wn = {n: sem("s_wn_" + n) for n in ("qps", "qkv", "qk", "sum", "sc", "ex", "pv", "used", "pr")}

        big_at = [0]

        def carve(cols, dt=F32):
            v = big[:, big_at[0]:big_at[0] + cols]
            big_at[0] += cols
            return v

        rope = carve(4 * T).rearrange("p (a t) -> p a t", a=4)
        vaug = carve(TB * H * 32).rearrange("p (k h w) -> p k h w", k=TB, h=H)
        pT = carve(2 * EC * T).rearrange("p (u c w) -> p u c w", u=2, c=EC)
        oT = [v.rearrange("p (g t) -> p g t", g=NG) for v in (carve(NG * T), xn[:].rearrange("p a c -> p (a c)"))]
        rden = carve(TB * H).rearrange("p (a h) -> p a h", a=TB)
        att = carve(TB * C).rearrange("p (a c) -> p a c", a=TB)
        attT = carve(T)
        big_at[0] = 0
        gqkv = carve(NT * 256).rearrange("p (t c) -> p t c", t=NT)
        gprod = carve(10 * 512).rearrange("p (i e) -> p i e", i=10)
        gsc = carve(SEQ * SEQ * 64).rearrange("p (s t e) -> p s t e", s=SEQ, t=SEQ)
        gp = carve(SEQ * SEQ * 64).rearrange("p (s t e) -> p s t e", s=SEQ, t=SEQ)
        gsm = carve(4 * 256).rearrange("p (i s e) -> p i s e", i=4, s=SEQ)
        go = carve(NT * C).rearrange("p (t c) -> p t c", t=NT)
        big_at[0] = 0
        wqkv = carve(NW * WS * 3 * C).rearrange("p (n o c) -> p n o c", n=NW, o=WS)
        wprod = [carve(NW * WS * C), carve(NW * WS * C), xn[:].rearrange("p a c -> p (a c)")]
        wsc = carve(WS * NW * WS * H).rearrange("p (q e) -> p q e", q=WS)
        wpp = carve(WS * NW * WS * H).rearrange("p (q e) -> p q e", q=WS)
        wsm = carve(3 * WS * NW * H).rearrange("p (i a h) -> p i a h", i=3, h=H)
        xW = carve(NW * WS * P).rearrange("p (n o w) -> p n o w", n=NW, o=WS)
        wbr = carve((2 * WS - 1) * H).rearrange("p (r h) -> p r h", h=H)
        big_at[0] = 0
        hid = carve(2 * HB * T).rearrange("p (u h t) -> p u h t", u=2, h=HB)
        accT = carve(B * T).rearrange("p (b t) -> p b t", b=B)
        gbc = carve(2 * B * T).rearrange("p (u b t) -> p u b t", u=2, b=B)
        ytmp = carve(2 * T).rearrange("p (u t) -> p u t", u=2)
        b2rep = ytmp[:, 0, 0:C]
        sel_raw = big[:, 4608:6656].rearrange("p (i c) -> p i c", i=4)
        gates_d = nc.dram_tensor("gates", (E, B * T), F32, kind="Internal").ap()

        block = ctx.enter_context(nc.Block())
        plan = [("AC" if s in "AC" else s) for s in stages]
        t_count = {"A": 1, "B": 1, "C": 1, "D": 3, "E": 2, "F": 3}
        n_count = {"A": 1, "B": 1, "C": 1, "D": 3, "E": 1, "F": 3}
        src_count = {"A": 1, "B": 1, "C": 1, "D": 2, "E": 1, "F": 2}
        first_src = {s: sum(src_count[v] for v in stages[0:k]) for k, s in enumerate(stages)}
        first_t, first_n, moe_no, gqa_no = {}, {}, {}, {}
        t0 = n0 = m0 = g0 = 0
        for s in stages:
            first_t[s], first_n[s], moe_no[s], gqa_no[s] = t0, n0, m0, g0
            t0, n0 = t0 + t_count[s], n0 + n_count[s]
            m0 += s in "ACDF"
            g0 += s in "DF"
        NCHUNK = E * B
        moe_after = [first_n[s] + n_count[s] - 1 for s in stages if s in "ACDF"]
        sp_e = E // 2

        def groups(t):
            return slice(4 * t, 4 * t + 4)

        kinds = [int(s in "DF") for s in stages if s in "ACDF"]
        rank_no = [sum(kinds[:r]) for r in range(len(kinds))]

        def loads():
            bc = lambda v, n: v.rearrange("(o n) -> o n", o=1).broadcast_to((P, n))
            yield const[:], a["const"][:, 0:sum(CONST_COLS.values())]
            yield wr0[:], a["L0_ffn_Wr"]
            yield br0[:], bc(a["L0_ffn_br"], E)
            yield wr1[:], a["L1_ffn_router_weight"]
            yield b1r[:], a["L0_ffn_b1"].rearrange("e (h p) -> (e h) p", p=P)
            yield b2rep, a["L0_ffn_b2"].rearrange("(o e) c -> o e c", o=1).broadcast_to((NT, E, C))
            yield w0qkv[:], a["L0_attn_W_qkv"]
            yield w0proj[:], a["L0_attn_W_proj"]
            yield w1qkv[:], a["L1_attn_w_qkv"]
            yield b1qkv[:], bc(a["L1_attn_b_qkv"], 3 * C)
            yield w1proj[:], a["L1_attn_w_proj"]
            yield b1proj[:], bc(a["L1_attn_b_proj"], C)
            first = (WS - 1) * (2 * WS - 1)
            rows = a["L1_attn_bias_table"][first:first + 2 * WS - 1, :]
            yield btab[:], rows.rearrange("(o r) h -> o r h", o=1).broadcast_to((P, 2 * WS - 1, H))
            yield gq_raw[:], a["L1_ffn_qkv_weight"].rearrange("(i p) c -> p i c", p=P)
            yield gp_raw[:], a["L1_ffn_proj_weight"]
            for i, n in enumerate(("ln1_weight", "ln1_bias", "ln2_weight", "ln2_bias")):
                yield lnr[i:i + 1, :], a["L1_ffn_" + n].rearrange("(o n) -> o n", o=1)

        N_IN = 16 * 19

        def rope_order():
            groups_ = B * NG
            for n in range(-2, groups_ + 3):
                b, g = divmod(n, NG)
                between = {c: [] for c in range(SC + 1)}
                if 0 <= n - 1 < groups_:
                    between[2].append(("outputs", (n - 1, 0)))
                    between[7].append(("outputs", (n - 1, 1)))
                if n >= 0 and b + 1 < B and g < 2:
                    between[2].append(("project", (b + 1, 2 * g)))
                    between[3].append(("project", (b + 1, 2 * g + 1)))
                    between[9].append(("project_high", (b + 1, 2 * g + 1)))
                if g == 0 and 1 <= b < B:
                    between[10].append(("values", (b,)))
                if n + 2 < groups_:
                    between[11].append(("keys", (n + 2,)))
                    between[9].append(("queries", (n + 2,)))
                if b >= 1 and g < 3:
                    between[9].append(("end", (b - 1, 2 * g)))
                    between[12].append(("end", (b - 1, 2 * g + 1)))
                if g == 3 and 1 <= b < B:
                    between[6].append(("stats", (b - 1,)))
                if 0 <= n < groups_:
                    between[0].insert(0, ("maxima", (n,)))
                for c in range(SC):
                    yield from between[c]
                    yield "fill", (n, c)
                yield from between[SC]
            yield "stats", (B - 1,)

        pairs = [(s_, u) for s_ in range(SEQ) for u in range(s_ + 1)]
        PE_PAIRS = 5

        @block.sync
        def _(sp):
            for half in range(2):
                bs = slice(B // 2 * half, B // 2 * (half + 1))
                sp.dma_start(x[:, NT // 2 * half:NT // 2 * (half + 1)],
                             a["L0_attn_x"][bs].rearrange("b (t p) c -> p (b t) c", p=P)).then_inc(s_x_in[half], 16)
            for tile, src in loads():
                sp.dma_start(tile, src).then_inc(s_in, 16)
            for s in stages:
                if s == "B":
                    sp.wait_ge(s_rope, 1)
                    sp.dma_start(sel_raw, a["const"][:, sum(CONST_COLS.values()):].rearrange("p (i c) -> p i c", i=4)).then_inc(s_selin, 16)
                if s not in "ACDF":
                    continue
                r = moe_no[s]
                w1_d, w2_d = (a["L0_ffn_W1"], a["L0_ffn_W2"]) if s in "AC" else (a["L1_ffn_moe_w1"], a["L1_ffn_moe_w2"])

                def weights(e, u, i):
                    sp.wait_ge(s_ws, 2 * i + u + r * E + 1)
                    sp.dma_start(w1[:, u], w1_d[e].rearrange("e p f -> (e p) f")).then_inc(s_w[u], 16)
                    sp.dma_start(w2[:, u], w2_d[e].rearrange("e (h p) c -> p (e h) c", p=P)).then_inc(s_w[u], 16)

                def gates(e, u, i):
                    sp.wait_ge(s_c, 8 * i + 4 * u + r * NCHUNK + 4)
                    sp.dma_start(gbc[:, u], gates_d[e].rearrange("e (b t) -> e b t", b=B).broadcast_to((P, B, T))).then_inc(s_gb[u], 16)

                for u in range(2):
                    weights(slice(u, u + 1), u, 0)
                sp.wait_ge(s_gd, 16 * (r + 1))
                with sp.Fori(0, E // 2 - 1) as i:
                    for u in range(2):
                        gates(bass.ds(2 * i + u, 1), u, i)
                        weights(bass.ds(2 * i + (2 + u), 1), u, i + 1)
                for u in range(2):
                    gates(slice(E - 2 + u, E - 1 + u), u, E // 2 - 1)
            for c in range(B):
                if stages[-1] in "ACDF":
                    sp.wait_ge(s_x, 4 * (len(kinds) - 1) + c + 1)
                else:
                    sp.wait_ge(s_done, 1)
                sp.dma_start(out[c].rearrange("(t p) c -> p t c", p=P), x[:, TB * c:TB * c + TB]).then_inc(s_out, 16)
            sp.wait_ge(s_out, 16 * B)


        @block.gpsimd
        def _(pool):
            nc.gpsimd.memset(mhalf[:], -0.5).then_inc(s_pool, 1)
            pool.wait_ge(s_pool, 1)

            def rope_sums():
                for b in range(B):
                    for i in (0, 2):
                        pool.wait_ge(s_qkr, 4 * b + i + 2)
                        nc.gpsimd.tensor_tensor(rope[:, i], rope[:, i], rope[:, i + 1], ALU.add).then_inc(s_qsum, 1)
                        pool.wait_ge(s_qhi, 2 * b + i // 2 + 1)
                        nc.gpsimd.tensor_tensor(qk_hl[b % 2][:, i + 1], rope[:, i], qk_hl[b % 2][:, i].bitcast(F32),
                                                ALU.subtract).then_inc(s_qkd, 1)

            for n in range(n0):
                if "B" in stages and n == first_n["B"] + 1:
                    rope_sums()
                for half in range(2):
                    ks = slice(NT // 2 * half, NT // 2 * (half + 1))
                    pool.wait_ge(s_var, 2 * n + half + 1)
                    nc.gpsimd.tensor_tensor(rstd[:, ks], veps[:, ks], mhalf[:, ks], ALU.pow).then_inc(s_rstd, 1)
                if n in moe_after:
                    r = moe_after.index(n)
                    pool.wait_ge(s_gT, r + 1)
                    pool.dma_start(gates_d.rearrange("e (t p) -> t e p", p=P), gT[:]).then_inc(s_gd, 16)
                    nc.gpsimd.memset(accT, 0.0).then_inc(s_acc, 1)
            if "B" in stages and n0 == first_n["B"] + 1:
                rope_sums()

        @block.tensor
        def _(pe):
            mm = nc.tensor.matmul
            pe.sem_inc(s_y, 5)
            pe.wait_ge(s_in, N_IN)
            nc.tensor.transpose(psum[4][:, 0:E * HB], b1r[:], ident[0:E * HB, 0:E * HB])
            nc.tensor.transpose(psum[4][:, 32:36], lnr[:], ident[0:4, 0:4])
            nc.tensor.transpose(psum[4][:, 128:256], gp_raw[:], ident)
            for i in range(2):
                last = nc.tensor.transpose(psum[4][:, 256 + 128 * i:384 + 128 * i], gq_raw[:, i], ident)
            last.then_inc(s_setup_ps, 1)

            def turn(v, src, behind=None):
                for g in range(4):
                    pe.wait_ge(s_src, 4 * v + g + 1)
                    for k in range(4):
                        ins = nc.tensor.transpose(psum[g][:, P * k:P * k + P], src(4 * g + k), ident)
                    ins.then_inc(s_tps, 1)
                    if behind and g:
                        behind(g - 1)
                if behind:
                    behind(3)

            def logits(kind, t, g):
                pe.wait_ge(s_xT, 4 * t + g + 1)
                for k in range(4 * g, 4 * g + 4):
                    ins = mm(psum[7][:, E * k:E * k + E], xT[:, g, P * (k % 4):P * (k % 4) + P],
                             (wr0 if kind == 0 else wr1)[:], start=True, stop=True)
                if g == 3:
                    ins.then_inc(s_logit, 1)

            def moe(kind, r, t):
                def first(i, m):
                    u, c = m // 4 % 2, m % 4
                    if c == 0:
                        pe.wait_ge(s_ws, 2 * i + r * E + m // 4 + 3)
                    for h in range(HB):
                        pe.wait_ge(s_h, 32 * i + r * NCHUNK * HB + 4 * m + h + 1)
                        hs = slice(P * h, P * h + P)
                        mm(psum[h][:], w1h[:, u, hs], xTh[:, c], start=True, stop=False)
                        mm(psum[h][:], w1h[:, u, hs], xTl[:, c], start=False, stop=False)
                        mm(psum[h][:], w1l[:, u, hs], xTh[:, c], start=False, stop=True).then_inc(s_hps, 1)

                def second(i, m):
                    u, c = m // 4, m % 4
                    pe.wait_ge(s_hl, 8 * i + r * NCHUNK + m + 1)
                    pe.wait_ge(s_c, 8 * i + r * NCHUNK + m + 7)
                    for h in range(HB):
                        y, v = psum[4 + m % 2][:], m % 2
                        mm(y, w2h[:, u, h], hh[:, v, h], start=(h == 0), stop=False)
                        mm(y, w2h[:, u, h], hl[:, v, h], start=False, stop=False)
                        ins = mm(y, w2l[:, u, h], hh[:, v, h], start=False, stop=(h == HB - 1))
                    ins.then_inc(s_y, 1)

                pe.wait_ge(s_xTl, 4 * r + 4)
                first(0, 0)
                if kind == 1:
                    pe.wait_ge(s_gate, 2 * r + 1)
                    chosen = rt[:, 10].rearrange("p t e -> p (t e)")
                    mm(psum[7][:, 0:P], cc["before"], chosen, start=True, stop=True)
                    mm(psum[7][:, P:2 * P], ones, chosen, start=True, stop=True).then_inc(s_rank, 1)
                pe.wait_ge(s_gate, 2 * r + 2)
                nc.tensor.transpose(psum[7][:, 0:P], gate[:].rearrange("p t e -> p (t e)"), ident).then_inc(s_gTp, 1)
                last = E // 2 - 1
                with pe.Fori(0, last) as i:
                    for m in range(8):
                        first(i, m + 1)
                        second(i, m)
                for m in range(8):
                    if m < 7:
                        first(last, m + 1)
                    second(last, m)
                if kind == 0:
                    pe.wait_ge(s_b2, 1)
                for c in range(B):
                    pe.wait_ge(s_c, (r + 1) * NCHUNK + 8 - (B - 1 - c))
                    if c < 2:
                        pe.wait_ge(s_c, (r + 1) * NCHUNK + 8 - (1 - c))
                    else:
                        pe.wait_ge(s_x, 4 * r + c - 1)
                    for k in range(4):
                        ins = mm(psum[4 + c % 2][:, P * k:P * k + P], accT[:, c, P * k:P * k + P], ident,
                                 start=True, stop=(kind == 1))
                        if kind == 0:
                            ins = mm(psum[4 + c % 2][:, P * k:P * k + P], gT[:], b2m[:, 4 * c + k], start=False, stop=True)
                    ins.then_inc(s_tail, 1)

            def rope_attention(t):
                pe.wait_ge(s_xT, 4 * t + 4)
                free = {6: None, 7: None}

                def take(bank, sem_, value):
                    if free[bank]:
                        pe.wait_ge(*free[bank])
                    free[bank] = (sem_, value)

                def project(b, i, bank=7):
                    if bank == 7:
                        take(7, s_qkr, 4 * b + i + 1)
                    w = (w0qkv[:, 0:C], w0rot[:, 0:C], w0qkv[:, C:2 * C], w0rot[:, C:2 * C])[i]
                    mm(psum[bank][:], w, xT[:, b, 0:T], start=True, stop=True).then_inc(s_qk, 1)

                def project_values(b):
                    take(7, s_vd, b + 1)
                    for k in range(TB):
                        ins = mm(psum[7][:, P * k:P * k + P], xT[:, b, P * k:P * k + P], w0qkv[:, 2 * C:3 * C],
                                 start=True, stop=True)
                    ins.then_inc(s_v, 1)

                def spread(n, i, sem_ps, sem_read):
                    b, g = divmod(n, NG)
                    take(7, sem_read, n + 1)
                    pe.wait_ge(s_qkd, 2 * b + (1 if i == 0 else 2))
                    gs = slice(P * g, P * g + P)
                    mm(psum[7][:], sel[:, i, gs], qk_hl[b % 2][:, i], start=True, stop=False)
                    mm(psum[7][:], sel[:, i + 1, gs], qk_hl[b % 2][:, i + 1], start=False, stop=True).then_inc(sem_ps, 1)

                def fill(n, c):
                    masks = []

                    def add_masks():
                        for bank, col, which, done in masks:
                            ins = mm(psum[bank][:, col:col + P], mask[:, 0], mask[:, which], start=False, stop=True, skip_group_check=True)
                            if done is not None:
                                ins.then_inc(done, 1)
                        masks.clear()

                    if 0 <= n + 1 < B * NG:
                        if c == 0:
                            pe.wait_ge(s_kd, n + 2)
                            pe.wait_ge(s_qd, n + 2)
                        m, j, col = SC * (n + 1) + c, c % 4, 0
                        if m >= 3:
                            pe.wait_ge(s_m, m - 2)
                        rows = slice(32 * j, 32 * j + 32)
                        for qt in ((3 - c // 4,) if c < 8 else (1, 0)):
                            w = P * (qt + 1)
                            add_masks()
                            mm(psum[m % 3][:, col:col + w], qaug[rows, (n + 1) % 2, P * qt:P * qt + P],
                               kaug[rows, (n + 1) % 3, 0:w], start=True, stop=False, skip_group_check=True)
                            col += w
                            masks.append((m % 3, col - P, 1, s_s if qt != 1 else None))
                    e = c - (SC - EC)
                    if 0 <= n < B * NG and e >= 0:
                        if e == 0:
                            pe.wait_ge(s_q2, n + 1)
                        m = EC * n + e
                        if e < 8:
                            parts = [(m, 0, e // 2, 0)] if e % 2 == 0 else [(m, 0, e // 2, 1), (m, 384, e // 2, 3)]
                        else:
                            parts = [(m, 0, 0, 2), (m + 1, 0, 2, 2)] if e == 8 else [(m - 1, 256, 1, 2), (m, 256, 3, 2)]
                        if e < 9 and m >= 3:
                            pe.wait_ge(s_p, m - (2 if e < 8 else 1))
                        if e == 9:
                            pe.wait_ge(s_row, n + 1)
                        for i, (bk, col, j, kt) in enumerate(parts):
                            rows, w = slice(32 * j, 32 * j + 32), T - P * kt
                            if i == 1 and e < 8:
                                add_masks()
                            mm(psum[3 + bk % 3][:, col:col + w], kaug[rows, n % 3, P * kt:P * kt + P],
                               qaug2[rows, n % 2, P * kt:T], start=True, stop=False, skip_group_check=True)
                            last = i == len(parts) - 1
                            done = s_st if e == 9 or (e < 8 and last) else s_row if last else None
                            masks.append((3 + bk % 3, col, 2, done))
                    add_masks()

                def maxima(n):
                    pe.wait_ge(s_m, SC * (n + 1))
                    take(7, s_q2, n + 1)
                    for qt in range(TB):
                        ins = mm(psum[7][:, P * qt:P * qt + P], mrow[n % 2][:, qt], negid[:], start=True, stop=True)
                    ins.then_inc(s_mt, 1)

                def outputs(n, half):
                    b, g = divmod(n, NG)
                    if half == 0:
                        pe.wait_ge(s_vd, b + 1)
                        pe.wait_ge(s_p, EC * (n + 1))
                        take(6, s_o, n + 1)
                    for kt in ((0,), (1, 2, 3))[half]:
                        for j in range(4):
                            c, o = {0: (2 * j, 0), 1: (2 * j + 1, 0), 2: (8 + j // 2, 256 * (j % 2)), 3: (2 * j + 1, 384)}[kt]
                            ins = mm(psum[6][32 * j:32 * j + 32, P * kt:T], vaug[:, kt, 4 * g + j, :],
                                     pT[:, n % 2, c, o:o + T - P * kt], start=(kt == 0), stop=(kt == TB - 1))
                    if half == 1:
                        ins.then_inc(s_pv, 1)

                def end(b, i):
                    if i < TB:
                        pe.wait_ge(s_o, NG * (b + 1))
                        bank = 6
                        if b == B - 1:
                            bank = i
                            pe.wait_ge(s_m, SC * NG * B)
                        else:
                            take(6, s_at, TB * b + i + 1)
                        for g in range(NG):
                            ins = nc.tensor.transpose(psum[bank][:, P * g:P * g + P], oT[b % 2][:, g, P * i:P * i + P], ident)
                        ins.then_inc(s_ot, 1)
                    elif i == TB:
                        pe.wait_ge(s_at, TB * (b + 1))
                        take(6, s_attT, b + 1)
                        for qt in range(TB):
                            ins = nc.tensor.transpose(psum[6][:, P * qt:P * qt + P], att[:, qt], ident)
                        ins.then_inc(s_att, 1)
                    else:
                        take(6, s_xa, b + 1)
                        for qt in range(TB):
                            ins = mm(psum[6][:, P * qt:P * qt + P], attT[:, P * qt:P * qt + P], w0proj[:], start=True, stop=True)
                        ins.then_inc(s_pr, 1)

                for i in range(4):
                    project(0, i, bank=2 + i)
                project_values(0)
                units = dict(
                    project=project, values=project_values, fill=fill, maxima=maxima,
                    outputs=outputs, end=end, keys=lambda n: spread(n, 2, s_kps, s_kd),
                    queries=lambda n: spread(n, 0, s_qps, s_qd))
                for name, args in rope_order():
                    if name in units:
                        units[name](*args)

            def grouped_attention(t, q):
                pe.wait_ge(s_xT, 4 * t + 4)
                for k in range(NT // 2):
                    m = q * 8 + k
                    if k >= 2:
                        pe.wait_ge(s_g["qkv"], m - 1)
                    for i in range(2):
                        ins = mm(psum[4 + k % 2][:, 256 * i:256 * i + 256],
                                 xT[:, k // 2, P * (2 * k + i - 4 * (k // 2)):P * (2 * k + i - 4 * (k // 2)) + P], gqT[:],
                                 start=True, stop=True)
                    ins.then_inc(s_g["qps"], 1)
                pe.wait_ge(s_g["qk"], q + 1)
                product = gprod[:, 0:PE_PAIRS].rearrange("p i (e d) -> p d i e", d=D)
                for d in range(D):
                    ins = mm(psum[6][:, 0:64 * PE_PAIRS], ident, product[:, d], start=(d == 0), stop=(d == D - 1))
                ins.then_inc(s_g["sum"], 1)
                for i, (s_, u) in enumerate(pairs):
                    pe.wait_ge(s_g["pv"], len(pairs) * q + i + 1)
                    if u < s_:
                        continue
                    for k in range(4):
                        for v in range(s_ + 1):
                            ins = mm(psum[s_][:, P * k:P * k + P], gprod[:, i - s_ + v, P * k:P * k + P], ident,
                                     start=(v == 0), stop=(v == s_))
                    ins.then_inc(s_tps, 1)
                for k in range(4):
                    pe.wait_ge(s_xT, 4 * (t + 1) + k + 1)
                    for i in range(4):
                        ins = mm(psum[4 + k][:, P * i:P * i + P], xT[:, k, P * i:P * i + P], gpT[:], start=True, stop=True)
                    ins.then_inc(s_g["pr"], 1)

            def window_attention(t):
                pe.wait_ge(s_xT, 4 * t + 4)
                for k in range(NW * WS):
                    n, o = divmod(k, WS)
                    if k >= 2:
                        pe.wait_ge(s_wn["qkv"], k - 1)
                    mm(psum[4 + k % 2][:, 0:3 * C], xW[:, n, o], w1qkv[:], start=True, stop=True).then_inc(s_wn["qps"], 1)
                pe.wait_ge(s_wn["qkv"], NW * WS)
                for q in PE_SUMS:
                    pe.wait_ge(s_wn["qk"], q + 1)
                    product = wprod[q % 3].rearrange("p (e d) -> p d e", d=D)
                    for d in range(D):
                        ins = mm(psum[q][:, 0:NW * WS * H], ident, product[:, d], start=(d == 0), stop=(d == D - 1))
                    ins.then_inc(s_wn["sum"], 1)
                for q in range(WS):
                    pe.wait_ge(s_wn["pv"], q + 1)
                    product = wprod[q % 3].rearrange("p (n k c) -> p n k c", n=NW, k=WS)
                    left = WS // 2 if q % 2 else WS
                    for n in range(NW):
                        for k in range(left):
                            ins = mm(psum[2 * n + q // 4][:, P * (q % 4):P * (q % 4) + P], product[:, n, k], ident,
                                     start=(k == 0), stop=(k == left - 1))
                        if q % 4 == 3:
                            ins.then_inc(s_tps, 1)
                    if q % 4 != 3:
                        ins.then_inc(s_wn["used"], 1)
                for k in range(4):
                    pe.wait_ge(s_xT, 4 * (t + 1) + 4)
                    for i in range(4):
                        ins = mm(psum[4 + k][:, P * i:P * i + P], xT[:, k, P * i:P * i + P], w1proj[:], start=True, stop=True)
                    ins.then_inc(s_wn["pr"], 1)

            for s in stages:
                t = first_t[s]
                pe.wait_ge(s_setup, 1)
                v = first_src[s]
                turn(v, (lambda k: go[:, k, :]) if s in "DF" else (lambda k: xn[:, k, :]),
                     (lambda g: logits(0, t, g)) if s in "AC" else None)
                if s in "AC":
                    moe(0, moe_no[s], t)
                elif s == "B":
                    pe.wait_ge(s_sel, 1)
                    rope_attention(t)
                elif s in "DF":
                    grouped_attention(t, gqa_no[s])
                    turn(v + 1, lambda k: xn[:, k, :], lambda g: logits(1, t + 2, g))
                    moe(1, moe_no[s], t + 2)
                else:
                    window_attention(t)


        @block.scalar
        def _(act):
            A = nc.scalar.activation
            act.sem_inc(s_h, 4)
            act.wait_ge(s_in, N_IN)
            act.wait_ge(s_setup_ps, 1)
            A(b1T[:], psum[4][:, 0:E * HB], ACT.Identity).then_inc(s_act, 1)
            A(lnw[:], psum[4][:, 32:36], ACT.Identity).then_inc(s_act, 1)
            A(gpT[:], psum[4][:, 128:256], ACT.Identity).then_inc(s_act, 1)
            A(gqT[:], psum[4][:, 256:512], ACT.Identity).then_inc(s_act, 1)
            act.wait_ge(s_act, 4)
            act.drain().then_inc(s_setup, 1)
            chain = [4]

            def turned(t, mode, split=False):
                for i, g in enumerate((0, 2, 1, 3) if mode == "windows" else range(4)):
                    act.wait_ge(s_tps, 4 * t + i + 1)
                    src = psum[g][:]
                    if mode == "windows":
                        n, o0 = g // 2, 4 * (g % 2)
                        dst = xT[:, 2 * n:2 * n + 2, SHIFT + o0:SHIFT + o0 + T]
                        dst = dst.rearrange("p b (w o) -> p b w o", o=WS)[:, :, :, 0:4]
                        ins = None
                        for o in range(4):
                            ins = A(dst[:, :, :, o], src[:, P * o:P * o + P].rearrange("p (b w) -> p b w", b=2), ACT.Identity)
                            if o < 3 or g == 3:
                                ins.then_inc(s_act, 1)
                                chain[0] += 1
                        if g == 3:
                            act.wait_ge(s_act, chain[0])
                            act.wait_ge(s_xT, 4 * t + 3)
                            ins = A(xT[:, :, 0:SHIFT], xT[:, :, T:T + SHIFT], ACT.Identity)
                        ins.then_inc(s_xT, 1)
                        continue
                    if mode == "to windows":
                        nw = T // WS
                        dst = xW[:, g // 2, :, nw * (g % 2):nw * (g % 2) + nw]
                        A(dst[:, :, 0:nw - 1], src[:, SHIFT:T - SHIFT].rearrange("p (w o) -> p o w", o=WS), ACT.Identity)
                        A(dst[:, 0:SHIFT, nw - 1], src[:, T - SHIFT:T], ACT.Identity)
                        A(dst[:, SHIFT:WS, nw - 1], src[:, 0:SHIFT], ACT.Identity).then_inc(s_xT, 1)
                        continue
                    affine = dict(scale=lnw[:, mode:mode + 1], bias=lnw[:, mode + 1:mode + 2]) if mode in (0, 2) else {}
                    ins = A(xT[:, g, 0:T], src, ACT.Identity, **affine)
                    if split:
                        ins = A(xTh[:, g], src, ACT.Identity, **affine)
                    ins.then_inc(s_xT, 1)

            def experts(kind, r):
                act.wait_ge(s_soft, r + 1)
                A(rt[:, 1], rt[:, 0], ACT.Exp).then_inc(s_exp, 1)
                hidden(kind, r, 0, 0)
                act.wait_ge(s_gTp, r + 1)
                A(gT[:], psum[7][:, 0:P], ACT.Identity).then_inc(s_gT, 1)
                last = E // 2 - 1
                with act.Fori(0, last) as i:
                    for m in range(1, 9):
                        hidden(kind, r, i, m)
                for m in range(1, 8):
                    hidden(kind, r, last, m)

            def hidden(kind, r, i, m):
                u, c = m // 4, m % 4
                act.wait_ge(s_y, 8 * i + r * NCHUNK + m + 4)
                for h in range(HB):
                    act.wait_ge(s_hps, 32 * i + r * NCHUNK * HB + 4 * m + h + 1)
                    if kind == 0:
                        act.sem_inc(s_tick, 1)
                        bias = b1T[:, bass.ds(i * (2 * HB) + (u * HB + h), 1)]
                        act_of = lambda dst: A(dst, psum[h][:], ACT.Relu, bias=bias)
                    else:
                        act_of = lambda dst: A(dst, psum[h][:], ACT.Gelu)
                    ins = act_of(hid[:, m % 2, h])
                    if h < HB - 1:
                        ins = act_of(hh[:, m % 2, h])
                    ins.then_inc(s_h, 1)

            def rope_attention(t):
                def values(b):
                    act.wait_ge(s_v, b + 1)
                    A(vaug[:, :, :, 0:D], psum[7][:].rearrange("p (k h d) -> p k h d", k=TB, h=H), ACT.Identity).then_inc(s_vd, 1)

                def project(b, i):
                    if i % 2:
                        act.wait_ge(s_qsum, 2 * b + i // 2 + 1)
                        A(qk_hl[b % 2][:, i - 1], rope[:, i - 1], ACT.Identity).then_inc(s_qhi, 1)

                def keys(n):
                    act.wait_ge(s_kps, n + 1)
                    A(kaug[:, n % 3], psum[7][:], ACT.Identity, bias=cc["one_row"]).then_inc(s_kd, 1)

                def fill(n, c):
                    e = c - (SC - EC)
                    if 0 <= n < B * NG and e >= 0 and e != 8:
                        for m in range(EC * n + e - (e == 9), EC * n + e + 1):
                            act.wait_ge(s_st, m + 1)
                            A(pT[:, n % 2, m % EC], psum[3 + m % 3][:], ACT.Exp, scale=SCALE).then_inc(s_p, 1)

                def outputs(n, half):
                    if half == 1:
                        act.wait_ge(s_pv, n + 1)
                        A(oT[n // NG % 2][:, n % NG], psum[6][:], ACT.Identity).then_inc(s_o, 1)

                def end(b, i):
                    if i == TB:
                        act.wait_ge(s_att, b + 1)
                        A(attT, psum[6][:], ACT.Identity).then_inc(s_attT, 1)

                act.wait_ge(s_vz, 1)
                values(0)
                for i in range(4):
                    project(0, i)
                units = dict(project_high=project, values=values, keys=keys, fill=fill, outputs=outputs, end=end)
                for name, args in rope_order():
                    if name in units:
                        units[name](*args)

            for s in stages:
                t = first_t[s]
                if s in "AC":
                    turned(t, "plain", split=True)
                    experts(0, moe_no[s])
                elif s == "B":
                    turned(t, "plain")
                    rope_attention(t)
                elif s in "DF":
                    turned(t, 0)
                    q = gqa_no[s]
                    act.wait_ge(s_g["sc"], q + 1)
                    A(gp, gsc, ACT.Exp, scale=SCALE).then_inc(s_g["ex"], 1)
                    turned(t + 1, "plain")
                    turned(t + 2, 2, split=True)
                    experts(1, moe_no[s])
                else:
                    turned(t, "to windows")
                    for half in range(2):
                        act.wait_ge(s_wn["sc"], half + 1)
                        hs = slice(WS // 2 * half, WS // 2 * (half + 1))
                        A(wpp[:, hs], wsc[:, hs], ACT.Exp).then_inc(s_wn["ex"], 1)
                    turned(t + 1, "windows")

        @block.vector
        def _(dve):
            V = nc.vector
            n = [0]

            def mark(ins):
                ins.then_inc(s_dve, 1)
                n[0] += 1

            def settle():
                dve.wait_ge(s_dve, n[0])

            def seq(ins):
                mark(ins)
                settle()

            tt = V.tensor_tensor
            dve.sem_inc(s_ws, 2)
            dve.sem_inc(s_c, 8)

            def convert():
                dve.wait_ge(s_in, N_IN)
                tt(b2m[:], b2rep.unsqueeze(1).broadcast_to((P, NT, C)), cc["tile_of"].unsqueeze(2).broadcast_to((P, NT, C)),
                   ALU.mult).then_inc(s_b2, 1)
                V.tensor_scalar(negid[:], ident, -1.0, None, ALU.mult).then_inc(s_const, 1)
                for i, name in enumerate(("ident", "mask_qk", "mask_kq")):
                    V.tensor_copy(mask[:, i], cc[name]).then_inc(s_const, 1)
                src = w0qkv[:, 0:2 * C].rearrange("p (a z d) -> p a z d", z=2, d=D // 2)
                dst = w0rot[:].rearrange("p (a z d) -> p a z d", z=2, d=D // 2)
                V.tensor_scalar(dst[:, :, 0], src[:, :, 1], -1.0, None, ALU.mult).then_inc(s_const, 1)
                V.tensor_copy(dst[:, :, 1], src[:, :, 0]).then_inc(s_const, 1)
                V.memset(rt[:, 11], 0.0).then_inc(s_const, 1)
                dve.wait_ge(s_b2, 1)
                dve.wait_ge(s_const, 7)

            def stats(src, c):
                ks = range(4 * c, 4 * c + 4)
                for k in ks:
                    mark(V.bn_stats(small[:, k], src[:, k]))
                settle()
                for k in ks:
                    mark(V.bn_aggr(mv[:, k], small[:, k]))
                if c % 2:
                    settle()
                    half = slice(4 * c - 4, 4 * c + 4)
                    V.tensor_scalar(veps[:, half], mv[:, half, 1], EPS, None, ALU.add).then_inc(s_var, 1)

            def norm(i, src, dst, turn=None, have_stats=False):
                if not have_stats:
                    for c in range(4):
                        if i == 0 and c % 2 == 0:
                            dve.wait_ge(s_x_in[c // 2], 16)
                        stats(src, c)
                normalise(2 * i, src, dst, rstd, turn)
                if i == 0:
                    convert()

            def normalise(i, src, dst, factor, turn):
                for k in range(NT):
                    if k % (NT // 2) == 0:
                        dve.wait_ge(s_rstd, i + 1 + k // (NT // 2))
                    ins = V.tensor_scalar(dst[:, k], src[:, k], mv[:, k, 0:1], factor[:, k:k + 1], ALU.subtract, ALU.mult)
                    if turn is not None and k % 4 == 3:
                        ins.then_inc(s_src, 1)
                    else:
                        mark(ins)
                if turn is not None:
                    dve.wait_ge(s_src, 4 * turn + 4)
                settle()

            def moe(kind, r, t, last_stage):
                L, Pr, eq, oh1, p2, oh2 = (rt[:, i] for i in (0, 1, 2, 3, 4, 5))
                bc = lambda v: v.unsqueeze(2).broadcast_to((P, NT, E))
                split_weights(0, 0, r, 0)
                split_weights(0, 0, r, 1)
                for g in range(4):
                    dve.wait_ge(s_xT, 4 * t + g + 1)
                    tt(xTl[:, g], xT[:, g, 0:T], xTh[:, g].bitcast(F32), ALU.subtract).then_inc(s_xTl, 1)
                dve.wait_ge(s_logit, r + 1)
                ps = psum[7][:, 0:P].rearrange("p (t e) -> p t e", e=E)
                if kind == 0:
                    seq(tt(L, ps, br0[:].unsqueeze(1).broadcast_to((P, NT, E)), ALU.add))
                else:
                    seq(V.tensor_copy(L, ps))
                seq(V.tensor_reduce(rs[:, 0], L, X, ALU.max))
                tt(L, L, bc(rs[:, 0]), ALU.subtract).then_inc(s_soft, 1)
                dve.wait_ge(s_exp, r + 1)
                seq(V.tensor_reduce(rs[:, 1], Pr, X, ALU.add))
                seq(V.reciprocal(rs[:, 2], rs[:, 1]))
                seq(tt(Pr, Pr, bc(rs[:, 2]), ALU.mult))
                rev = cc["rev"].rearrange("p (t e) -> p t e", e=E)
                for src, top, onehot in ((Pr, 3, oh1), (p2, 4, oh2)):
                    seq(V.tensor_reduce(rs[:, top], src, X, ALU.max))
                    seq(tt(eq, src, bc(rs[:, top]), ALU.is_equal))
                    seq(tt(eq, eq, rev, ALU.mult))
                    seq(V.tensor_reduce(rs[:, 5], eq, X, ALU.max))
                    seq(tt(onehot, eq, bc(rs[:, 5]), ALU.is_equal))
                    if top == 3:
                        seq(V.scalar_tensor_tensor(out=p2, in0=oh1, scalar=-2.0, in1=Pr, op0=ALU.mult, op1=ALU.add))
                seq(tt(rs[:, 6], rs[:, 3], rs[:, 4], ALU.add))
                seq(V.reciprocal(rs[:, 7], rs[:, 6]))
                chosen = rt[:, 10]
                seq(tt(chosen, oh1, oh2, ALU.add))
                if kind == 1:
                    dve.drain().then_inc(s_gate, 1)
                seq(tt(gate[:], Pr, chosen, ALU.mult))
                seq(V.scalar_tensor_tensor(out=gate[:], in0=gate[:], scalar=0.5, in1=bc(rs[:, 7]), op0=ALU.mult, op1=ALU.mult))
                if kind == 1:
                    dve.wait_ge(s_rank, rank_no[r] + 1)
                    tot = psum[7][:, P:2 * P].rearrange("p (t e) -> p t e", e=E)
                    mark(V.tensor_copy(rt[:, 6, 1:NT], tot[:, 0:NT - 1]))
                    seq(V.tensor_copy(rt[:, 6, 0:1], rt[:, 11, 0:1]))
                    cur, other, step = 6, 7, 1
                    while step < NT:
                        mark(tt(rt[:, other, step:NT], rt[:, cur, step:NT], rt[:, cur, 0:NT - step], ALU.add))
                        seq(V.tensor_copy(rt[:, other, 0:step], rt[:, cur, 0:step]))
                        cur, other, step = other, cur, 2 * step
                    seq(tt(rt[:, 8], psum[7][:, 0:P].rearrange("p (t e) -> p t e", e=E), rt[:, cur], ALU.add))
                    seq(V.tensor_scalar(rt[:, 9], rt[:, 8], float(CAP), None, ALU.is_lt))
                    seq(tt(gate[:], gate[:], rt[:, 9], ALU.mult))
                dve.drain().then_inc(s_gate, 1 if kind == 1 else 2)
                experts(kind, r, last_stage)

            def split_weights(i, e, r, second):
                u, k = e % 2, e // 2
                if not second:
                    dve.wait_ge(s_w[u], 32 * i + 32 * (r * (E // 2) + k + 1))
                    dve.wait_ge(s_y, 8 * i + r * NCHUNK + 4 * e + 1)
                raw, high, low = ((w1[:, u], w1h[:, u], w1l[:, u]), (w2[:, u], w2h[:, u], w2l[:, u]))[second]
                V.tensor_copy(high, raw).then_inc(s_split, 1)
                dve.wait_ge(s_split, 4 * i + 2 * (e + r * E) + 1 + second)
                tt(low, raw, high.bitcast(F32), ALU.subtract).then_inc(s_ws if second else s_wl, 1)

            def split_hidden(i, m, r):
                v = m % 2
                n4 = r * NCHUNK * HB + 4 * m + 4
                dve.wait_ge(s_h, 32 * i + n4 + 4)
                V.tensor_copy(hh[:, v, HB - 1], hid[:, v, HB - 1]).then_inc(s_hcopy, 1)
                for h in range(HB - 1):
                    tt(hl[:, v, h], hid[:, v, h], hh[:, v, h].bitcast(F32), ALU.subtract).then_inc(s_hpart, 1)
                dve.wait_ge(s_hcopy, 8 * i + r * NCHUNK + m + 1)
                tt(hl[:, v, HB - 1], hid[:, v, HB - 1], hh[:, v, HB - 1].bitcast(F32), ALU.subtract).then_inc(s_hl, 1)

            def add_up(i, m, r):
                u, c = m // 4, m % 4
                if c == 0:
                    dve.wait_ge(s_gb[u], 16 * i + 16 * (r * (E // 2) + 1))
                dve.wait_ge(s_y, 8 * i + r * NCHUNK + m + 6)
                tt(ytmp[:, m % 2], psum[4 + m % 2][:], gbc[:, u, c], ALU.mult).then_inc(s_ytmp, 1)
                dve.wait_ge(s_ytmp, 8 * i + r * NCHUNK + m + 1)
                dve.wait_ge(s_c, 8 * i + r * NCHUNK + m + 5)
                tt(accT[:, c], accT[:, c], ytmp[:, m % 2], ALU.add).then_inc(s_c, 1)

            def experts(kind, r, last_stage):
                split_hidden(0, 0, r)
                dve.wait_ge(s_acc, r + 1)
                last = E // 2 - 1

                def step(i, m):
                    if m in (1, 2):
                        split_weights(i, 1, r, m - 1)
                    if m - 4 in (1, 2) and not (isinstance(i, int) and i == last):
                        split_weights(i, 2, r, m - 4 - 1)
                    if not (isinstance(i, int) and m == 7):
                        split_hidden(i, m + 1, r)
                    add_up(i, m, r)

                with dve.Fori(0, last) as i:
                    for m in range(8):
                        step(i, m)
                for m in range(8):
                    step(last, m)
                for c in range(B):
                    xs = x[:, 4 * c:4 * c + 4]
                    if kind == 1:
                        seq(V.scalar_tensor_tensor(out=xs, in0=go[:, 4 * c:4 * c + 4], scalar=0.5, in1=xs, op0=ALU.mult, op1=ALU.add))
                    dve.wait_ge(s_tail, 4 * r + c + 1)
                    xf = xs.rearrange("p a c -> p (a c)")
                    tt(xf, psum[4 + c % 2][:], xf, ALU.add).then_inc(s_x, 1)
                    dve.wait_ge(s_x, 4 * r + c + 1)
                    if not last_stage:
                        stats(x, c)

            def rope_attention(t, last_stage):
                dve.drain().then_inc(s_rope, 1)
                seq(V.memset(vaug, 0.0))
                for v in mrow:
                    mark(V.memset(v.bitcast(F32), 0.0))
                dve.wait_ge(s_selin, 16)
                V.tensor_copy(sel, sel_raw).then_inc(s_sel, 1)
                dve.wait_ge(s_sel, 1)
                settle()
                V.memset(vaug[:, :, :, D:D + 1], 1.0).then_inc(s_vz, 1)

                def project(b, i):
                    dve.wait_ge(s_qk, 4 * b + i + 1)
                    bank = 2 + i if b == 0 else 7
                    tt(rope[:, i], psum[bank][:], cc["sin"] if i % 2 else cc["cos"], ALU.mult).then_inc(s_qkr, 1)

                def queries(n_):
                    dve.wait_ge(s_qps, n_ + 1)
                    V.tensor_copy(qaug[:, n_ % 2], psum[7][:]).then_inc(s_qd, 1)

                def fill(n_, c):
                    if 0 <= n_ + 1 < B * NG:
                        m, at, col = SC * (n_ + 1) + c, 32 * (c % 4) + MAX_ROW, 0
                        dve.wait_ge(s_s, m + 1)
                        for qt in ((3 - c // 4,) if c < 8 else (1, 0)):
                            w = P * (qt + 1)
                            ins = V.tensor_reduce(mrow[(n_ + 1) % 2][:, qt, at:at + 1], psum[m % 3][:, col:col + w], X, ALU.max)
                            col += w
                        ins.then_inc(s_m, 1)

                def maxima(n_):
                    dve.wait_ge(s_mt, n_ + 1)
                    dve.wait_ge(s_qd, n_ + 1)
                    tt(qaug2[:, n_ % 2], psum[7][:], qaug[:, n_ % 2].bitcast(F32), ALU.add).then_inc(s_q2, 1)

                def end(b, i):
                    if i < TB:
                        dve.wait_ge(s_ot, TB * b + i + 1)
                        o4 = psum[i if b == B - 1 else 6][:].rearrange("p (h w) -> p h w", h=H)
                        seq(V.reciprocal(rden[:, i], o4[:, :, D]))
                        tt(att[:, i].rearrange("p (h d) -> p h d", h=H), o4[:, :, 0:D],
                           rden[:, i].unsqueeze(2).broadcast_to((P, H, D)), ALU.mult).then_inc(s_at, 1)
                    elif i > TB:
                        dve.wait_ge(s_pr, b + 1)
                        xs = x[:, TB * b:TB * b + TB].rearrange("p a c -> p (a c)")
                        tt(xs, psum[6][:], xs, ALU.add).then_inc(s_xa, 1)

                for i in range(4):
                    project(0, i)
                def next_stats(b):
                    dve.wait_ge(s_xa, b + 1)
                    if not last_stage:
                        stats(x, b)

                units = dict(stats=next_stats, project=project, queries=queries, fill=fill, maxima=maxima, end=end)
                for name, args in rope_order():
                    if name in units:
                        units[name](*args)

            def grouped_attention(t, q):
                mark(V.memset(gsc, MASKED))
                for k in range(NT // 2):
                    dve.wait_ge(s_g["qps"], q * 8 + k + 1)
                    V.tensor_copy(gqkv[:, 2 * k:2 * k + 2].rearrange("p a c -> p (a c)"), psum[4 + k % 2][:]).then_inc(s_g["qkv"], 1)
                dve.wait_ge(s_g["qkv"], q * 8 + 8)
                settle()
                at = lambda s: gqkv[:, 4 * s:4 * s + 4].rearrange("p a (n w) -> p (a n) w", w=4 * D)
                q_of = lambda s: at(s)[:, :, 0:2 * D].rearrange("p m (i d) -> p m i d", i=2)
                k_of = lambda s: at(s)[:, :, 2 * D:3 * D].unsqueeze(2).broadcast_to((P, 32, 2, D))
                v_of = lambda s: at(s)[:, :, 3 * D:4 * D].unsqueeze(2).broadcast_to((P, 32, 2, D))
                v4 = lambda v: v.rearrange("p (m i d) -> p m i d", i=2, d=D)
                for i, (s, u) in enumerate(pairs):
                    ins = tt(v4(gprod[:, i]), q_of(s), k_of(u), ALU.mult)
                    if i == PE_PAIRS - 1:
                        settle()
                        ins.then_inc(s_g["qk"], 1)
                    else:
                        mark(ins)
                settle()
                for i, (s, u) in enumerate(pairs):
                    if i >= PE_PAIRS:
                        mark(V.tensor_reduce(gsc[:, s, u], gprod[:, i].rearrange("p (e d) -> p e d", d=D), X, ALU.add))
                dve.wait_ge(s_g["sum"], q + 1)
                for i, (s, u) in enumerate(pairs[0:PE_PAIRS]):
                    mark(V.tensor_copy(gsc[:, s, u], psum[6][:, 64 * i:64 * i + 64]))
                settle()
                key_last = lambda v: v.rearrange("p s t e -> p s e t")
                seq(V.tensor_reduce(gsm[:, 0], key_last(gsc), X, ALU.max))
                over = lambda v: v.unsqueeze(2).broadcast_to((P, SEQ, SEQ, 64))
                tt(gsc, gsc, over(gsm[:, 0]), ALU.subtract).then_inc(s_g["sc"], 1)
                dve.wait_ge(s_g["ex"], q + 1)
                seq(V.tensor_reduce(gsm[:, 1], key_last(gp), X, ALU.add))
                seq(V.reciprocal(gsm[:, 2], gsm[:, 1]))
                seq(tt(gp, gp, over(gsm[:, 2]), ALU.mult))
                for i, (s, u) in enumerate(pairs):
                    pr = gp[:, s, u].rearrange("p (m i) -> p m i", i=2).unsqueeze(3).broadcast_to((P, 32, 2, D))
                    tt(v4(gprod[:, i]), pr, v_of(u), ALU.mult).then_inc(s_g["pv"], 1)
                for k in range(4):
                    dve.wait_ge(s_g["pr"], 4 * q + k + 1)
                    flat = lambda v: v[:, 4 * k:4 * k + 4].rearrange("p a c -> p (a c)")
                    seq(tt(flat(go), psum[4 + k][:], flat(xn), ALU.add))
                    stats(go, k)

            def window_attention(t, last_stage):
                for r in range(2 * WS - 1):
                    mark(V.tensor_copy(wbr[:, r], btab[:, 2 * WS - 2 - r]))
                for k in range(NW * WS):
                    i, o = divmod(k, WS)
                    dve.wait_ge(s_wn["qps"], k + 1)
                    tt(wqkv[:, i, o], psum[4 + k % 2][:, 0:3 * C], b1qkv[:], ALU.add).then_inc(s_wn["qkv"], 1)
                dve.wait_ge(s_wn["qkv"], NW * WS)
                settle()
                K16 = NW * WS
                keys = wqkv.rearrange("p n o c -> p (n o) c")
                for q in range(WS):
                    if q >= 3 and q - 3 in PE_SUMS:
                        dve.wait_ge(s_wn["sum"], PE_SUMS.index(q - 3) + 1)
                    qv = wqkv[:, :, q, 0:C].unsqueeze(2).broadcast_to((P, NW, WS, C))
                    tt(wprod[q % 3].rearrange("p (n k c) -> p n k c", n=NW, k=WS), qv,
                       wqkv[:, :, :, C:2 * C], ALU.mult).then_inc(s_wn["qk"], 1)
                    if q not in PE_SUMS:
                        dve.wait_ge(s_wn["qk"], q + 1)
                        seq(V.tensor_reduce(wsc[:, q], wprod[q % 3].rearrange("p (e d) -> p e d", d=D), X, ALU.add))
                for q in range(WS):
                    bias = wbr[:, WS - 1 - q:2 * WS - 1 - q].rearrange("p k h -> p (k h)").unsqueeze(1).broadcast_to((P, NW, WS * H))
                    src = wsc[:, q]
                    if q in PE_SUMS:
                        dve.wait_ge(s_wn["sum"], PE_SUMS.index(q) + 1)
                        src = psum[q][:, 0:NW * WS * H]
                    mark(V.scalar_tensor_tensor(out=wsc[:, q].rearrange("p (n e) -> p n e", n=NW),
                                                in0=src.rearrange("p (n e) -> p n e", n=NW), scalar=SCALE, in1=bias,
                                                op0=ALU.mult, op1=ALU.add))
                settle()
                halves = [slice(WS // 2 * v, WS // 2 * (v + 1)) for v in range(2)]
                flat = lambda v: v.rearrange("p q (n k h) -> p (q n) k h", n=NW, k=WS)
                last = lambda v: flat(v).rearrange("p a k h -> p a h k")
                small_of = lambda i, v: wsm[:, i, NW * WS // 2 * v:NW * WS // 2 * (v + 1)]
                over = lambda v: v.unsqueeze(2).broadcast_to((P, NW * WS // 2, WS, H))
                for v, hs in enumerate(halves):
                    seq(V.tensor_reduce(small_of(0, v), last(wsc[:, hs]), X, ALU.max))
                    tt(flat(wsc[:, hs]), flat(wsc[:, hs]), over(small_of(0, v)), ALU.subtract).then_inc(s_wn["sc"], 1)
                for v, hs in enumerate(halves):
                    dve.wait_ge(s_wn["ex"], v + 1)
                    seq(V.tensor_reduce(small_of(1, v), last(wpp[:, hs]), X, ALU.add))
                    seq(V.reciprocal(small_of(2, v), small_of(1, v)))
                    seq(tt(flat(wpp[:, hs]), flat(wpp[:, hs]), over(small_of(2, v)), ALU.mult))
                for q in range(WS):
                    if q == 6:
                        dve.wait_ge(s_tps, 4 * (t + 1) + 2)
                    elif q >= 3:
                        dve.wait_ge(s_wn["used"], q - 2 - (q > 6))
                    pr = wpp[:, q].rearrange("p (m h) -> p m h", h=H).unsqueeze(3).broadcast_to((P, K16, H, D))
                    vv = keys[:, :, 2 * C:3 * C].rearrange("p m (h d) -> p m h d", h=H)
                    ins = tt(wprod[q % 3].rearrange("p (m h d) -> p m h d", h=H, d=D), pr, vv, ALU.mult)
                    if q % 2:
                        seq(ins)
                        product = wprod[q % 3].rearrange("p (n k e) -> p n k e", n=NW, k=2)
                        ins = tt(product[:, :, 0], product[:, :, 0], product[:, :, 1], ALU.add)
                    ins.then_inc(s_wn["pv"], 1)
                for k in range(4):
                    dve.wait_ge(s_wn["pr"], k + 1)
                    xs = x[:, 4 * k:4 * k + 4]
                    seq(tt(xs, xs, b1proj[:].unsqueeze(1).broadcast_to((P, 4, C)), ALU.add))
                    xf = xs.rearrange("p a c -> p (a c)")
                    seq(tt(xf, psum[4 + k][:], xf, ALU.add))
                    if not last_stage:
                        stats(x, k)

            for s in stages:
                t, i, v, last_stage = first_t[s], first_n[s], first_src[s], s == stages[-1]
                if s in "DF":
                    norm(i, x, xn, have_stats=i > 0)
                    norm(i + 1, xn, go, v)
                    grouped_attention(t, gqa_no[s])
                    norm(i + 2, go, xn, v + 1, have_stats=True)
                    moe(1, moe_no[s], t + 2, last_stage)
                    continue
                norm(i, x, xn, v, have_stats=i > 0)
                if s in "AC":
                    moe(0, moe_no[s], t, last_stage)
                elif s == "B":
                    rope_attention(t, last_stage)
                else:
                    window_attention(t, last_stage)
            dve.drain().then_inc(s_done, 1)


_INS = ["L0_attn_x", "L0_attn_W_qkv", "L0_attn_W_proj", "L0_ffn_W1", "L0_ffn_b1", "L0_ffn_W2", "L0_ffn_b2",
        "L0_ffn_Wr", "L0_ffn_br", "L1_attn_w_qkv", "L1_attn_b_qkv", "L1_attn_w_proj", "L1_attn_b_proj",
        "L1_attn_bias_table", "L1_ffn_ln1_weight", "L1_ffn_ln1_bias", "L1_ffn_ln2_weight", "L1_ffn_ln2_bias",
        "L1_ffn_qkv_weight", "L1_ffn_proj_weight", "L1_ffn_router_weight", "L1_ffn_moe_w1", "L1_ffn_moe_w2"]


def kernel(**inputs):
    import concourse.bacc as bacc
    from concourse.bass_utils import run_bass_kernel_spmd

    nc = bacc.Bacc("TRN2", target_bir_lowering=False, num_devices=1)
    arrays = {name: np.ascontiguousarray(inputs[name]) for name in _INS}
    arrays["const"] = const_array()
    a = {n: nc.dram_tensor(f"in_{n}_dram", v.shape, mybir.dt.from_np(v.dtype), kind="ExternalInput").ap()
         for n, v in arrays.items()}
    out = nc.dram_tensor("out_0_dram", (B, T, C), F32, kind="ExternalOutput").ap()
    build(nc, a, out)
    r = run_bass_kernel_spmd(nc, [{f"in_{n}_dram": v for n, v in arrays.items()}], core_ids=[0])
    return r.results[0]["out_0_dram"]
```
